# Optimizing a Trainium2 kernel written in Bass

```python
import numpy as np
import jax
import jax.numpy as jnp

def _softmax(x, axis=-1):
    return jax.nn.softmax(x, axis=axis)

def _gelu(x):
    return jax.nn.gelu(x, approximate=True)

def _silu(x):
    return jax.nn.silu(x)

def _sigmoid(x):
    return jax.nn.sigmoid(x)

def _layernorm(x, axis=-1, eps=1e-05):
    m = jnp.mean(x, axis=axis, keepdims=True)
    v = jnp.var(x, axis=axis, keepdims=True)
    return (x - m) / jnp.sqrt(v + eps)

def _scatter_add(tgt, idx, src, axis=0):
    return tgt.at[idx].add(src)

def _segment_sum(src, seg, n):
    return jax.ops.segment_sum(src, seg, n)
kernel_name = 'mk_gnn_resnorm_d4_gnn_r32_eb3e30'

def setup_inputs(seed: int=0):
    np.random.seed(seed)
    _w = jnp.asarray

    def _rec_inputs():
        import jax
        import jax.numpy as jnp
        _gk = jax.random.key(seed)
        x = -0.0005121 + 1.001 * jax.random.normal(jax.random.fold_in(_gk, 1), (3125, 64), jnp.float32)
        _s = jax.random.randint(jax.random.fold_in(_gk, 2), (50000,), 0, 3125, jnp.int32)
        _d = jax.random.randint(jax.random.fold_in(_gk, 3), (50000,), 0, 3125, jnp.int32)
        _loop = jnp.arange(3125, dtype=jnp.int32)
        src = jnp.concatenate([_s, _d, _loop])
        dst = jnp.concatenate([_d, _s, _loop])
        _o = jnp.argsort(dst, stable=True)
        src = src[_o]
        dst = dst[_o]
        edge_attr_16 = -0.00010739 + 0.99994 * jax.random.normal(jax.random.fold_in(_gk, 13), (103125, 16), jnp.float32)
        edge_attr_32 = -5.16925e-05 + 1.00005 * jax.random.normal(jax.random.fold_in(_gk, 14), (103125, 32), jnp.float32)
        edge_weight1 = jax.random.uniform(jax.random.fold_in(_gk, 16), (103125, 1), jnp.float32, 0.0, 0.999999)
        return (x, src, dst, edge_attr_16, edge_attr_32, edge_weight1)
    x, src, dst, edge_attr_16, edge_attr_32, edge_weight1 = _rec_inputs()

    def _L0_gnn_setup():
        import jax, jax.numpy as jnp
        import numpy as np
        N, D, E, DE, DG, H, DOUT = (50000, 64, 25000, 16, 64, 256, 64)

        def mish(x):
            return x * jnp.tanh(jax.nn.softplus(x))
        key = jax.random.key(seed)
        ks = jax.random.split(key, 8)
        return {'nodes': jax.random.normal(ks[0], (N, D), dtype=jnp.float32), 'edges': jax.random.normal(ks[1], (E, DE), dtype=jnp.float32), 'globals_': jax.random.normal(ks[2], (1, DG), dtype=jnp.float32), 'senders': jax.random.randint(ks[3], (E,), 0, N, dtype=jnp.int32), 'receivers': jax.random.randint(ks[4], (E,), 0, N, dtype=jnp.int32), 'We_kernel': jax.random.normal(ks[5], (DE, D), dtype=jnp.float32) * (1.0 / np.sqrt(DE)), 'We_bias': jnp.zeros((D,), dtype=jnp.float32), 'epsilon': jnp.zeros((1, 1), dtype=jnp.float32), 'W1': jax.random.normal(ks[6], (D + DG, H), dtype=jnp.float32) * (1.0 / np.sqrt(D + DG)), 'b1': jnp.zeros((H,), dtype=jnp.float32), 'W2': jax.random.normal(ks[7], (H, DOUT), dtype=jnp.float32) * (1.0 / np.sqrt(H)), 'b2': jnp.zeros((DOUT,), dtype=jnp.float32)}
    _L0_gnn_all = _L0_gnn_setup()
    _L0_gnn_in = {k: v for k, v in _L0_gnn_all.items() if k in ('globals_', 'We_kernel', 'We_bias', 'epsilon', 'W1', 'b1', 'W2', 'b2')}
    del _L0_gnn_all

    def _L1_gnn_setup():
        import jax, jax.numpy as jnp
        import numpy as np
        N_NODES = 3125
        N_EDGES = 100000
        EDGE_OUT = 32
        HID = 128
        NODE_OUT = 64
        N_GRAPHS = 16
        key = jax.random.key(seed)
        ks = jax.random.split(key, 9)
        x = jax.random.normal(ks[0], (N_NODES, 64), dtype=jnp.float32)
        edge_index = jax.random.randint(ks[1], (2, N_EDGES), 0, N_NODES, dtype=jnp.int64)
        edge_attr = jax.random.normal(ks[2], (N_EDGES, EDGE_OUT), dtype=jnp.float32)
        u = jax.random.normal(ks[3], (N_GRAPHS, 1), dtype=jnp.float32)
        batch = jnp.sort(jax.random.randint(ks[4], (N_NODES,), 0, N_GRAPHS, dtype=jnp.int64))
        d_in = 3 * EDGE_OUT + 1
        W1 = jax.random.normal(ks[5], (d_in, HID), dtype=jnp.float32) / np.sqrt(d_in)
        b1 = jnp.zeros((HID,), dtype=jnp.float32)
        W2 = jax.random.normal(ks[6], (HID, NODE_OUT), dtype=jnp.float32) / np.sqrt(HID)
        b2 = jnp.zeros((NODE_OUT,), dtype=jnp.float32)
        return {'x': x, 'edge_index': edge_index, 'edge_attr': edge_attr, 'u': u, 'batch': batch, 'W1': W1, 'b1': b1, 'W2': W2, 'b2': b2}
    _L1_gnn_all = _L1_gnn_setup()
    _L1_gnn_in = {k: v for k, v in _L1_gnn_all.items() if k in ('u', 'W1', 'b1', 'W2', 'b2')}
    del _L1_gnn_all

    def _L2_gnn_setup():
        import math
        import jax, jax.numpy as jnp
        import numpy as np
        N_NODES = 50000
        N_EDGES = 18750
        IN_CH = 64
        HEADS = 2
        C = 64
        HC = HEADS * C
        EDGE_DIM = 32

        def _layernorm(x, g, b, eps=1e-05):
            m = jnp.mean(x, axis=-1, keepdims=True)
            v = jnp.mean(jnp.square(x - m), axis=-1, keepdims=True)
            return (x - m) / jnp.sqrt(v + eps) * g + b
        key = jax.random.key(seed)
        ks = jax.random.split(key, 12)
        s = 0.05
        return {'x': jax.random.normal(ks[0], (N_NODES, IN_CH), jnp.float32), 'edge_index': jax.random.randint(ks[1], (2, N_EDGES), 0, N_NODES, dtype=jnp.int64), 'edge_attr': jax.random.normal(ks[2], (N_EDGES, EDGE_DIM), jnp.float32), 'Wq': s * jax.random.normal(ks[3], (IN_CH, HC), jnp.float32), 'bq': jnp.zeros((HC,), jnp.float32), 'Wk': s * jax.random.normal(ks[4], (IN_CH, HC), jnp.float32), 'bk': jnp.zeros((HC,), jnp.float32), 'Wv': s * jax.random.normal(ks[5], (IN_CH, HC), jnp.float32), 'bv': jnp.zeros((HC,), jnp.float32), 'We': s * jax.random.normal(ks[6], (EDGE_DIM, HC), jnp.float32), 'Wp': s * jax.random.normal(ks[7], (HC, IN_CH), jnp.float32), 'bp': jnp.zeros((IN_CH,), jnp.float32), 'ln1_g': jnp.ones((IN_CH,), jnp.float32), 'ln1_b': jnp.zeros((IN_CH,), jnp.float32), 'ln2_g': jnp.ones((IN_CH,), jnp.float32), 'ln2_b': jnp.zeros((IN_CH,), jnp.float32), 'W1': s * jax.random.normal(ks[8], (IN_CH, IN_CH), jnp.float32), 'b1': jnp.zeros((IN_CH,), jnp.float32), 'W2': s * jax.random.normal(ks[9], (IN_CH, IN_CH), jnp.float32), 'b2': jnp.zeros((IN_CH,), jnp.float32)}
    _L2_gnn_all = _L2_gnn_setup()
    _L2_gnn_in = {k: v for k, v in _L2_gnn_all.items() if k in ('Wq', 'bq', 'Wk', 'bk', 'Wv', 'bv', 'We', 'Wp', 'bp', 'ln1_g', 'ln1_b', 'ln2_g', 'ln2_b', 'W1', 'b1', 'W2', 'b2')}
    del _L2_gnn_all

    def _L3_gnn_setup():
        import jax, jax.numpy as jnp
        import numpy as np
        N_NODES = 50000
        N_EDGES = 25000
        NODE_NF = 64
        HIDDEN_NF = 128

        def _linear_params(key, fan_in, fan_out):
            kw, kb = jax.random.split(key)
            bound = 1.0 / np.sqrt(fan_in)
            W = jax.random.uniform(kw, (fan_in, fan_out), minval=-bound, maxval=bound, dtype=jnp.float32)
            b = jax.random.uniform(kb, (fan_out,), minval=-bound, maxval=bound, dtype=jnp.float32)
            return (W, b)
        key = jax.random.key(seed)
        ks = jax.random.split(key, 8)
        h = jax.random.normal(ks[0], (N_NODES, NODE_NF), dtype=jnp.float32)
        row = jax.random.randint(ks[1], (N_EDGES,), 0, N_NODES)
        col = jax.random.randint(ks[2], (N_EDGES,), 0, N_NODES)
        dist = jax.random.uniform(ks[3], (N_EDGES, 1), dtype=jnp.float32)
        eW1, eb1 = _linear_params(ks[4], 2 * NODE_NF + 1, HIDDEN_NF)
        eW2, eb2 = _linear_params(ks[5], HIDDEN_NF, HIDDEN_NF)
        nW1, nb1 = _linear_params(ks[6], HIDDEN_NF + NODE_NF, HIDDEN_NF)
        nW2, nb2 = _linear_params(ks[7], HIDDEN_NF, NODE_NF)
        return {'h': h, 'row': row, 'col': col, 'dist': dist, 'eW1': eW1, 'eb1': eb1, 'eW2': eW2, 'eb2': eb2, 'nW1': nW1, 'nb1': nb1, 'nW2': nW2, 'nb2': nb2}
    _L3_gnn_all = _L3_gnn_setup()
    _L3_gnn_in = {k: v for k, v in _L3_gnn_all.items() if k in ('eW1', 'eb1', 'eW2', 'eb2', 'nW1', 'nb1', 'nW2', 'nb2')}
    del _L3_gnn_all
    return {'x': x, 'src': src, 'dst': dst, 'edge_attr_16': edge_attr_16, 'edge_attr_32': edge_attr_32, 'edge_weight1': edge_weight1, 'L0_gnn_globals_': _L0_gnn_in['globals_'], 'L0_gnn_We_kernel': _L0_gnn_in['We_kernel'], 'L0_gnn_We_bias': _L0_gnn_in['We_bias'], 'L0_gnn_epsilon': _L0_gnn_in['epsilon'], 'L0_gnn_W1': _L0_gnn_in['W1'], 'L0_gnn_b1': _L0_gnn_in['b1'], 'L0_gnn_W2': _L0_gnn_in['W2'], 'L0_gnn_b2': _L0_gnn_in['b2'], 'L1_gnn_u': _L1_gnn_in['u'], 'L1_gnn_W1': _L1_gnn_in['W1'], 'L1_gnn_b1': _L1_gnn_in['b1'], 'L1_gnn_W2': _L1_gnn_in['W2'], 'L1_gnn_b2': _L1_gnn_in['b2'], 'L2_gnn_Wq': _L2_gnn_in['Wq'], 'L2_gnn_bq': _L2_gnn_in['bq'], 'L2_gnn_Wk': _L2_gnn_in['Wk'], 'L2_gnn_bk': _L2_gnn_in['bk'], 'L2_gnn_Wv': _L2_gnn_in['Wv'], 'L2_gnn_bv': _L2_gnn_in['bv'], 'L2_gnn_We': _L2_gnn_in['We'], 'L2_gnn_Wp': _L2_gnn_in['Wp'], 'L2_gnn_bp': _L2_gnn_in['bp'], 'L2_gnn_ln1_g': _L2_gnn_in['ln1_g'], 'L2_gnn_ln1_b': _L2_gnn_in['ln1_b'], 'L2_gnn_ln2_g': _L2_gnn_in['ln2_g'], 'L2_gnn_ln2_b': _L2_gnn_in['ln2_b'], 'L2_gnn_W1': _L2_gnn_in['W1'], 'L2_gnn_b1': _L2_gnn_in['b1'], 'L2_gnn_W2': _L2_gnn_in['W2'], 'L2_gnn_b2': _L2_gnn_in['b2'], 'L3_gnn_eW1': _L3_gnn_in['eW1'], 'L3_gnn_eb1': _L3_gnn_in['eb1'], 'L3_gnn_eW2': _L3_gnn_in['eW2'], 'L3_gnn_eb2': _L3_gnn_in['eb2'], 'L3_gnn_nW1': _L3_gnn_in['nW1'], 'L3_gnn_nb1': _L3_gnn_in['nb1'], 'L3_gnn_nW2': _L3_gnn_in['nW2'], 'L3_gnn_nb2': _L3_gnn_in['nb2']}

def reference(x, src, dst, edge_attr_16, edge_attr_32, edge_weight1, L0_gnn_globals_, L0_gnn_We_kernel, L0_gnn_We_bias, L0_gnn_epsilon, L0_gnn_W1, L0_gnn_b1, L0_gnn_W2, L0_gnn_b2, L1_gnn_u, L1_gnn_W1, L1_gnn_b1, L1_gnn_W2, L1_gnn_b2, L2_gnn_Wq, L2_gnn_bq, L2_gnn_Wk, L2_gnn_bk, L2_gnn_Wv, L2_gnn_bv, L2_gnn_We, L2_gnn_Wp, L2_gnn_bp, L2_gnn_ln1_g, L2_gnn_ln1_b, L2_gnn_ln2_g, L2_gnn_ln2_b, L2_gnn_W1, L2_gnn_b1, L2_gnn_W2, L2_gnn_b2, L3_gnn_eW1, L3_gnn_eb1, L3_gnn_eW2, L3_gnn_eb2, L3_gnn_nW1, L3_gnn_nb1, L3_gnn_nW2, L3_gnn_nb2):
    import jax
    import jax.numpy as jnp

    def _L0_gnn_ref(nodes, edges, globals_, senders, receivers, We_kernel, We_bias, epsilon, W1, b1, W2, b2):
        import jax, jax.numpy as jnp
        import numpy as np
        N, D, E, DE, DG, H, DOUT = (50000, 64, 25000, 16, 64, 256, 64)

        def mish(x):
            return x * jnp.tanh(jax.nn.softplus(x))
        num_nodes = nodes.shape[-2]
        sent = jnp.take(nodes, senders, axis=0)
        edge_feat = mish(sent + edges @ We_kernel + We_bias)
        aggr = jax.ops.segment_sum(edge_feat, receivers, num_segments=num_nodes)
        nodes = (1.0 + epsilon) * nodes + aggr
        glob = jnp.repeat(globals_, num_nodes, axis=-2)
        nodes = jnp.concatenate([nodes, glob], axis=-1)
        hidden = mish(nodes @ W1 + b1)
        out = hidden @ W2 + b2
        return out

    def _L1_gnn_ref(x, edge_index, edge_attr, u, batch, W1, b1, W2, b2):
        import jax, jax.numpy as jnp
        import numpy as np
        N_NODES = 3125
        N_EDGES = 100000
        EDGE_OUT = 32
        HID = 128
        NODE_OUT = 64
        N_GRAPHS = 16
        N = x.shape[0]
        row = edge_index[0]
        seg_sum = jax.ops.segment_sum(edge_attr, row, num_segments=N)
        seg_max = jax.ops.segment_max(edge_attr, row, num_segments=N)
        cnt = jax.ops.segment_sum(jnp.ones((edge_attr.shape[0], 1), edge_attr.dtype), row, num_segments=N)
        seg_mean = seg_sum / jnp.maximum(cnt, 1.0)
        seg_max = jnp.where(cnt > 0, seg_max, 0.0)
        h = jnp.concatenate([seg_sum, seg_max, seg_mean, u[batch]], axis=1)
        h = jax.nn.relu(h @ W1 + b1)
        return h @ W2 + b2

    def _L2_gnn_ref(x, edge_index, edge_attr, Wq, bq, Wk, bk, Wv, bv, We, Wp, bp, ln1_g, ln1_b, ln2_g, ln2_b, W1, b1, W2, b2):
        import math
        import jax, jax.numpy as jnp
        import numpy as np
        N_NODES = 50000
        N_EDGES = 18750
        IN_CH = 64
        HEADS = 2
        C = 64
        HC = HEADS * C
        EDGE_DIM = 32

        def _layernorm(x, g, b, eps=1e-05):
            m = jnp.mean(x, axis=-1, keepdims=True)
            v = jnp.mean(jnp.square(x - m), axis=-1, keepdims=True)
            return (x - m) / jnp.sqrt(v + eps) * g + b
        n = x.shape[0]
        residual = x
        h = _layernorm(x, ln1_g, ln1_b)
        q = (h @ Wq + bq).reshape(n, HEADS, C)
        k = (h @ Wk + bk).reshape(n, HEADS, C)
        v = (h @ Wv + bv).reshape(n, HEADS, C)
        src, tgt = (edge_index[0], edge_index[1])
        e = (edge_attr @ We).reshape(-1, HEADS, C)
        qi = q[tgt]
        kj = k[src] + e
        vj = v[src] + e
        alpha = jnp.sum(qi * kj, axis=-1) / math.sqrt(C)
        amax = jax.ops.segment_max(alpha, tgt, num_segments=n)
        ex = jnp.exp(alpha - amax[tgt])
        den = jax.ops.segment_sum(ex, tgt, num_segments=n)
        a = ex / (den[tgt] + 1e-08)
        agg = jax.ops.segment_sum(a[:, :, None] * vj, tgt, num_segments=n)
        out = agg.reshape(n, HC) @ Wp + bp
        out = out + residual
        res2 = out
        o = _layernorm(out, ln2_g, ln2_b)
        o = jax.nn.gelu(o @ W1 + b1, approximate=False) @ W2 + b2
        return o + res2

    def _L3_gnn_ref(h, row, col, dist, eW1, eb1, eW2, eb2, nW1, nb1, nW2, nb2):
        import jax, jax.numpy as jnp
        import numpy as np
        N_NODES = 50000
        N_EDGES = 25000
        NODE_NF = 64
        HIDDEN_NF = 128

        def _linear_params(key, fan_in, fan_out):
            kw, kb = jax.random.split(key)
            bound = 1.0 / np.sqrt(fan_in)
            W = jax.random.uniform(kw, (fan_in, fan_out), minval=-bound, maxval=bound, dtype=jnp.float32)
            b = jax.random.uniform(kb, (fan_out,), minval=-bound, maxval=bound, dtype=jnp.float32)
            return (W, b)
        edge_in = jnp.concatenate([h[row], h[col], dist], axis=1)
        e = jax.nn.silu(edge_in @ eW1 + eb1)
        e = jax.nn.silu(e @ eW2 + eb2)
        agg = jax.ops.segment_sum(e, row, num_segments=h.shape[0])
        node_in = jnp.concatenate([h, agg], axis=1)
        out = jax.nn.silu(node_in @ nW1 + nb1) @ nW2 + nb2
        return out
    edge_index = jnp.stack([src, dst])
    batch0 = jnp.zeros((3125,), jnp.int32)
    x = _layernorm(x + _L0_gnn_ref(x, edge_attr_16, L0_gnn_globals_, src, dst, L0_gnn_We_kernel, L0_gnn_We_bias, L0_gnn_epsilon, L0_gnn_W1, L0_gnn_b1, L0_gnn_W2, L0_gnn_b2), axis=-1)
    x = _layernorm(x + _L1_gnn_ref(x, edge_index, edge_attr_32, L1_gnn_u, batch0, L1_gnn_W1, L1_gnn_b1, L1_gnn_W2, L1_gnn_b2), axis=-1)
    x = _layernorm(x + _L2_gnn_ref(x, edge_index, edge_attr_32, L2_gnn_Wq, L2_gnn_bq, L2_gnn_Wk, L2_gnn_bk, L2_gnn_Wv, L2_gnn_bv, L2_gnn_We, L2_gnn_Wp, L2_gnn_bp, L2_gnn_ln1_g, L2_gnn_ln1_b, L2_gnn_ln2_g, L2_gnn_ln2_b, L2_gnn_W1, L2_gnn_b1, L2_gnn_W2, L2_gnn_b2), axis=-1)
    x = _layernorm(x + _L3_gnn_ref(x, src, dst, edge_weight1, L3_gnn_eW1, L3_gnn_eb1, L3_gnn_eW2, L3_gnn_eb2, L3_gnn_nW1, L3_gnn_nb1, L3_gnn_nW2, L3_gnn_nb2), axis=-1)
    return x

_drawn_inputs = setup_inputs


def setup_inputs(seed=0):
    import zlib

    import numpy as np

    out = dict(_drawn_inputs(seed))
    spreads = {'L0_gnn_We_bias': (0.0, 0.1),
     'L0_gnn_b1': (0.0, 0.8),
     'L0_gnn_b2': (0.0, 0.8),
     'L1_gnn_b1': (0.0, 0.287),
     'L1_gnn_b2': (0.0, 0.1),
     'L2_gnn_bq': (0.0, 0.8),
     'L2_gnn_bk': (0.0, 2.0),
     'L2_gnn_bv': (0.0, 0.294),
     'L2_gnn_bp': (0.0, 0.1),
     'L2_gnn_ln1_g': (1.0, 0.6),
     'L2_gnn_ln1_b': (0.0, 0.8),
     'L2_gnn_ln2_g': (1.0, 0.6),
     'L2_gnn_ln2_b': (0.0, 2.0),
     'L2_gnn_b1': (0.0, 0.774),
     'L2_gnn_b2': (0.0, 0.1)}
    factors = {'edge_weight1': 30.836,
     'L1_gnn_u': 2.67,
     'L2_gnn_Wq': 8.0,
     'L2_gnn_Wk': 8.0,
     'L2_gnn_We': 4.039,
     'L3_gnn_nb1': 4.453}
    for name, (base, spread) in spreads.items():
        noise = np.random.default_rng([zlib.crc32(name.encode()), seed]).standard_normal(out[name].shape)
        drawn = base * np.exp(spread * noise) if base else spread * noise
        out[name] = jnp.asarray(drawn.astype(out[name].dtype))
    for name, factor in factors.items():
        out[name] = (out[name] * factor).astype(out[name].dtype)
    return out
```

```python
from contextlib import ExitStack

import concourse.bass as bass
from concourse import mybir

P = 128
D = 64
NODES = 3125
BLOCKS = -(-NODES // P)
NP_ = BLOCKS * P
EDGES = 103125
TPC = 4
CH = TPC * P
TILES = 808
EP = TILES * P
CHUNKS = TILES // TPC
DE = 32
RECF = DE + 1
REC = RECF + 2
GB = 5
GROUPS = BLOCKS // GB
BIG = 3.0e38
LN_EPS = 1e-5

ALU = mybir.AluOpType
ACT = mybir.ActivationFunctionType
F32 = mybir.dt.float32
BF16 = mybir.dt.bfloat16
I32 = mybir.dt.int32
AX = mybir.AxisListType.X

C_EYE, C_BEFORE, C_UPPER, C_IOTA, C_ONES, C_SPARE = 0, P, 2 * P, 3 * P, 4 * P, 5 * P
C_COLS = 5 * P + BLOCKS


class Chunk:

    def __init__(self, c, d):
        self.n = c + d
        self.s = d % 2
        self.even = c + (d - self.s)

    def landed(self, per_chunk):
        return self.even * (8 * per_chunk) + 16 * per_chunk

    def landed_before(self, per_chunk):
        return self.even * (8 * per_chunk)


def wait(eng, sem, value):
    if isinstance(value, int) and value <= 0:
        return
    eng.wait_ge(sem, value)


def pipeline(eng, now, late=None):
    def pair(c):
        for u in range(2):
            now(Chunk(c, u))
            if late is not None and not (isinstance(c, int) and c + u == 0):
                late(Chunk(c, u - 1))
    pair(0)
    with eng.Fori(2, CHUNKS - 1, 2) as c:
        pair(c)
    if late is not None:
        late(Chunk(CHUNKS, -1))


def groups(eng, step):
    step(0)
    with eng.Fori(1, GROUPS, 1) as g:
        step(g)


def program(nc, a, out):
    top = ExitStack()

    def dram(name, shape, dt=F32):
        return nc.dram_tensor(name, shape, dt).ap()

    rec_s = dram("rec_s", (EP, REC))
    weight_s = dram("weight_s", (EP,))
    keep_d = dram("keep_d", (EP + NP_, 1))
    keep_s = dram("keep_s", (EP + NP_, 1))
    run0 = dram("run0", (EP, D))
    run1 = dram("run1", (EP, 2 * DE))
    run2 = dram("run2", (EP, 130))
    run3 = dram("run3", (EP, P))
    q_tab = dram("q_tab", (NP_, P))
    kv_tab = dram("kv_tab", (NP_, 2 * P))
    a_tab = dram("a_tab", (NP_, P))
    b_tab = dram("b_tab", (NP_, P))

    with top:
        def sb(name, shape, dt=F32, ctx=top):
            return ctx.enter_context(nc.sbuf_tensor(name, shape, dt))

        taken_sems = []

        def sem(name):
            taken_sems.append(nc.alloc_semaphore(name=name))
            return taken_sems[-1]

        gate = top.enter_context(nc.semaphore("gate"))

        def hold(eng):
            eng.sem_inc(gate, 1)

        def end_stage():
            nc.all_engine_barrier()
            nc.clear_and_free_semaphores(taken_sems)
            taken_sems.clear()
            nc.all_engine_barrier()

        consts = sb("consts", [P, C_COLS])
        eye = consts[:, C_EYE:C_EYE + P]
        before = consts[:, C_BEFORE:C_BEFORE + P]
        upper = consts[:, C_UPPER:C_UPPER + P]
        iota = consts[:, C_IOTA:C_IOTA + P]
        ones = consts[:, C_ONES:C_ONES + P]
        spare = consts[:, C_SPARE:C_SPARE + BLOCKS]
        eye_b = sb("eye_b", [P, P], BF16)
        src_i = sb("src_i", [P, TILES], I32)
        dst_i = sb("dst_i", [P, TILES], I32)
        ids_s = sb("ids_s", [P, TILES, 2], I32)
        x = sb("x", [P, BLOCKS, D])
        end_i = [sb(f"end_i{k}", [P, BLOCKS], I32) for k in "sd"]
        has = [sb(f"has{k}", [P, BLOCKS]) for k in "sd"]
        count = [sb(f"count{k}", [P, BLOCKS]) for k in "sd"]
        start = [sb(f"start{k}", [P, BLOCKS]) for k in "sd"]
        eps_col = sb("eps_col", [P, 1])

        def bank(name, ctx, parts, *shape, dt=F32):
            t = ctx.enter_context(nc.psum_tensor(name, [P, 512 * 4 // (2 if dt == BF16 else 4)], dt))
            n = 1
            for d in shape:
                n *= d
            v = t[0:parts, 0:n]
            return v.rearrange("p (a b) -> p a b", a=shape[0]) if len(shape) == 2 else v

        def bcast_mid(ap, n):
            return ap.unsqueeze(1).to_broadcast([ap.shape[0], n, ap.shape[-1]])

        def bcast_last(ap, n):
            return ap.unsqueeze(2).to_broadcast([ap.shape[0], ap.shape[1], n])

        sort = ExitStack()
        keys_i = sb("keys_i", [P, 2, TILES], I32, sort)
        half_i = sb("half_i", [P, 2, 2, TILES], I32, sort)
        key = sb("key", [P, TILES], F32, sort)
        lane = [sb(f"lane{k}", [P, TILES], F32, sort) for k in "sd"]
        blk = [sb(f"blk{k}", [P, TILES], F32, sort) for k in "sd"]

        def load_keys():
            loaded, split, made = sem("k_loaded"), sem("k_split"), sem("k_made")
            with nc.Block() as block:
                @block.sync
                def _(sp):
                    sp.dma_start(consts[:, :], a["consts"]).then_inc(loaded, 16)
                    sp.dma_start(keys_i[:, 0, :], a["src_cols"]).then_inc(loaded, 16)
                    sp.dma_start(keys_i[:, 1, :], a["dst_cols"]).then_inc(loaded, 16)
                    sp.dma_start(x[:, :, :], a["x"].rearrange("(b p) f -> p b f", p=P)).then_inc(loaded, 16)

                @block.vector
                def _(dve):
                    dve.memset(eps_col[:, :], LN_EPS)
                    dve.wait_ge(loaded, 64)
                    for k in range(2):
                        dve.tensor_scalar(half_i[:, k, 0, :], keys_i[:, k, :], P - 1, None,
                                          ALU.bitwise_and).then_inc(split, 1)
                        dve.tensor_scalar(half_i[:, k, 1, :], keys_i[:, k, :], 7, None,
                                          ALU.logical_shift_right).then_inc(split, 1)
                    dve.tensor_copy(eye_b[:, :], eye)
                    dve.tensor_copy(key[:, :], keys_i[:, 0, :])
                    dve.tensor_copy(src_i[:, :], keys_i[:, 0, :])
                    dve.wait_ge(split, 4)
                    for k in range(2):
                        dve.tensor_copy(lane[k][:, :], half_i[:, k, 0, :])
                        last = dve.tensor_copy(blk[k][:, :], half_i[:, k, 1, :])
                    last.then_inc(made, 1)
                    dve.wait_ge(made, 1)

        def histograms():
            with ExitStack() as ctx:
                hot_lane = sb("h_lane", [P, 2, TPC, P], BF16, ctx)
                hot_blk = sb("h_blk", [P, 2, TPC, BLOCKS], BF16, ctx)
                zero = sb("h_zero", [P, P], BF16, ctx)
                sums = ctx.enter_context(nc.psum_tensor("h_sums", [P, 2, 512], F32))
                zeroed, lanes, blks, added = sem("h_zeroed"), sem("h_lanes"), sem("h_blks"), sem("h_added")
                final, copied, prefixed, chain = sem("h_final"), sem("h_copied"), sem("h_prefixed"), sem("h_chain")
                with nc.Block() as block:
                    @block.vector
                    def _(dve):
                        dve.memset(zero[:, :], 0.0).then_inc(zeroed, 1)
                        for k in range(2):
                            def hot(ch, k=k):
                                wait(dve, added, ch.n + (k * CHUNKS - 1))
                                dve.tensor_tensor(hot_lane[:, ch.s], bcast_mid(iota, TPC),
                                                  bcast_last(lane[k][:, bass.ds(ch.n * TPC, TPC)], P),
                                                  ALU.is_equal).then_inc(lanes, 1)
                                dve.tensor_tensor(hot_blk[:, ch.s], bcast_mid(iota[:, 0:BLOCKS], TPC),
                                                  bcast_last(blk[k][:, bass.ds(ch.n * TPC, TPC)], BLOCKS),
                                                  ALU.is_equal).then_inc(blks, 1)
                            pipeline(dve, hot)

                    @block.tensor
                    def _(pe):
                        pe.wait_ge(zeroed, 1)
                        for k in range(2):
                            acc = sums[:, k, 0:BLOCKS]
                            pe.matmul(acc, zero[:, :], zero[:, 0:BLOCKS], start=True, stop=False)

                            def add(ch, k=k, acc=acc):
                                wait(pe, lanes, ch.n + (k * CHUNKS + 1))
                                wait(pe, blks, ch.n + (k * CHUNKS + 1))
                                for t in range(TPC):
                                    mm = pe.matmul(acc, hot_lane[:, ch.s, t], hot_blk[:, ch.s, t],
                                                   start=False, stop=False)
                                mm.then_inc(added, 1)
                            pipeline(pe, add)
                            pe.matmul(acc, zero[:, :], zero[:, 0:BLOCKS], start=False, stop=True).then_inc(final, 1)

                starts(sums, final)

        def starts(sums, final):
            with ExitStack() as ctx:
                tot = ctx.enter_context(nc.psum_tensor("p_tot", [P, 2, 2, 64], F32))
                w = sb("p_w", [P, 2, 6, BLOCKS], F32, ctx)
                mark_i = [sb(f"mark_i{k}", [P, BLOCKS], I32, ctx) for k in "sd"]
                keep1 = sb("p_keep1", [P, TILES + BLOCKS], F32, ctx)
                zero = sb("p_zero", [P, 1], F32, ctx)
                copied, prefixed, chain = sem("p_copied"), sem("p_prefixed"), sem("p_chain")
                filled, inited, marked = sem("p_filled"), sem("p_inited"), sem("p_marked")
                with nc.Block() as block:
                    @block.vector
                    def _(dve):
                        links = [0]

                        def link(ins):
                            links[0] += 1
                            ins.then_inc(chain, 1)
                            dve.wait_ge(chain, links[0])

                        dve.memset(keep1[:, :], 1.0)
                        link(dve.memset(zero[:, :], 0.0))
                        dve.memset(zero[:, :], 0.0).then_inc(filled, 1)
                        dve.wait_ge(final, 2)
                        for k in range(2):
                            dve.tensor_copy(count[k][:, :], sums[:, k, 0:BLOCKS]).then_inc(copied, 1)
                        dve.wait_ge(copied, 2)
                        dve.wait_ge(prefixed, 1)
                        for k in range(2):
                            below, total = tot[:, k, 0, 0:BLOCKS], tot[:, k, 1, 0:BLOCKS]
                            incl, excl, nz, t0, t1, t2 = (w[:, k, j, :] for j in range(6))
                            link(dve.tensor_copy(t0, total))
                            link(dve.tensor_tensor_scan(incl, t0, ones[:, 0:BLOCKS], 0.0, ALU.add, ALU.mult))
                            link(dve.tensor_tensor(excl, incl, t0, ALU.subtract))
                            link(dve.tensor_tensor(start[k][:, :], excl, below, ALU.add))
                            link(dve.tensor_scalar(has[k][:, :], count[k][:, :], 0.0, None, ALU.is_gt))
                            link(dve.scalar_tensor_tensor(t1, start[k][:, :], -1.0, count[k][:, :], ALU.add, ALU.add))
                            link(dve.tensor_tensor(end_i[k][:, :], t1, has[k][:, :], ALU.mult))
                            link(dve.tensor_tensor(t1, start[k][:, :], spare, ALU.subtract))
                            link(dve.tensor_tensor(t2, t1, has[k][:, :], ALU.mult))
                            dve.tensor_tensor(mark_i[k][:, :], t2, spare, ALU.add).then_inc(filled, 1)

                    @block.tensor
                    def _(pe):
                        pe.wait_ge(copied, 2)
                        for k in range(2):
                            pe.matmul(tot[:, k, 0, 0:BLOCKS], upper, count[k][:, :], start=True, stop=True)
                            mm = pe.matmul(tot[:, k, 1, 0:BLOCKS], ones, count[k][:, :], start=True, stop=True)
                        mm.then_inc(prefixed, 1)

                    @block.sync
                    def _(sp):
                        sp.wait_ge(filled, 1)
                        for t in (keep_s, keep_d):
                            sp.dma_start(t.rearrange("(p f) o -> p (f o)", p=P), keep1[:, :]).then_inc(inited, 16)

                    @block.gpsimd
                    def _(pool):
                        pool.wait_ge(inited, 32)
                        pool.wait_ge(filled, 3)
                        for k, t in enumerate((keep_s, keep_d)):
                            for b in range(BLOCKS):
                                pool.indirect_dma_start(t, bass.IndirectOffsetOnAxis(mark_i[k][:, b:b + 1], 0),
                                                        zero[:, :], None).then_inc(marked, 16)
                        pool.wait_ge(marked, 16 * 2 * BLOCKS)

        def sort_by_source():
            with ExitStack() as ctx:
                hot_lane = sb("r_lane", [P, 2, TPC, P], BF16, ctx)
                hot_blk = sb("r_blk", [P, 2, TPC, BLOCKS], F32, ctx)
                hot_blk_b = sb("r_blk_b", [P, 2, TPC, BLOCKS], BF16, ctx)
                hot_t = sb("r_hot_t", [P, 2, TPC * P], F32, ctx)
                row = sb("r_row", [P, 2, CH], I32, ctx)
                junk = sb("r_junk", [P, 2, TPC, P], BF16, ctx)
                seen = sb("r_seen", [P, 2, TPC, BLOCKS], F32, ctx)
                picked = sb("r_picked", [P, 2, TPC, BLOCKS], F32, ctx)
                place = sb("r_place", [P, 2, TPC], F32, ctx)
                inside = sb("r_inside", [P, 2, TPC], F32, ctx)
                place_i = sb("r_place_i", [P, 2, TPC], I32, ctx)
                rec = sb("r_rec", [P, 2, TPC, REC], F32, ctx)
                flip = [bank(f"r_flip{s}", ctx, P, TPC * P, dt=BF16) for s in range(2)]
                hist = [bank(f"r_hist{s}", ctx, P, TPC, BLOCKS) for s in range(2)]
                got = [bank(f"r_got{s}", ctx, P, TPC, BLOCKS) for s in range(2)]
                hot_made, eq_made, flipped, flip_copied = sem("r_hot"), sem("r_eq"), sem("r_flip"), sem("r_flipc")
                hist_made, seen_made, got_made, pick_made = sem("r_hist"), sem("r_seen"), sem("r_got"), sem("r_pick")
                place_made, place_cast, seeded = sem("r_place"), sem("r_cast"), sem("r_seeded")
                row_in = [sem(f"r_row{s}") for s in range(2)]
                rec_in = [sem(f"r_rec{s}") for s in range(2)]
                sent = [sem(f"r_sent{s}") for s in range(2)]
                with nc.Block() as block:
                    @block.sync
                    def _(sp):
                        def load(ch):
                            wait(sp, eq_made, (ch.n - 1) * TPC)
                            hold(sp)
                            sp.dma_start(row[:, ch.s], a["src_flat"][bass.ds(ch.n * CH, CH)].partition_broadcast(P)
                                         ).then_inc(row_in[ch.s], 16)
                            wait(sp, sent[ch.s], ch.landed_before(TPC))
                            hold(sp)
                            rows = bass.ds(ch.n * CH, CH)
                            sp.dma_start(rec[:, ch.s, :, 0:RECF],
                                         a["rec_f"][rows, :].rearrange("(t p) f -> p t f", p=P)).then_inc(rec_in[ch.s], 16)
                            sp.dma_start(rec[:, ch.s, :, RECF:REC].bitcast(I32),
                                         a["rec_i"][rows, :].rearrange("(t p) f -> p t f", p=P)).then_inc(rec_in[ch.s], 16)
                        pipeline(sp, load)

                    @block.vector
                    def _(dve):
                        dve.tensor_copy(seen[:, 1, TPC - 1], start[0][:, :]).then_inc(seeded, 1)
                        dve.wait_ge(seeded, 1)

                        def hots(ch):
                            cols = bass.ds(ch.n * TPC, TPC)
                            wait(dve, hist_made, ch.n - 1)
                            wait(dve, place_cast, ch.n - 1)
                            dve.tensor_tensor(hot_lane[:, ch.s], bcast_mid(iota, TPC),
                                              bcast_last(lane[0][:, cols], P), ALU.is_equal).then_inc(hot_made, 1)
                            dve.tensor_tensor(hot_blk_b[:, ch.s], bcast_mid(iota[:, 0:BLOCKS], TPC),
                                              bcast_last(blk[0][:, cols], BLOCKS), ALU.is_equal).then_inc(hot_made, 1)
                            dve.tensor_tensor(hot_blk[:, ch.s], bcast_mid(iota[:, 0:BLOCKS], TPC),
                                              bcast_last(blk[0][:, cols], BLOCKS), ALU.is_equal).then_inc(hot_made, 1)
                            wait(dve, row_in[ch.s], ch.landed(1))
                            for t in range(TPC):
                                dve.scalar_tensor_tensor(junk[:, ch.s, t], row[:, ch.s, t * P:(t + 1) * P],
                                                         key[:, bass.ds(ch.n * TPC + t, 1)], before,
                                                         ALU.is_equal, ALU.mult,
                                                         accum_out=inside[:, ch.s, t:t + 1]).then_inc(eq_made, 1)

                        def places(ch):
                            wait(dve, hist_made, ch.n + 1)
                            wait(dve, seen_made, ch.n)
                            wait(dve, got_made, ch.n)
                            dve.tensor_tensor(seen[:, ch.s], hist[ch.s][:, :, :],
                                              bcast_mid(seen[:, 1 - ch.s, TPC - 1], TPC), ALU.add).then_inc(seen_made, 1)
                            wait(dve, got_made, ch.n + 1)
                            wait(dve, hot_made, (ch.n + 1) * 3)
                            dve.tensor_tensor(picked[:, ch.s], got[ch.s][:, :, :], hot_blk[:, ch.s],
                                              ALU.mult).then_inc(pick_made, 1)
                            wait(dve, pick_made, ch.n + 1)
                            dve.tensor_reduce(place[:, ch.s], picked[:, ch.s], AX, ALU.add).then_inc(place_made, 1)
                            wait(dve, place_made, ch.n + 1)
                            wait(dve, eq_made, (ch.n + 1) * TPC)
                            wait(dve, sent[ch.s], ch.landed_before(TPC))
                            dve.tensor_tensor(place_i[:, ch.s], place[:, ch.s], inside[:, ch.s],
                                              ALU.add).then_inc(place_cast, 1)
                        pipeline(dve, hots, places)

                    @block.tensor
                    def _(pe):
                        pe.wait_ge(seeded, 1)

                        def products(ch):
                            wait(pe, hot_made, (ch.n + 1) * 3)
                            wait(pe, flip_copied, ch.n - 1)
                            for t in range(TPC):
                                mm = pe.transpose(flip[ch.s][:, t * P:(t + 1) * P], hot_lane[:, ch.s, t], eye_b[:, :])
                            mm.then_inc(flipped, 1)
                            wait(pe, seen_made, ch.n - 1)
                            for t in range(TPC):
                                for j in range(t + 1):
                                    mm = pe.matmul(hist[ch.s][:, t, :], hot_lane[:, ch.s, j], hot_blk_b[:, ch.s, j],
                                                   start=(j == 0), stop=(j == t))
                            mm.then_inc(hist_made, 1)

                        def fetch(ch):
                            wait(pe, flip_copied, ch.n + 1)
                            wait(pe, seen_made, ch.n + 1)
                            wait(pe, pick_made, ch.n - 1)
                            for t in range(TPC):
                                now = seen[:, ch.s, t - 1] if t else seen[:, 1 - ch.s, TPC - 1]
                                mm = pe.matmul(got[ch.s][:, t, :], hot_t[:, ch.s, t * P:(t + 1) * P], now,
                                               start=True, stop=True)
                            mm.then_inc(got_made, 1)
                        pipeline(pe, products, fetch)

                    @block.scalar
                    def _(act):
                        def copy(ch):
                            wait(act, flipped, ch.n + 1)
                            wait(act, got_made, ch.n - 1)
                            act.copy(hot_t[:, ch.s], flip[ch.s][:, :]).then_inc(flip_copied, 1)
                        pipeline(act, copy)

                    @block.gpsimd
                    def _(pool):
                        def send(ch):
                            wait(pool, place_cast, ch.n + 1)
                            wait(pool, rec_in[ch.s], ch.landed(2))
                            hold(pool)
                            for t in range(TPC):
                                pool.indirect_dma_start(rec_s, bass.IndirectOffsetOnAxis(place_i[:, ch.s, t:t + 1], 0),
                                                        rec[:, ch.s, t, :], None).then_inc(sent[ch.s], 16)
                        pipeline(pool, send)
                        for s in range(2):
                            pool.wait_ge(sent[s], CHUNKS // 2 * 16 * TPC)

        def column(name, ap, ctx):
            t = sb(name, [ap.shape[0], 1], F32, ctx)
            return t, ap.rearrange("(p o) -> p o", o=1)

        def load(pairs, tag):
            done = sem(tag + "_loaded")
            with nc.Block() as block:
                @block.sync
                def _(sp):
                    for t, view in pairs:
                        sp.dma_start(t, view).then_inc(done, 16)
                    sp.wait_ge(done, 16 * len(pairs))

        def collect(tag, table, k, agg):
            landed, masked = sem(tag + "_landed"), sem(tag + "_masked")
            with nc.Block() as block:
                @block.gpsimd
                def _(pool):
                    for b in range(BLOCKS):
                        pool.indirect_dma_start(agg[:, b, :], None, table,
                                                bass.IndirectOffsetOnAxis(end_i[k][:, b:b + 1], 0)).then_inc(landed, 16)

                @block.vector
                def _(dve):
                    dve.wait_ge(landed, 16 * BLOCKS)
                    dve.tensor_tensor(agg[:, :, :], agg[:, :, :], bcast_last(has[k][:, :], agg.shape[2]),
                                      ALU.mult).then_inc(masked, 1)
                    dve.wait_ge(masked, 1)

        def norm(tag, src, dst, gain=None, shift=None):
            with ExitStack() as ctx:
                stat = sb(tag + "_stat", [P, 4, BLOCKS], F32, ctx)
                cent = sb(tag + "_cent", [P, BLOCKS, D], F32, ctx)
                sq = sb(tag + "_sq", [P, BLOCKS, D], F32, ctx)
                chain, var_made, rooted = sem(tag + "_chain"), sem(tag + "_var"), sem(tag + "_root")
                with nc.Block() as block:
                    @block.vector
                    def _(dve):
                        links = [0]

                        def link(ins):
                            links[0] += 1
                            ins.then_inc(chain, 1)
                            dve.wait_ge(chain, links[0])

                        link(dve.tensor_reduce(stat[:, 0, :], src[:, :, :], AX, ALU.add))
                        link(dve.tensor_scalar(stat[:, 1, :], stat[:, 0, :], 1.0 / D, None, ALU.mult))
                        link(dve.tensor_tensor(cent[:, :, :], src[:, :, :], bcast_last(stat[:, 1, :], D), ALU.subtract))
                        link(dve.tensor_tensor(sq[:, :, :], cent[:, :, :], cent[:, :, :], ALU.mult))
                        dve.tensor_reduce(stat[:, 2, :], sq[:, :, :], AX, ALU.add).then_inc(var_made, 1)
                        dve.wait_ge(rooted, 1)
                        link(dve.reciprocal(stat[:, 0, :], stat[:, 3, :]))
                        link(dve.tensor_tensor(dst[:, :, :], cent[:, :, :], bcast_last(stat[:, 0, :], D), ALU.mult))
                        if gain is not None:
                            link(dve.tensor_tensor(dst[:, :, :], dst[:, :, :], bcast_mid(gain, BLOCKS), ALU.mult))
                            link(dve.tensor_tensor(dst[:, :, :], dst[:, :, :], bcast_mid(shift, BLOCKS), ALU.add))

                    @block.scalar
                    def _(act):
                        act.wait_ge(var_made, 1)
                        act.activation(stat[:, 3, :], stat[:, 2, :], ACT.Sqrt, bias=eps_col[:, :],
                                       scale=1.0 / D).then_inc(rooted, 1)

        def node_product(tag, src, width, w2, cols, emit):
            with ExitStack() as ctx:
                part = sb(tag + "_part", [P, GB, width], F32, ctx)
                flat = sb(tag + "_flat", [width, GB * P], F32, ctx)
                flip = ctx.enter_context(nc.psum_tensor(tag + "_flip", [width, 2 * 512], F32))
                prod = ctx.enter_context(nc.psum_tensor(tag + "_prod", [P, GB, 512 if cols > 64 else 64], F32))
                taken, flipped, copied, made, used = (sem(f"{tag}_{n}") for n in ("taken", "flipped", "copied", "made", "used"))
                with nc.Block() as block:
                    @block.scalar
                    def _(act):
                        def step(g):
                            wait(act, flipped, g)
                            act.copy(part[:, :, :], src[:, bass.ds(g * GB, GB), 0:width]).then_inc(taken, 1)
                            wait(act, flipped, g + 1)
                            wait(act, made, g)
                            act.copy(flat[:, :], flip[:, 0:GB * P]).then_inc(copied, 1)
                        groups(act, step)

                    @block.tensor
                    def _(pe):
                        def step(g):
                            wait(pe, copied, g)
                            wait(pe, taken, g + 1)
                            hold(pe)
                            for b in range(GB):
                                mm = pe.transpose(flip[:, b * P:(b + 1) * P], part[:, b, :], eye)
                            mm.then_inc(flipped, 1)
                            wait(pe, used, g)
                            wait(pe, copied, g + 1)
                            hold(pe)
                            for b in range(GB):
                                mm = pe.matmul(prod[:, b, 0:cols], flat[:, b * P:(b + 1) * P], w2, start=True, stop=True)
                            mm.then_inc(made, 1)
                        groups(pe, step)

                    @block.vector
                    def _(dve):
                        def step(g):
                            wait(dve, made, g + 1)
                            emit(dve, g, prod[:, :, 0:cols]).then_inc(used, 1)
                        groups(dve, step)

        def node_mlp(tag, parts, w2, bias1, bias2, func, dst, add):
            halves = len(w2)
            hid_w = 128 if halves > 1 else w2[0].shape[0]
            with ExitStack() as ctx:
                part = [sb(f"{tag}_part{i}", [P, GB, w], F32, ctx) for i, (_, w, _) in enumerate(parts)]
                flat = [sb(f"{tag}_flat{i}", [w, GB * P], F32, ctx) for i, (_, w, _) in enumerate(parts)]
                flip = [ctx.enter_context(nc.psum_tensor(f"{tag}_flip{i}", [w, 2 * 512], F32))
                        for i, (_, w, _) in enumerate(parts[:1])]
                flip = flip * len(parts)
                if len(parts) > 1:
                    wide = max(w for _, w, _ in parts)
                    ctx_flip = ctx.enter_context(nc.psum_tensor(f"{tag}_flipw", [wide, 2 * 512], F32))
                    flip = [flip[0], ctx_flip]
                hid_ps = ctx.enter_context(nc.psum_tensor(f"{tag}_hid", [hid_w, 2 * 512], F32))
                prod = bank(f"{tag}_prod", ctx, P, GB, D)
                hid = sb(f"{tag}_hid_s", [hid_w, halves, GB * P], F32, ctx)
                tmp = sb(f"{tag}_tmp", [hid_w, 5, GB * P], F32, ctx) if func == "mish" else None
                names = ("taken", "flipped", "copied", "hidden", "acted", "made", "used", "capped", "exped", "lin", "chain")
                taken, flipped, copied, hidden, acted, made, used, capped, exped, lin, chain = (
                    sem(f"{tag}_{n}") for n in names)
                N = len(parts)
                with nc.Block() as block:
                    @block.scalar
                    def _(act):
                        def step(g):
                            wait(act, flipped, g)
                            for i, (src, w, _) in enumerate(parts):
                                ins = act.copy(part[i][:, :, :], src[:, bass.ds(g * GB, GB), 0:w])
                                ins.then_inc(taken, 1)
                            wait(act, flipped, g + 1)
                            wait(act, hidden, g * halves)
                            for i, (_, w, _) in enumerate(parts):
                                act.copy(flat[i][:, :], flip[i][0:w, 0:GB * P]).then_inc(copied, 1)
                            for h in range(halves):
                                wait(act, hidden, g * halves + (h + 1))
                                wait(act, made, g)
                                if func == "mish":
                                    wait(act, acted, g * halves + h)
                                    act.activation(tmp[:, 0, :], hid_ps[:, 0:GB * P], ACT.Identity,
                                                   bias=bias1[h]).then_inc(lin, 1)
                                    wait(act, capped, g * halves + (h + 1))
                                    act.activation(tmp[:, 2, :], tmp[:, 1, :], ACT.Exp).then_inc(exped, 1)
                                else:
                                    act.activation(hid[:, h, :], hid_ps[:, 0:GB * P], func,
                                                   bias=bias1[h]).then_inc(acted, 1)
                        groups(act, step)

                    @block.tensor
                    def _(pe):
                        def step(g):
                            wait(pe, copied, g * N)
                            wait(pe, taken, g * N + N)
                            hold(pe)
                            for i, (_, w, _) in enumerate(parts):
                                for b in range(GB):
                                    mm = pe.transpose(flip[i][0:w, b * P:(b + 1) * P], part[i][:, b, :], eye)
                            mm.then_inc(flipped, 1)
                            wait(pe, copied, g * N + N)
                            for h in range(halves):
                                wait(pe, acted, g * halves + h)
                                hold(pe)
                                for lo, hi in ((0, 512), (512, GB * P)):
                                    for i, (_, w, w1) in enumerate(parts):
                                        mm = pe.matmul(hid_ps[:, lo:hi], w1[:, h * P:h * P + hid_w], flat[i][:, lo:hi],
                                                       start=(i == 0), stop=(i == N - 1))
                                mm.then_inc(hidden, 1)
                            wait(pe, used, g)
                            wait(pe, acted, g * halves + halves)
                            hold(pe)
                            for b in range(GB):
                                for h in range(halves):
                                    mm = pe.matmul(prod[:, b, :], hid[:, h, b * P:(b + 1) * P], w2[h],
                                                   start=(h == 0), stop=(h == halves - 1))
                            mm.then_inc(made, 1)
                        groups(pe, step)

                    @block.vector
                    def _(dve):
                        def step(g):
                            if func == "mish":
                                for h in range(halves):
                                    n = g * halves + h
                                    y, cap, u, q, r = (tmp[:, j, :] for j in range(5))
                                    wait(dve, lin, n + 1)
                                    wait(dve, exped, n)
                                    dve.tensor_scalar(cap, y, 30.0, None, ALU.min).then_inc(capped, 1)
                                    wait(dve, exped, n + 1)
                                    dve.scalar_tensor_tensor(q, u, 2.0, u, ALU.add, ALU.mult).then_inc(chain, 1)
                                    wait(dve, chain, n * 4 + 1)
                                    dve.tensor_scalar(cap, q, 2.0, None, ALU.add).then_inc(chain, 1)
                                    wait(dve, chain, n * 4 + 2)
                                    dve.reciprocal(r, cap).then_inc(chain, 1)
                                    wait(dve, chain, n * 4 + 3)
                                    dve.tensor_tensor(q, q, r, ALU.mult).then_inc(chain, 1)
                                    wait(dve, chain, n * 4 + 4)
                                    wait(dve, made, g)
                                    dve.tensor_tensor(hid[:, h, :], q, y, ALU.mult).then_inc(acted, 1)
                            wait(dve, made, g + 1)
                            dve.tensor_tensor(dst[:, bass.ds(g * GB, GB), :], prod[:, :, :],
                                              add[:, bass.ds(g * GB, GB), :], ALU.add).then_inc(used, 1)
                        groups(dve, step)
                        dve.wait_ge(used, GROUPS)
                        dve.tensor_tensor(dst[:, :, :], dst[:, :, :], bcast_mid(bias2, BLOCKS), ALU.add).then_inc(used, 1)
                        dve.wait_ge(used, GROUPS + 1)

        def edges0():
            with ExitStack() as ctx:
                we = sb("e0_we", [16, D], F32, ctx)
                be, be_view = column("e0_be", a["L0_We_bias"], ctx)
                idx = sb("e0_idx", [P, 2, TPC], I32, ctx)
                sent_x = sb("e0_x", [P, 2, TPC, D], F32, ctx)
                attr = sb("e0_attr", [16, 2, CH], F32, ctx)
                keep = sb("e0_keep", [D, 2, CH], F32, ctx)
                y, cap, u, w, d, r, t, m, scan = (sb("e0_" + n, [D, 2, CH], F32, ctx) for n in
                                                 ("y", "cap", "u", "w", "d", "r", "t", "m", "scan"))
                rows = sb("e0_rows", [P, 2, TPC, D], F32, ctx)
                z = [ctx.enter_context(nc.psum_tensor(f"e0_z{s}", [D, CH], F32)) for s in range(2)]
                back = [bank(f"e0_back{s}", ctx, P, TPC, D) for s in range(2)]
                load([(we[:, :], a["L0_We_kernel"]), (be[:, :], be_view)], "e0w")
                idx_made, z_made, y_made, cap_made, u_made, w_made, d_made, r_made, t_made, m_made, scanned, flipped, copied = (
                    sem("e0_" + n) for n in ("si", "sz", "sy", "sc", "su", "sw", "sd", "sr", "st", "sm", "ss", "sf", "so"))
                got, loaded, stored = ([sem(f"e0_{n}{s}") for s in range(2)] for n in ("got", "ld", "st_"))
                with nc.Block() as block:
                    @block.gpsimd
                    def _(pool):
                        def gather(ch):
                            wait(pool, got[ch.s], ch.landed_before(TPC))
                            pool.tensor_copy(idx[:, ch.s], src_i[:, bass.ds(ch.n * TPC, TPC)]).then_inc(idx_made, 1)
                            wait(pool, idx_made, ch.n + 1)
                            wait(pool, z_made, ch.n - 1)
                            hold(pool)
                            for q in range(TPC):
                                pool.indirect_dma_start(sent_x[:, ch.s, q, :], None, a["x"],
                                                        bass.IndirectOffsetOnAxis(idx[:, ch.s, q:q + 1], 0)
                                                        ).then_inc(got[ch.s], 16)
                        pipeline(pool, gather)

                    @block.sync
                    def _(sp):
                        def fetch(ch):
                            wait(sp, z_made, ch.n - 1)
                            wait(sp, scanned, ch.n - 1)
                            hold(sp)
                            sp.dma_start(attr[:, ch.s], a["attr16_t"][:, bass.ds(ch.n * CH, CH)]).then_inc(loaded[ch.s], 16)
                            sp.dma_start(keep[:, ch.s], keep_d[bass.ds(ch.n * CH, CH), :].rearrange("e o -> (e o)")
                                         .partition_broadcast(D)).then_inc(loaded[ch.s], 16)
                        pipeline(sp, fetch)

                    @block.tensor
                    def _(pe):
                        def make_z(ch):
                            wait(pe, loaded[ch.s], ch.landed(2))
                            wait(pe, got[ch.s], ch.landed(TPC))
                            wait(pe, y_made, ch.n - 1)
                            pe.matmul(z[ch.s][:, :], we[:, :], attr[:, ch.s], start=True, stop=False)
                            for q in range(TPC):
                                mm = pe.matmul(z[ch.s][:, q * P:(q + 1) * P], sent_x[:, ch.s, q, :], eye,
                                               start=False, stop=(q == TPC - 1))
                            mm.then_inc(z_made, 1)

                        def turn(ch):
                            wait(pe, copied, ch.n - 1)
                            wait(pe, scanned, ch.n + 1)
                            hold(pe)
                            for q in range(TPC):
                                mm = pe.transpose(back[ch.s][:, q, :], scan[:, ch.s, q * P:(q + 1) * P], eye[0:D, 0:D])
                            mm.then_inc(flipped, 1)
                        pipeline(pe, make_z, turn)

                    @block.scalar
                    def _(act):
                        def front(ch):
                            wait(act, z_made, ch.n + 1)
                            wait(act, m_made, ch.n - 1)
                            act.activation(y[:, ch.s], z[ch.s][:, :], ACT.Identity, bias=be[:, :]).then_inc(y_made, 1)
                            wait(act, cap_made, ch.n + 1)
                            wait(act, w_made, ch.n - 1)
                            act.activation(u[:, ch.s], cap[:, ch.s], ACT.Exp).then_inc(u_made, 1)

                        def rear(ch):
                            wait(act, w_made, ch.n + 1)
                            wait(act, r_made, ch.n - 1)
                            act.activation(d[:, ch.s], w[:, ch.s], ACT.Copy, bias=2.0).then_inc(d_made, 1)
                            wait(act, flipped, ch.n + 1)
                            wait(act, stored[ch.s], ch.landed_before(1))
                            act.copy(rows[:, ch.s], back[ch.s][:, :, :]).then_inc(copied, 1)
                            wait(act, copied, ch.n + 1)
                            act.dma_start(run0[bass.ds(ch.n * CH, CH), :].rearrange("(t p) f -> p t f", p=P),
                                          rows[:, ch.s]).then_inc(stored[ch.s], 16)
                        pipeline(act, front, rear)
                        for s in range(2):
                            act.wait_ge(stored[s], CHUNKS // 2 * 16)

                    @block.vector
                    def _(dve):
                        def front(ch):
                            wait(dve, y_made, ch.n + 1)
                            wait(dve, u_made, ch.n - 1)
                            dve.tensor_scalar(cap[:, ch.s], y[:, ch.s], 30.0, None, ALU.min).then_inc(cap_made, 1)

                        def rear(ch):
                            wait(dve, scanned, ch.n - 1)
                            wait(dve, u_made, ch.n + 1)
                            wait(dve, d_made, ch.n - 1)
                            dve.scalar_tensor_tensor(w[:, ch.s], u[:, ch.s], 2.0, u[:, ch.s], ALU.add,
                                                     ALU.mult).then_inc(w_made, 1)
                            wait(dve, d_made, ch.n + 1)
                            dve.reciprocal(r[:, ch.s], d[:, ch.s]).then_inc(r_made, 1)
                            wait(dve, w_made, ch.n + 1)
                            wait(dve, r_made, ch.n + 1)
                            dve.tensor_tensor(t[:, ch.s], w[:, ch.s], r[:, ch.s], ALU.mult).then_inc(t_made, 1)
                            wait(dve, t_made, ch.n + 1)
                            wait(dve, y_made, ch.n + 1)
                            dve.tensor_tensor(m[:, ch.s], t[:, ch.s], y[:, ch.s], ALU.mult).then_inc(m_made, 1)
                            wait(dve, m_made, ch.n + 1)
                            wait(dve, loaded[ch.s], ch.landed(2))
                            wait(dve, scanned, ch.n)
                            wait(dve, flipped, ch.n - 1)
                            dve.tensor_tensor_scan(scan[:, ch.s], keep[:, ch.s], m[:, ch.s],
                                                   0.0 if isinstance(ch.n, int) and ch.n == 0
                                                   else scan[:, 1 - ch.s, CH - 1:CH],
                                                   ALU.mult, ALU.add).then_inc(scanned, 1)
                        pipeline(dve, front, rear)

        def edges1():
            with ExitStack() as ctx:
                rec = sb("e1_rec", [P, 2, TPC, REC], F32, ctx)
                keep = sb("e1_keep", [DE, 2, CH], F32, ctx)
                fresh = sb("e1_fresh", [DE, 2, CH], F32, ctx)
                scan = sb("e1_scan", [2 * DE, 2, CH], F32, ctx)
                top_ = sb("e1_top", [DE, 2, CH], F32, ctx)
                wrow = sb("e1_wrow", [1, 2, CH], F32, ctx)
                rows = sb("e1_rows", [P, 2, TPC, 2 * DE], F32, ctx)
                flat = [ctx.enter_context(nc.psum_tensor(f"e1_flat{s}", [RECF, CH], F32)) for s in range(2)]
                back = [bank(f"e1_back{s}", ctx, P, TPC, 2 * DE) for s in range(2)]
                names = ("sum", "max", "flat", "fresh", "back", "copied", "w", "ids")
                summed, maxed, flat_made, fresh_made, flipped, copied, w_made, ids_made = (sem("e1_s" + n) for n in names)
                loaded, stored, kept = ([sem(f"e1_{n}{s}") for s in range(2)] for n in ("ld", "st_", "kp"))
                with nc.Block() as block:
                    @block.sync
                    def _(sp):
                        def fetch(ch):
                            wait(sp, flat_made, ch.n - 1)
                            wait(sp, ids_made, ch.n - 1)
                            hold(sp)
                            sp.dma_start(rec[:, ch.s], rec_s[bass.ds(ch.n * CH, CH), :].rearrange("(t p) f -> p t f", p=P)
                                         ).then_inc(loaded[ch.s], 16)
                            wait(sp, summed, ch.n - 1)
                            wait(sp, fresh_made, ch.n - 1)
                            hold(sp)
                            sp.dma_start(keep[:, ch.s], keep_s[bass.ds(ch.n * CH, CH), :].rearrange("e o -> (e o)")
                                         .partition_broadcast(DE)).then_inc(kept[ch.s], 16)
                        pipeline(sp, fetch)

                    @block.tensor
                    def _(pe):
                        def turn_in(ch):
                            wait(pe, summed, ch.n - 1)
                            wait(pe, maxed, ch.n - 1)
                            wait(pe, w_made, ch.n - 1)
                            wait(pe, loaded[ch.s], ch.landed(1))
                            hold(pe)
                            for q in range(TPC):
                                mm = pe.transpose(flat[ch.s][:, q * P:(q + 1) * P], rec[:, ch.s, q, 0:RECF], eye)
                            mm.then_inc(flat_made, 1)

                        def turn_out(ch):
                            wait(pe, copied, ch.n - 1)
                            wait(pe, summed, ch.n + 1)
                            wait(pe, maxed, ch.n + 1)
                            hold(pe)
                            for q in range(TPC):
                                pe.transpose(back[ch.s][:, q, 0:DE], scan[0:DE, ch.s, q * P:(q + 1) * P], eye[0:DE, 0:DE])
                                mm = pe.transpose(back[ch.s][:, q, DE:2 * DE], top_[:, ch.s, q * P:(q + 1) * P],
                                                  eye[0:DE, 0:DE])
                            mm.then_inc(flipped, 1)
                        pipeline(pe, turn_in, turn_out)

                    @block.gpsimd
                    def _(pool):
                        def ids(ch):
                            wait(pool, loaded[ch.s], ch.landed(1))
                            pool.tensor_copy(ids_s[:, bass.ds(ch.n * TPC, TPC), :],
                                             rec[:, ch.s, :, RECF:REC].bitcast(I32)).then_inc(ids_made, 1)
                        pipeline(pool, ids)
                        pool.wait_ge(ids_made, CHUNKS)

                    @block.scalar
                    def _(act):
                        def front(ch):
                            wait(act, kept[ch.s], ch.landed(1))
                            wait(act, maxed, ch.n - 1)
                            act.activation(fresh[:, ch.s], keep[:, ch.s], ACT.Copy, bias=-BIG, scale=BIG).then_inc(fresh_made, 1)
                            wait(act, flat_made, ch.n + 1)
                            wait(act, stored[ch.s], ch.landed_before(2))
                            act.copy(wrow[:, ch.s], flat[ch.s][DE:DE + 1, :]).then_inc(w_made, 1)
                            wait(act, w_made, ch.n + 1)
                            act.dma_start(weight_s[bass.ds(ch.n * CH, CH)].rearrange("(o e) -> o e", o=1),
                                          wrow[:, ch.s]).then_inc(stored[ch.s], 16)

                        def rear(ch):
                            wait(act, flipped, ch.n + 1)
                            act.copy(rows[:, ch.s], back[ch.s][:, :, :]).then_inc(copied, 1)
                            wait(act, copied, ch.n + 1)
                            act.dma_start(run1[bass.ds(ch.n * CH, CH), :].rearrange("(t p) f -> p t f", p=P),
                                          rows[:, ch.s]).then_inc(stored[ch.s], 16)
                        pipeline(act, front, rear)
                        for s in range(2):
                            act.wait_ge(stored[s], CHUNKS // 2 * 32)

                    @block.vector
                    def _(dve):
                        def scans(ch):
                            first = isinstance(ch.n, int) and ch.n == 0
                            wait(dve, flat_made, ch.n + 1)
                            wait(dve, kept[ch.s], ch.landed(1))
                            wait(dve, fresh_made, ch.n + 1)
                            wait(dve, flipped, ch.n - 1)
                            wait(dve, summed, ch.n)
                            dve.tensor_tensor_scan(scan[0:DE, ch.s], keep[:, ch.s], flat[ch.s][0:DE, :],
                                                   0.0 if first else scan[0:DE, 1 - ch.s, CH - 1:CH],
                                                   ALU.mult, ALU.add).then_inc(summed, 1)
                            wait(dve, maxed, ch.n)
                            dve.tensor_tensor_scan(top_[:, ch.s], fresh[:, ch.s], flat[ch.s][0:DE, :],
                                                   0.0 if first else top_[:, 1 - ch.s, CH - 1:CH],
                                                   ALU.add, ALU.max).then_inc(maxed, 1)
                        pipeline(dve, scans)

        def edges2():
            with ExitStack() as ctx:
                we = sb("e2_we", [DE, P], F32, ctx)
                heads = sb("e2_heads", [P, P], F32, ctx)
                idx = sb("e2_idx", [P, 2, 2, TPC], I32, ctx)
                q_g = sb("e2_q", [P, 2, TPC, P], F32, ctx)
                kv_g = sb("e2_kv", [P, 2, TPC, 2 * P], F32, ctx)
                attr = sb("e2_attr", [DE, 2, CH], F32, ctx)
                keep, fresh, q_s, qk, low, drop, pr, fade, pv, num, den = (
                    sb("e2_" + n, [P, 2, CH], F32, ctx) for n in
                    ("keep", "fresh", "qs", "qk", "low", "drop", "pr", "fade", "pv", "num", "den"))
                top_ = sb("e2_top", [P, 2, CH + 1], F32, ctx)
                rows = sb("e2_rows", [P, 2, TPC, 130], F32, ctx)
                ps = lambda n, shape: ctx.enter_context(nc.psum_tensor(n, shape, F32))
                q_p, al_p, num_p, den_p = ps("e2_qp", [P, CH]), ps("e2_alp", [P, CH]), ps("e2_nump", [P, TPC, P]), bank("e2_denp", ctx, P, TPC, 2)
                k_p = [ps(f"e2_kp{s}", [P, CH]) for s in range(2)]
                v_p = [ps(f"e2_vp{s}", [P, CH]) for s in range(2)]
                load([(we[:, :], a["L2_We"]), (heads[:, :], a["heads"])], "e2w")
                names = ("idx", "q", "kv", "qc", "qk", "al", "fresh", "edge", "top", "low", "drop", "pr", "fade",
                         "pv", "num", "den", "flip", "copy", "rise")
                (idx_made, q_made, kv_made, q_copied, qk_made, al_made, fresh_made, edge_made, top_made, low_made,
                 drop_made, pr_made, fade_made, pv_made, num_made, den_made, flipped, copied, rise_made) = (sem("e2_s" + n) for n in names)
                got, loaded, stored = ([sem(f"e2_{n}{s}") for s in range(2)] for n in ("got", "ld", "st_"))
                with nc.Block() as block:
                    @block.gpsimd
                    def _(pool):
                        def gather(ch):
                            wait(pool, got[ch.s], ch.landed_before(2 * TPC))
                            cols = bass.ds(ch.n * TPC, TPC)
                            pool.tensor_copy(idx[:, ch.s, 0], src_i[:, cols]).then_inc(idx_made, 1)
                            pool.tensor_copy(idx[:, ch.s, 1], dst_i[:, cols]).then_inc(idx_made, 1)
                            wait(pool, idx_made, (ch.n + 1) * 2)
                            wait(pool, kv_made, ch.n - 1)
                            hold(pool)
                            for t in range(TPC):
                                pool.indirect_dma_start(q_g[:, ch.s, t, :], None, q_tab,
                                                        bass.IndirectOffsetOnAxis(idx[:, ch.s, 1, t:t + 1], 0)
                                                        ).then_inc(got[ch.s], 16)
                                pool.indirect_dma_start(kv_g[:, ch.s, t, :], None, kv_tab,
                                                        bass.IndirectOffsetOnAxis(idx[:, ch.s, 0, t:t + 1], 0)
                                                        ).then_inc(got[ch.s], 16)
                        pipeline(pool, gather)

                    @block.sync
                    def _(sp):
                        def fetch(ch):
                            wait(sp, kv_made, ch.n - 1)
                            hold(sp)
                            sp.dma_start(attr[:, ch.s], a["attr32_t"][:, bass.ds(ch.n * CH, CH)]).then_inc(loaded[ch.s], 16)
                            wait(sp, fresh_made, ch.n - 1)
                            hold(sp)
                            sp.dma_start(keep[:, ch.s], keep_d[bass.ds(ch.n * CH, CH), :].rearrange("e o -> (e o)")
                                         .partition_broadcast(P)).then_inc(loaded[ch.s], 16)
                        pipeline(sp, fetch)

                    @block.tensor
                    def _(pe):
                        def project(ch):
                            wait(pe, got[ch.s], ch.landed(2 * TPC))
                            wait(pe, q_copied, ch.n)
                            for t in range(TPC):
                                mm = pe.transpose(q_p[:, t * P:(t + 1) * P], q_g[:, ch.s, t, :], eye)
                            mm.then_inc(q_made, 1)
                            wait(pe, loaded[ch.s], ch.landed(2))
                            wait(pe, qk_made, ch.n - 1)
                            wait(pe, pv_made, ch.n - 1)
                            for j, dst in ((0, k_p[ch.s]), (1, v_p[ch.s])):
                                pe.matmul(dst[:, :], we[:, :], attr[:, ch.s], start=True, stop=False)
                                for t in range(TPC):
                                    mm = pe.matmul(dst[:, t * P:(t + 1) * P], kv_g[:, ch.s, t, j * P:(j + 1) * P], eye,
                                                   start=False, stop=(t == TPC - 1))
                            mm.then_inc(kv_made, 1)

                        def rest(ch):
                            wait(pe, qk_made, ch.n + 1)
                            wait(pe, low_made, ch.n)
                            pe.matmul(al_p[:, :], heads[:, :], qk[:, ch.s], start=True, stop=True).then_inc(al_made, 1)

                        def turn(ch):
                            wait(pe, num_made, ch.n + 1)
                            wait(pe, den_made, ch.n + 1)
                            wait(pe, copied, 2 * ch.n)
                            for t in range(TPC):
                                pe.transpose(num_p[:, t, :], num[:, ch.s, t * P:(t + 1) * P], eye)
                                mm = pe.matmul(den_p[:, t, :], den[:, ch.s, t * P:(t + 1) * P], eye[:, 0:P:D],
                                               start=True, stop=True)
                            mm.then_inc(flipped, 1)

                        def pair(c):
                            for u in range(2):
                                known = isinstance(c, int)
                                project(Chunk(c, u))
                                rest(Chunk(c, u))
                                if not (known and c + u == 0):
                                    turn(Chunk(c, u - 1))
                        pair(0)
                        with pe.Fori(2, CHUNKS - 1, 2) as c:
                            pair(c)
                        turn(Chunk(CHUNKS, -1))

                    @block.scalar
                    def _(act):
                        def front(ch):
                            wait(act, q_made, ch.n + 1)
                            wait(act, qk_made, ch.n - 1)
                            act.copy(q_s[:, ch.s], q_p[:, :]).then_inc(q_copied, 1)
                            wait(act, loaded[ch.s], ch.landed(2))
                            wait(act, drop_made, ch.n - 1)
                            act.activation(fresh[:, ch.s], keep[:, ch.s], ACT.Copy, bias=-BIG, scale=BIG).then_inc(fresh_made, 1)

                        def rear(ch):
                            wait(act, low_made, ch.n + 1)
                            wait(act, den_made, ch.n - 1)
                            act.activation(pr[:, ch.s], low[:, ch.s], ACT.Exp, scale=D ** -0.5).then_inc(pr_made, 1)
                            wait(act, drop_made, ch.n + 1)
                            act.activation(fade[:, ch.s], drop[:, ch.s], ACT.Exp, scale=D ** -0.5).then_inc(fade_made, 1)
                            wait(act, flipped, ch.n + 1)
                            wait(act, stored[ch.s], ch.landed_before(1))
                            act.copy(rows[:, ch.s, :, 0:P], num_p[:, :, :]).then_inc(copied, 1)
                            act.copy(rows[:, ch.s, :, P:130], den_p[:, :, :]).then_inc(copied, 1)
                            wait(act, copied, 2 * ch.n + 2)
                            act.dma_start(run2[bass.ds(ch.n * CH, CH), :].rearrange("(t p) f -> p t f", p=P),
                                          rows[:, ch.s]).then_inc(stored[ch.s], 16)
                        pipeline(act, front, rear)
                        for s in range(2):
                            act.wait_ge(stored[s], CHUNKS // 2 * 16)

                    @block.vector
                    def _(dve):
                        dve.memset(top_[:, 1, CH:CH + 1], 0.0).then_inc(edge_made, 1)

                        def front(ch):
                            wait(dve, q_copied, ch.n + 1)
                            wait(dve, kv_made, ch.n + 1)
                            wait(dve, al_made, ch.n - 1)
                            dve.tensor_tensor(qk[:, ch.s], q_s[:, ch.s], k_p[ch.s][:, :], ALU.mult).then_inc(qk_made, 1)

                        def rear(ch):
                            wait(dve, den_made, ch.n)
                            if isinstance(ch.n, int) and ch.n == 0:
                                dve.wait_ge(edge_made, 1)
                            dve.tensor_copy(top_[:, ch.s, 0:1], top_[:, 1 - ch.s, CH:CH + 1]).then_inc(edge_made, 1)
                            wait(dve, edge_made, ch.n + 2)
                            wait(dve, al_made, ch.n + 1)
                            wait(dve, fresh_made, ch.n + 1)
                            dve.tensor_tensor_scan(top_[:, ch.s, 1:CH + 1], fresh[:, ch.s], al_p[:, :],
                                                   top_[:, ch.s, 0:1], ALU.add, ALU.max).then_inc(top_made, 1)
                            wait(dve, top_made, ch.n + 1)
                            wait(dve, pr_made, ch.n - 1)
                            dve.tensor_tensor(low[:, ch.s], al_p[:, :], top_[:, ch.s, 1:CH + 1], ALU.subtract).then_inc(low_made, 1)
                            wait(dve, fade_made, ch.n - 1)
                            dve.tensor_tensor(drop[:, ch.s], top_[:, ch.s, 0:CH], top_[:, ch.s, 1:CH + 1],
                                              ALU.subtract).then_inc(rise_made, 1)
                            wait(dve, rise_made, ch.n + 1)
                            dve.scalar_tensor_tensor(drop[:, ch.s], fresh[:, ch.s], 0.0, drop[:, ch.s],
                                                     ALU.add, ALU.add).then_inc(drop_made, 1)
                            wait(dve, pr_made, ch.n + 1)
                            dve.tensor_tensor(pv[:, ch.s], pr[:, ch.s], v_p[ch.s][:, :], ALU.mult).then_inc(pv_made, 1)
                            wait(dve, fade_made, ch.n + 1)
                            wait(dve, pv_made, ch.n + 1)
                            wait(dve, flipped, ch.n - 1)
                            wait(dve, num_made, ch.n)
                            first = isinstance(ch.n, int) and ch.n == 0
                            dve.tensor_tensor_scan(num[:, ch.s], fade[:, ch.s], pv[:, ch.s],
                                                   0.0 if first else num[:, 1 - ch.s, CH - 1:CH],
                                                   ALU.mult, ALU.add).then_inc(num_made, 1)
                            wait(dve, den_made, ch.n)
                            dve.tensor_tensor_scan(den[:, ch.s], fade[:, ch.s], pr[:, ch.s],
                                                   0.0 if first else den[:, 1 - ch.s, CH - 1:CH],
                                                   ALU.mult, ALU.add).then_inc(den_made, 1)
                        pipeline(dve, front, rear)

        def edges3():
            with ExitStack() as ctx:
                w_d = sb("e3_wd", [1, P], F32, ctx)
                w2 = sb("e3_w2", [P, P], F32, ctx)
                b1, b1v = column("e3_b1", a["L3_eb1"], ctx)
                b2, b2v = column("e3_b2", a["L3_eb2"], ctx)
                idx = sb("e3_idx", [P, 2, TPC, 2], I32, ctx)
                a_g = sb("e3_ag", [P, 2, TPC, P], F32, ctx)
                b_g = sb("e3_bg", [P, 2, TPC, P], F32, ctx)
                wrow = sb("e3_wrow", [1, 2, CH], F32, ctx)
                keep, h1, h2, scan = (sb("e3_" + n, [P, 2, CH], F32, ctx) for n in ("keep", "h1", "h2", "scan"))
                rows = sb("e3_rows", [P, 2, TPC, P], F32, ctx)
                ps = lambda n: [ctx.enter_context(nc.psum_tensor(f"{n}{s}", [P, CH], F32)) for s in range(2)]
                z, z2, back = ps("e3_z"), ps("e3_z2"), ps("e3_back")
                load([(w_d[:, :], a["L3_eW1"][2 * D:2 * D + 1, :]), (w2[:, :], a["L3_eW2"]), (b1[:, :], b1v),
                      (b2[:, :], b2v)], "e3w")
                names = ("idx", "z", "h1", "z2", "h2", "scan", "flip", "copy")
                idx_made, z_made, h1_made, z2_made, h2_made, scanned, flipped, copied = (sem("e3_s" + n) for n in names)
                got, loaded, kept, stored = ([sem(f"e3_{n}{s}") for s in range(2)] for n in ("got", "ld", "kp", "st_"))
                with nc.Block() as block:
                    @block.gpsimd
                    def _(pool):
                        def gather(ch):
                            wait(pool, got[ch.s], ch.landed_before(2 * TPC))
                            pool.tensor_copy(idx[:, ch.s], ids_s[:, bass.ds(ch.n * TPC, TPC), :]).then_inc(idx_made, 1)
                            wait(pool, idx_made, ch.n + 1)
                            wait(pool, z_made, ch.n - 1)
                            hold(pool)
                            for t in range(TPC):
                                pool.indirect_dma_start(a_g[:, ch.s, t, :], None, a_tab,
                                                        bass.IndirectOffsetOnAxis(idx[:, ch.s, t, 1:2], 0)
                                                        ).then_inc(got[ch.s], 16)
                                pool.indirect_dma_start(b_g[:, ch.s, t, :], None, b_tab,
                                                        bass.IndirectOffsetOnAxis(idx[:, ch.s, t, 0:1], 0)
                                                        ).then_inc(got[ch.s], 16)
                        pipeline(pool, gather)

                    @block.sync
                    def _(sp):
                        def fetch(ch):
                            wait(sp, z_made, ch.n - 1)
                            hold(sp)
                            sp.dma_start(wrow[:, ch.s], weight_s[bass.ds(ch.n * CH, CH)].rearrange("(o e) -> o e", o=1)
                                         ).then_inc(loaded[ch.s], 16)
                            wait(sp, scanned, ch.n - 1)
                            hold(sp)
                            sp.dma_start(keep[:, ch.s], keep_s[bass.ds(ch.n * CH, CH), :].rearrange("e o -> (e o)")
                                         .partition_broadcast(P)).then_inc(kept[ch.s], 16)
                        pipeline(sp, fetch)

                    @block.tensor
                    def _(pe):
                        def first(ch):
                            wait(pe, got[ch.s], ch.landed(2 * TPC))
                            wait(pe, loaded[ch.s], ch.landed(1))
                            wait(pe, h1_made, ch.n - 1)
                            pe.matmul(z[ch.s][:, :], w_d[:, :], wrow[:, ch.s], start=True, stop=False)
                            for t in range(TPC):
                                cols = z[ch.s][:, t * P:(t + 1) * P]
                                pe.matmul(cols, a_g[:, ch.s, t, :], eye, start=False, stop=False)
                                mm = pe.matmul(cols, b_g[:, ch.s, t, :], eye, start=False, stop=(t == TPC - 1))
                            mm.then_inc(z_made, 1)
                            wait(pe, h1_made, ch.n + 1)
                            wait(pe, h2_made, ch.n - 1)
                            pe.matmul(z2[ch.s][:, :], w2[:, :], h1[:, ch.s], start=True, stop=True).then_inc(z2_made, 1)

                        def turn(ch):
                            wait(pe, scanned, ch.n + 1)
                            wait(pe, copied, ch.n - 1)
                            for t in range(TPC):
                                mm = pe.transpose(back[ch.s][:, t * P:(t + 1) * P], scan[:, ch.s, t * P:(t + 1) * P], eye)
                            mm.then_inc(flipped, 1)
                        pipeline(pe, first, turn)

                    @block.scalar
                    def _(act):
                        def front(ch):
                            wait(act, z_made, ch.n + 1)
                            wait(act, z2_made, ch.n - 1)
                            act.activation(h1[:, ch.s], z[ch.s][:, :], ACT.Silu, bias=b1[:, :]).then_inc(h1_made, 1)
                            wait(act, z2_made, ch.n + 1)
                            wait(act, scanned, ch.n - 1)
                            act.activation(h2[:, ch.s], z2[ch.s][:, :], ACT.Silu, bias=b2[:, :]).then_inc(h2_made, 1)

                        def rear(ch):
                            wait(act, flipped, ch.n + 1)
                            wait(act, stored[ch.s], ch.landed_before(1))
                            act.copy(rows[:, ch.s].rearrange("p t f -> p (t f)"), back[ch.s][:, :]).then_inc(copied, 1)
                            wait(act, copied, ch.n + 1)
                            act.dma_start(run3[bass.ds(ch.n * CH, CH), :].rearrange("(t p) f -> p t f", p=P),
                                          rows[:, ch.s]).then_inc(stored[ch.s], 16)
                        pipeline(act, front, rear)
                        for s in range(2):
                            act.wait_ge(stored[s], CHUNKS // 2 * 16)

                    @block.vector
                    def _(dve):
                        def step(ch):
                            wait(dve, h2_made, ch.n + 1)
                            wait(dve, kept[ch.s], ch.landed(1))
                            wait(dve, scanned, ch.n)
                            wait(dve, flipped, ch.n - 1)
                            dve.tensor_tensor_scan(scan[:, ch.s], keep[:, ch.s], h2[:, ch.s],
                                                   0.0 if isinstance(ch.n, int) and ch.n == 0
                                                   else scan[:, 1 - ch.s, CH - 1:CH],
                                                   ALU.mult, ALU.add).then_inc(scanned, 1)
                        pipeline(dve, step)

        def small(tag, build):
            chain = sem(tag + "_chain")
            with nc.Block() as block:
                @block.vector
                def _(dve):
                    n = 0
                    for make in build:
                        make(dve).then_inc(chain, 1)
                        n += 1
                        dve.wait_ge(chain, n)

        def bias_column(tag, w_rows, vec, base, dst, ctx):
            halves = len(dst)
            ps = ctx.enter_context(nc.psum_tensor(tag + "_ps", [P, halves], F32))
            made, added = sem(tag + "_made"), sem(tag + "_added")
            with nc.Block() as block:
                @block.tensor
                def _(pe):
                    for h in range(halves):
                        mm = pe.matmul(ps[:, h:h + 1], w_rows[:, h * P:(h + 1) * P], vec, start=True, stop=True)
                    mm.then_inc(made, 1)

                @block.vector
                def _(dve):
                    dve.wait_ge(made, 1)
                    for h in range(halves):
                        last = dve.tensor_tensor(dst[h], ps[:, h:h + 1], base[h], ALU.add)
                        last.then_inc(added, 1)
                    dve.wait_ge(added, halves)

        def nodes0():
            with ExitStack() as ctx:
                agg = sb("n0_agg", [P, BLOCKS, D], F32, ctx)
                w1a = sb("n0_w1a", [D, 2 * P], F32, ctx)
                w1g = sb("n0_w1g", [D, 2 * P], F32, ctx)
                w2 = [sb(f"n0_w2{h}", [P, D], F32, ctx) for h in range(2)]
                glob, gv = column("n0_glob", a["L0_globals_"].rearrange("a b -> (a b)"), ctx)
                b1 = sb("n0_b1", [P, 2], F32, ctx)
                b1g = [sb(f"n0_b1g{h}", [P, 1], F32, ctx) for h in range(2)]
                b2 = sb("n0_b2", [P, D], F32, ctx)
                eps = sb("n0_eps", [P, 1], F32, ctx)
                load([(w1a[:, :], a["L0_W1"][0:D, :]), (w1g[:, :], a["L0_W1"][D:2 * D, :]),
                      (w2[0][:, :], a["L0_W2"][0:P, :]), (w2[1][:, :], a["L0_W2"][P:2 * P, :]), (glob[:, :], gv),
                      (b1[:, 0:1], a["L0_b1"][0:P].rearrange("(p o) -> p o", o=1)),
                      (b1[:, 1:2], a["L0_b1"][P:2 * P].rearrange("(p o) -> p o", o=1)),
                      (b2[:, :], a["L0_b2"].partition_broadcast(P)),
                      (eps[:, :], a["L0_epsilon"].rearrange("a b -> (a b)").partition_broadcast(P))], "n0")
                collect("n0c", run0, 1, agg)
                with ExitStack() as c2:
                    bias_column("n0b", w1g, glob[:, :], [b1[:, 0:1], b1[:, 1:2]], [t[:, :] for t in b1g], c2)
                small("n0s", [
                    lambda dve: dve.tensor_scalar(eps[:, :], eps[:, :], 1.0, None, ALU.add),
                    lambda dve: dve.scalar_tensor_tensor(agg[:, :, :], x[:, :, :], eps[:, :], agg[:, :, :],
                                                         ALU.mult, ALU.add)])
                node_mlp("n0m", [(agg, D, w1a)], [t[:, :] for t in w2], [t[:, :] for t in b1g], b2[:, :], "mish", x, x)
                norm("n0n", x, x)

        def nodes1():
            with ExitStack() as ctx:
                agg = sb("n1_agg", [P, BLOCKS, 2 * DE], F32, ctx)
                cat = sb("n1_cat", [P, BLOCKS, 3 * DE], F32, ctx)
                w1 = sb("n1_w1", [3 * DE, P], F32, ctx)
                w1u, w1uv = column("n1_w1u", a["L1_W1"][3 * DE:3 * DE + 1, :].rearrange("a b -> (a b)"), ctx)
                b1, b1v = column("n1_b1", a["L1_b1"], ctx)
                u0 = sb("n1_u0", [P, 1], F32, ctx)
                w2 = sb("n1_w2", [P, D], F32, ctx)
                b2 = sb("n1_b2", [P, D], F32, ctx)
                inv = sb("n1_inv", [P, 2, BLOCKS], F32, ctx)
                load([(w1[:, :], a["L1_W1"][0:3 * DE, :]), (w1u[:, :], w1uv), (b1[:, :], b1v),
                      (u0[:, :], a["L1_u"][0:1, :].rearrange("a b -> (a b)").partition_broadcast(P)),
                      (w2[:, :], a["L1_W2"]), (b2[:, :], a["L1_b2"].partition_broadcast(P))], "n1")
                collect("n1c", run1, 0, agg)
                small("n1s", [
                    lambda dve: dve.scalar_tensor_tensor(b1[:, :], w1u[:, :], u0[:, :], b1[:, :], ALU.mult, ALU.add),
                    lambda dve: dve.tensor_scalar(inv[:, 0, :], count[0][:, :], 1.0, None, ALU.max),
                    lambda dve: dve.reciprocal(inv[:, 1, :], inv[:, 0, :]),
                    lambda dve: dve.tensor_copy(cat[:, :, 0:2 * DE], agg[:, :, :]),
                    lambda dve: dve.tensor_tensor(cat[:, :, 2 * DE:3 * DE], agg[:, :, 0:DE],
                                                  bcast_last(inv[:, 1, :], DE), ALU.mult)])
                node_mlp("n1m", [(cat, 3 * DE, w1)], [w2[:, :]], [b1[:, :]], b2[:, :], ACT.Relu, x, x)
                norm("n1n", x, x)

        def store_rows(tag, pairs):
            done = sem(tag + "_done")
            with nc.Block() as block:
                @block.sync
                def _(sp):
                    for t, view in pairs:
                        sp.dma_start(view.rearrange("(b p) f -> p b f", p=P), t).then_inc(done, 16)
                    sp.wait_ge(done, 16 * len(pairs))

        def tables2():
            with ExitStack() as ctx:
                h = sb("t2_h", [P, BLOCKS, D], F32, ctx)
                g, b = sb("t2_g", [P, D], F32, ctx), sb("t2_b", [P, D], F32, ctx)
                w = sb("t2_w", [D, 3 * P], F32, ctx)
                bias = sb("t2_bias", [P, 3 * P], F32, ctx)
                qkv = sb("t2_qkv", [P, BLOCKS, 3 * P], F32, ctx)
                pairs = [(g[:, :], a["L2_ln1_g"].partition_broadcast(P)), (b[:, :], a["L2_ln1_b"].partition_broadcast(P))]
                for j, n in enumerate("qkv"):
                    pairs.append((w[:, j * P:(j + 1) * P], a["L2_W" + n]))
                    pairs.append((bias[:, j * P:(j + 1) * P], a["L2_b" + n].partition_broadcast(P)))
                load(pairs, "t2")
                norm("t2n", x, h, g[:, :], b[:, :])
                node_product("t2p", h, D, w[:, :], 3 * P, lambda dve, i, rows: dve.tensor_tensor(
                    qkv[:, bass.ds(i * GB, GB), :], rows, bcast_mid(bias[:, :], GB), ALU.add))
                store_rows("t2s", [(qkv[:, :, 0:P], q_tab), (qkv[:, :, P:3 * P], kv_tab)])

        def nodes2():
            with ExitStack() as ctx:
                agg = sb("n2_agg", [P, BLOCKS, 130], F32, ctx)
                res = sb("n2_res", [P, BLOCKS, D], F32, ctx)
                o = sb("n2_o", [P, BLOCKS, D], F32, ctx)
                wp = sb("n2_wp", [P, D], F32, ctx)
                w1, w2 = sb("n2_w1", [D, D], F32, ctx), sb("n2_w2", [D, D], F32, ctx)
                b1, b1v = column("n2_b1", a["L2_b1"], ctx)
                bp, g, b, b2 = (sb("n2_" + n, [P, D], F32, ctx) for n in ("bp", "g", "b", "b2"))
                inv = sb("n2_inv", [P, BLOCKS, 2], F32, ctx)
                load([(wp[:, :], a["L2_Wp"]), (w1[:, :], a["L2_W1"]), (w2[:, :], a["L2_W2"]), (b1[:, :], b1v),
                      (bp[:, :], a["L2_bp"].partition_broadcast(P)), (g[:, :], a["L2_ln2_g"].partition_broadcast(P)),
                      (b[:, :], a["L2_ln2_b"].partition_broadcast(P)), (b2[:, :], a["L2_b2"].partition_broadcast(P))], "n2")
                collect("n2c", run2, 1, agg)

                def scaled(h):
                    part = agg[:, :, h * D:(h + 1) * D]
                    return lambda dve: dve.tensor_tensor(part, part, bcast_last(inv[:, :, h], D), ALU.mult)
                small("n2s", [
                    lambda dve: dve.tensor_scalar(inv[:, :, :], agg[:, :, P:130], 1e-8, None, ALU.add),
                    lambda dve: dve.reciprocal(inv[:, :, :], inv[:, :, :]),
                    scaled(0), scaled(1)])
                node_product("n2p", agg, P, wp[:, :], D, lambda dve, i, rows: dve.tensor_tensor(
                    res[:, bass.ds(i * GB, GB), :], rows, bcast_mid(bp[:, :], GB), ALU.add))
                small("n2t", [lambda dve: dve.tensor_tensor(res[:, :, :], res[:, :, :], x[:, :, :], ALU.add)])
                norm("n2n", res, o, g[:, :], b[:, :])
                small("n2u", [lambda dve: dve.tensor_tensor(x[:, :, :], res[:, :, :], x[:, :, :], ALU.add)])
                node_mlp("n2m", [(o, D, w1)], [w2[:, :]], [b1[:, :]], b2[:, :], ACT.Gelu, x, x)
                norm("n2o", x, x)

        def tables3():
            with ExitStack() as ctx:
                w = sb("t3_w", [D, 2 * P], F32, ctx)
                ab = sb("t3_ab", [P, BLOCKS, 2 * P], F32, ctx)
                load([(w[:, 0:P], a["L3_eW1"][0:D, :]), (w[:, P:2 * P], a["L3_eW1"][D:2 * D, :])], "t3")
                node_product("t3p", x, D, w[:, :], 2 * P, lambda dve, i, rows: dve.tensor_copy(
                    ab[:, bass.ds(i * GB, GB), :], rows))
                store_rows("t3s", [(ab[:, :, 0:P], a_tab), (ab[:, :, P:2 * P], b_tab)])

        def nodes3():
            with ExitStack() as ctx:
                agg = sb("n3_agg", [P, BLOCKS, P], F32, ctx)
                w1x, w1a = sb("n3_w1x", [D, P], F32, ctx), sb("n3_w1a", [P, P], F32, ctx)
                w2 = sb("n3_w2", [P, D], F32, ctx)
                b1, b1v = column("n3_b1", a["L3_nb1"], ctx)
                b2 = sb("n3_b2", [P, D], F32, ctx)
                load([(w1x[:, :], a["L3_nW1"][0:D, :]), (w1a[:, :], a["L3_nW1"][D:D + P, :]), (w2[:, :], a["L3_nW2"]),
                      (b1[:, :], b1v), (b2[:, :], a["L3_nb2"].partition_broadcast(P))], "n3")
                collect("n3c", run3, 0, agg)
                node_mlp("n3m", [(x, D, w1x), (agg, P, w1a)], [w2[:, :]], [b1[:, :]], b2[:, :], ACT.Silu, x, x)
                norm("n3n", x, x)
                store_rows("n3s", [(x[:, :, :], out)])

        with sort:
            load_keys()
            small("dcopy", [lambda dve: dve.tensor_copy(dst_i[:, :], keys_i[:, 1, :])])
            histograms()
            sort_by_source()
            end_stage()
        edges0()
        end_stage()
        nodes0()
        end_stage()
        edges1()
        end_stage()
        nodes1()
        end_stage()
        tables2()
        end_stage()
        edges2()
        end_stage()
        nodes2()
        end_stage()
        tables3()
        end_stage()
        edges3()
        end_stage()
        nodes3()


def kernel(**inputs):
    import numpy as np
    import concourse.bacc as bacc
    from concourse.bass_utils import run_bass_kernel_spmd as run

    v = {k: np.asarray(t) for k, t in inputs.items()}
    pad = EP - EDGES

    def pad_rows(t, rows, fill=0):
        return np.concatenate([t, np.full((rows - t.shape[0],) + t.shape[1:], fill, t.dtype)])

    src, dst = pad_rows(v["src"], EP, NODES), pad_rows(v["dst"], EP, NODES)
    ea16, ea32 = pad_rows(v["edge_attr_16"], EP), pad_rows(v["edge_attr_32"], EP)
    weight = pad_rows(v["edge_weight1"], EP)
    lanes = np.arange(P)
    consts = np.zeros((P, C_COLS), np.float32)
    consts[:, C_EYE:C_EYE + P] = np.eye(P)
    consts[:, C_BEFORE:C_BEFORE + P] = lanes[None, :] < lanes[:, None]
    consts[:, C_UPPER:C_UPPER + P] = lanes[:, None] < lanes[None, :]
    consts[:, C_IOTA:C_IOTA + P] = lanes[None, :]
    consts[:, C_ONES:C_ONES + P] = 1.0
    consts[:, C_SPARE:] = EP + np.arange(BLOCKS)[None, :] * P + lanes[:, None]
    heads = (lanes[:, None] // D == lanes[None, :] // D).astype(np.float32)
    arrays = {
        "consts": consts, "heads": heads,
        "x": pad_rows(v["x"], NP_),
        "src_flat": src, "src_cols": np.ascontiguousarray(src.reshape(TILES, P).T),
        "dst_cols": np.ascontiguousarray(dst.reshape(TILES, P).T),
        "rec_f": np.concatenate([ea32, weight], axis=1), "rec_i": np.stack([dst, src], axis=1),
        "attr16_t": np.ascontiguousarray(ea16.T), "attr32_t": np.ascontiguousarray(ea32.T),
    }
    for k, t in v.items():
        if "_gnn_" in k:
            arrays[k.replace("_gnn", "")] = t
    arrays = {k: np.ascontiguousarray(t) for k, t in arrays.items()}
    nc = bacc.Bacc("TRN2", target_bir_lowering=False, num_devices=1)
    a = {k: nc.dram_tensor("in_" + k, t.shape, mybir.dt.from_np(t.dtype), kind="ExternalInput").ap()
         for k, t in arrays.items()}
    out = nc.dram_tensor("out", (NP_, D), F32, kind="ExternalOutput").ap()
    program(nc, a, out)
    r = run(nc, [{"in_" + k: t for k, t in arrays.items()}], core_ids=[0])
    return r.results[0]["out"][:NODES]
```

```python
from contextlib import ExitStack

import concourse.bass as bass
from concourse import mybir

P = 128
D = 64
NODES = 3125
BLOCKS = -(-NODES // P)
NP_ = BLOCKS * P
EDGES = 103125
TPC = 4
CH = TPC * P
TILES = 808
EP = TILES * P
CHUNKS = TILES // TPC
DE = 32
RECF = DE + 1
REC = RECF + 1
GB = 5
GROUPS = BLOCKS // GB
BIG = 1.0e38
STREAMS_D, STREAMS_S = 2, 4
UNITS = CHUNKS // 2
RING = 4
LN_EPS = 1e-5
CAP = 20.0

ALU = mybir.AluOpType
ACT = mybir.ActivationFunctionType
F32 = mybir.dt.float32
BF16 = mybir.dt.bfloat16
I32 = mybir.dt.int32
AX = mybir.AxisListType.X

C_EYE, C_BEFORE, C_UPPER, C_IOTA, C_ONES, C_SPARE = 0, P, 2 * P, 3 * P, 4 * P, 5 * P
C_COLS = 5 * P + BLOCKS


class Step:

    def __init__(self, i, k, ring):
        self.n = i * ring + k if not isinstance(i, int) else k
        self.s = k % ring
        self.p = k % 2
        self.first = isinstance(i, int) and k == 0
        self.last = (k - 1) % ring
        self.uses = i + k // ring
        self.uses2 = i * (ring // 2) + k // 2

    def landed(self, per_step):
        return (self.uses + 1) * (16 * per_step)

    def landed_before(self, per_step):
        return self.uses * (16 * per_step)


def wait(eng, sem, value):
    if isinstance(value, int) and value <= 0:
        return
    eng.wait_ge(sem, value)


def pipeline(eng, parts, steps=CHUNKS, ring=RING):
    lag = max(d for _, d in parts)
    head = ring + lag + (steps - ring - lag) % ring

    def turn(i, k):
        for part, d in parts:
            if isinstance(i, int) and not 0 <= k - d < steps:
                continue
            part(Step(i, k - d, ring))
    for k in range(head):
        turn(0, k)
    with eng.Fori(0, (steps - head) // ring, 1) as i:
        for k in range(head, head + ring):
            turn(i, k)
    for k in range(steps, steps + lag):
        turn(0, k)


def uses_of(slot, steps, ring):
    return (steps - slot - 1) // ring + 1


def groups(eng, step):
    step(0)
    with eng.Fori(1, GROUPS, 1) as g:
        step(g)


def program(nc, a, out):
    top = ExitStack()

    def dram(name, shape, dt=F32):
        return nc.dram_tensor(name, shape, dt).ap()

    rec_s = dram("rec_s", (EP, REC))
    keep_f = {k: dram("keep_f_" + k, (EP + NP_, 1)) for k in "sd"}
    keep = {k: dram("keep_" + k, (EP,), BF16) for k in "sd"}
    run0 = dram("run0", (EP, D))
    run1 = dram("run1", (EP, 2 * DE))
    run2 = dram("run2", (EP, 130))
    run3 = dram("run3", (EP, P))
    q_rows = dram("q_rows", (EP + NP_, P))
    a_rows = dram("a_rows", (EP + NP_, P))
    kv_tab = dram("kv_tab", (NP_, 2 * P))
    b_tab = dram("b_tab", (NP_, P))

    with top:
        def sb(name, shape, dt=F32, ctx=top):
            return ctx.enter_context(nc.sbuf_tensor(name, shape, dt))

        taken_sems = []

        def sem(name):
            taken_sems.append(nc.alloc_semaphore(name=name))
            return taken_sems[-1]

        gate = top.enter_context(nc.semaphore("gate"))

        def hold(eng):
            eng.sem_inc(gate, 1)

        def end_stage():
            nc.all_engine_barrier()
            nc.clear_and_free_semaphores(taken_sems)
            taken_sems.clear()
            nc.all_engine_barrier()

        consts = sb("consts", [P, C_COLS])
        eye = consts[:, C_EYE:C_EYE + P]
        before = consts[:, C_BEFORE:C_BEFORE + P]
        upper = consts[:, C_UPPER:C_UPPER + P]
        iota = consts[:, C_IOTA:C_IOTA + P]
        ones = consts[:, C_ONES:C_ONES + P]
        spare = consts[:, C_SPARE:C_SPARE + BLOCKS]
        eye_b = sb("eye_b", [P, P], BF16)
        src_i = sb("src_i", [P, TILES], I32)
        ids_s = sb("ids_s", [P, TILES], I32)
        weight_s = sb("weight_s", [P, TILES])
        x = sb("x", [P, BLOCKS, D])
        end_i = [sb(f"end_i{k}", [P, BLOCKS], I32) for k in "sd"]
        has = [sb(f"has{k}", [P, BLOCKS]) for k in "sd"]
        count = [sb(f"count{k}", [P, BLOCKS]) for k in "sd"]
        start = [sb(f"start{k}", [P, BLOCKS]) for k in "sd"]
        mark_i = [sb(f"mark_i{k}", [P, BLOCKS], I32) for k in "sd"]
        spans = [sb("span_s", [P, STREAMS_S - 1, BLOCKS]), sb("span_d", [P, STREAMS_D - 1, BLOCKS])]
        eps_col = sb("eps_col", [P, 1])

        def bank(name, ctx, parts, *shape, dt=F32):
            t = ctx.enter_context(nc.psum_tensor(name, [P, 512 * 4 // (2 if dt == BF16 else 4)], dt))
            n = 1
            for d in shape:
                n *= d
            v = t[0:parts, 0:n]
            return v.rearrange("p (a b) -> p a b", a=shape[0]) if len(shape) == 2 else v

        def tile_cols(ap, t, per):
            return ap.rearrange("f (p t) -> f t p", t=per)[:, t, :]

        def bcast_mid(ap, n):
            return ap.unsqueeze(1).to_broadcast([ap.shape[0], n, ap.shape[-1]])

        def bcast_last(ap, n):
            return ap.unsqueeze(2).to_broadcast([ap.shape[0], ap.shape[1], n])

        sort = ExitStack()
        keys_i = sb("keys_i", [P, 2, TILES], I32, sort)
        half_i = sb("half_i", [P, 2, 2, TILES], I32, sort)
        key = sb("key", [P, TILES], F32, sort)
        lane = [sb(f"lane{k}", [P, TILES], BF16, sort) for k in "sd"]
        blk = [sb(f"blk{k}", [P, TILES], BF16, sort) for k in "sd"]
        iota_b = sb("iota_b", [P, P], BF16, sort)

        def load_keys():
            loaded, split, made = sem("k_loaded"), sem("k_split"), sem("k_made")
            with nc.Block() as block:
                @block.sync
                def _(sp):
                    sp.dma_start(consts[:, :], a["consts"]).then_inc(loaded, 16)
                    sp.dma_start(keys_i[:, 0, :], a["src_cols"]).then_inc(loaded, 16)
                    sp.dma_start(keys_i[:, 1, :], a["dst_cols"]).then_inc(loaded, 16)
                    sp.dma_start(src_i[:, :], a["src_rows"]).then_inc(loaded, 16)
                    sp.dma_start(x[:, :, :], a["x"].rearrange("(b p) f -> p b f", p=P)).then_inc(loaded, 16)

                @block.vector
                def _(dve):
                    dve.memset(eps_col[:, :], LN_EPS)
                    dve.wait_ge(loaded, 80)
                    for k in range(2):
                        dve.tensor_scalar(half_i[:, k, 0, :], keys_i[:, k, :], P - 1, None,
                                          ALU.bitwise_and).then_inc(split, 1)
                        dve.tensor_scalar(half_i[:, k, 1, :], keys_i[:, k, :], 7, None,
                                          ALU.logical_shift_right).then_inc(split, 1)
                    dve.tensor_copy(eye_b[:, :], eye)
                    dve.tensor_copy(iota_b[:, :], iota)
                    dve.tensor_copy(key[:, :], keys_i[:, 0, :])
                    dve.wait_ge(split, 4)
                    for k in range(2):
                        dve.tensor_copy(lane[k][:, :], half_i[:, k, 0, :])
                        last = dve.tensor_copy(blk[k][:, :], half_i[:, k, 1, :])
                    last.then_inc(made, 1)
                    dve.wait_ge(made, 1)

        def histograms():
            with ExitStack() as ctx:
                hot_lane = sb("h_lane", [P, RING, TPC, P], BF16, ctx)
                hot_blk = sb("h_blk", [P, RING, TPC, BLOCKS], BF16, ctx)
                zero = sb("h_zero", [P, P], BF16, ctx)
                sums = ctx.enter_context(nc.psum_tensor("h_sums", [P, 2, 512], F32))
                zeroed, lanes, blks, added = sem("h_zeroed"), sem("h_lanes"), sem("h_blks"), sem("h_added")
                final = sem("h_final")
                with nc.Block() as block:
                    @block.vector
                    def _(dve):
                        dve.memset(zero[:, :], 0.0).then_inc(zeroed, 1)
                        for k in range(2):
                            def hot(ch, k=k):
                                wait(dve, added, ch.n + (k * CHUNKS + 1 - RING))
                                dve.tensor_tensor(hot_lane[:, ch.s], bcast_mid(iota_b[:, :], TPC),
                                                  bcast_last(lane[k][:, bass.ds(ch.n * TPC, TPC)], P),
                                                  ALU.is_equal).then_inc(lanes, 1)
                                dve.tensor_tensor(hot_blk[:, ch.s], bcast_mid(iota_b[:, 0:BLOCKS], TPC),
                                                  bcast_last(blk[k][:, bass.ds(ch.n * TPC, TPC)], BLOCKS),
                                                  ALU.is_equal).then_inc(blks, 1)
                            if k:
                                dve.wait_ge(added, CHUNKS)
                            pipeline(dve, [(hot, 0)])

                    @block.tensor
                    def _(pe):
                        pe.wait_ge(zeroed, 1)
                        for k in range(2):
                            acc = sums[:, k, 0:BLOCKS]
                            pe.matmul(acc, zero[:, :], zero[:, 0:BLOCKS], start=True, stop=False)

                            def add(ch, k=k, acc=acc):
                                wait(pe, lanes, ch.n + (k * CHUNKS + 1))
                                wait(pe, blks, ch.n + (k * CHUNKS + 1))
                                for t in range(TPC):
                                    mm = pe.matmul(acc, hot_lane[:, ch.s, t], hot_blk[:, ch.s, t],
                                                   start=False, stop=False)
                                mm.then_inc(added, 1)
                            pipeline(pe, [(add, 0)])
                            pe.matmul(acc, zero[:, :], zero[:, 0:BLOCKS], start=False, stop=True).then_inc(final, 1)

                starts(sums, final)

        def starts(sums, final):
            with ExitStack() as ctx:
                tot = ctx.enter_context(nc.psum_tensor("p_tot", [P, 2, 2, 64], F32))
                w = sb("p_w", [P, 2, 6, BLOCKS], F32, ctx)
                bits = sb("p_bits", [P, TILES], F32, ctx)
                bits_b = sb("p_bits_b", [P, 2, TILES], BF16, ctx)
                keep1 = sb("p_keep1", [P, TILES + BLOCKS], F32, ctx)
                zero = sb("p_zero", [P, 1], F32, ctx)
                copied, prefixed, chain = sem("p_copied"), sem("p_prefixed"), sem("p_chain")
                filled, inited, marked = sem("p_filled"), sem("p_inited"), sem("p_marked")
                read, narrowed, written = sem("p_read"), sem("p_narrowed"), sem("p_written")
                with nc.Block() as block:
                    @block.vector
                    def _(dve):
                        links = [0]

                        def link(ins):
                            links[0] += 1
                            ins.then_inc(chain, 1)
                            dve.wait_ge(chain, links[0])

                        dve.memset(keep1[:, :], 1.0)
                        link(dve.memset(zero[:, :], 0.0))
                        dve.memset(zero[:, :], 0.0).then_inc(filled, 1)
                        dve.wait_ge(final, 2)
                        for k in range(2):
                            dve.tensor_copy(count[k][:, :], sums[:, k, 0:BLOCKS]).then_inc(copied, 1)
                        dve.wait_ge(copied, 2)
                        dve.wait_ge(prefixed, 1)
                        for k in range(2):
                            below, total = tot[:, k, 0, 0:BLOCKS], tot[:, k, 1, 0:BLOCKS]
                            incl, excl, nz, t0, t1, t2 = (w[:, k, j, :] for j in range(6))
                            link(dve.tensor_copy(t0, total))
                            link(dve.tensor_tensor_scan(incl, t0, ones[:, 0:BLOCKS], 0.0, ALU.add, ALU.mult))
                            link(dve.tensor_tensor(excl, incl, t0, ALU.subtract))
                            link(dve.tensor_tensor(start[k][:, :], excl, below, ALU.add))
                            link(dve.tensor_scalar(has[k][:, :], count[k][:, :], 0.0, None, ALU.is_gt))
                            link(dve.scalar_tensor_tensor(t1, start[k][:, :], -1.0, count[k][:, :], ALU.add, ALU.add))
                            link(dve.tensor_tensor(end_i[k][:, :], t1, has[k][:, :], ALU.mult))
                            link(dve.tensor_tensor(t1, start[k][:, :], spare, ALU.subtract))
                            link(dve.tensor_tensor(t2, t1, has[k][:, :], ALU.mult))
                            dve.tensor_tensor(mark_i[k][:, :], t2, spare, ALU.add).then_inc(filled, 1)
                            link(dve.tensor_tensor(t1, start[k][:, :], count[k][:, :], ALU.add))
                            streams = spans[k].shape[1] + 1
                            for j in range(1, streams):
                                border = float(j * EP // streams)
                                link(dve.tensor_scalar(t0, t1, border, None, ALU.is_gt))
                                link(dve.scalar_tensor_tensor(spans[k][:, j - 1, :], start[k][:, :], border, t0,
                                                              ALU.is_lt, ALU.mult))
                        for k in range(2):
                            dve.wait_ge(read, 16 * (k + 1))
                            dve.tensor_copy(bits_b[:, k, :], bits[:, :]).then_inc(narrowed, 1)

                    @block.tensor
                    def _(pe):
                        pe.wait_ge(copied, 2)
                        for k in range(2):
                            pe.matmul(tot[:, k, 0, 0:BLOCKS], upper, count[k][:, :], start=True, stop=True)
                            mm = pe.matmul(tot[:, k, 1, 0:BLOCKS], ones, count[k][:, :], start=True, stop=True)
                        mm.then_inc(prefixed, 1)

                    @block.sync
                    def _(sp):
                        sp.wait_ge(filled, 1)
                        for k in "sd":
                            sp.dma_start(keep_f[k].rearrange("(p f) o -> p (f o)", p=P), keep1[:, :]).then_inc(inited, 16)
                        for k, name in enumerate("sd"):
                            sp.wait_ge(marked, 16 * 2 * BLOCKS)
                            if k:
                                sp.wait_ge(narrowed, k)
                            sp.dma_start(bits[:, :], keep_f[name][0:EP, :].rearrange("(p f) o -> p (f o)", p=P)).then_inc(read, 16)
                            sp.wait_ge(narrowed, k + 1)
                            sp.dma_start(keep[name].rearrange("(p f) -> p f", p=P), bits_b[:, k, :]).then_inc(written, 16)
                        sp.wait_ge(written, 32)

                    @block.gpsimd
                    def _(pool):
                        pool.wait_ge(inited, 32)
                        pool.wait_ge(filled, 3)
                        for k, name in enumerate("sd"):
                            for b in range(BLOCKS):
                                pool.indirect_dma_start(keep_f[name], bass.IndirectOffsetOnAxis(mark_i[k][:, b:b + 1], 0),
                                                        zero[:, :], None).then_inc(marked, 16)
                        pool.wait_ge(marked, 16 * 2 * BLOCKS)

        def sort_by_source():
            with ExitStack() as ctx:
                hot_lane = sb("r_lane", [P, RING, TPC, P], BF16, ctx)
                hot_blk = sb("r_blk", [P, RING, TPC, BLOCKS], BF16, ctx)
                hot_t = sb("r_hot_t", [P, RING, TPC * P], F32, ctx)
                row = sb("r_row", [P, RING, CH], I32, ctx)
                junk = sb("r_junk", [P, RING, TPC, P], BF16, ctx)
                seen = sb("r_seen", [P, RING, TPC, BLOCKS], F32, ctx)
                picked = sb("r_picked", [P, RING, TPC, BLOCKS], F32, ctx)
                place = sb("r_place", [P, RING, TPC], F32, ctx)
                inside = sb("r_inside", [P, RING, TPC], F32, ctx)
                place_i = sb("r_place_i", [P, RING, TPC], I32, ctx)
                rec = sb("r_rec", [P, RING, TPC, REC], F32, ctx)
                zero = sb("r_zero", [P, CH], F32, ctx)
                flip = [bank(f"r_flip{s}", ctx, P, TPC * P, dt=BF16) for s in range(2)]
                hist = [bank(f"r_hist{s}", ctx, P, TPC, BLOCKS) for s in range(2)]
                got = [bank(f"r_got{s}", ctx, P, TPC, BLOCKS) for s in range(2)]
                hot_made, eq_made, flipped, flip_copied = sem("r_hot"), sem("r_eq"), sem("r_flip"), sem("r_flipc")
                hist_made, seen_made, got_made, pick_made = sem("r_hist"), sem("r_seen"), sem("r_got"), sem("r_pick")
                place_made, place_cast, seeded = sem("r_place"), sem("r_cast"), sem("r_seeded")
                zero_made, cleared, id_made = sem("r_zerom"), sem("r_cleared"), sem("r_id")
                row_in = [sem(f"r_row{s}") for s in range(RING)]
                rec_in = [sem(f"r_rec{s}") for s in range(RING)]
                sent = [sem(f"r_sent{s}") for s in range(RING)]
                with nc.Block() as block:
                    @block.sync
                    def _(sp):
                        sp.wait_ge(zero_made, 1)

                        def fetch(ch):
                            rows = bass.ds(ch.n * CH, CH)
                            wait(sp, eq_made, (ch.n + 1 - RING) * TPC)
                            hold(sp)
                            sp.dma_start(row[:, ch.s], a["src_flat"][rows].partition_broadcast(P)
                                         ).then_inc(row_in[ch.s], 16)
                            wait(sp, sent[ch.s], ch.landed_before(TPC))
                            hold(sp)
                            sp.dma_start(rec[:, ch.s, :, 0:RECF],
                                         a["rec_f"][rows, :].rearrange("(t p) f -> p t f", p=P)).then_inc(rec_in[ch.s], 16)
                            for table in (q_rows, a_rows):
                                sp.dma_start(table[rows, :].rearrange("(p t) f -> p (t f)", p=P), zero[:, :]).then_inc(cleared, 16)
                        pipeline(sp, [(fetch, 0)])
                        sp.wait_ge(cleared, 2 * CHUNKS * 16)

                    @block.vector
                    def _(dve):
                        dve.memset(zero[:, :], 0.0).then_inc(zero_made, 1)
                        dve.tensor_copy(seen[:, RING - 1, TPC - 1], start[0][:, :]).then_inc(seeded, 1)
                        dve.wait_ge(seeded, 1)

                        def hots(ch):
                            cols = bass.ds(ch.n * TPC, TPC)
                            wait(dve, hist_made, ch.n + 1 - RING)
                            wait(dve, place_cast, ch.n + 1 - RING)
                            dve.tensor_tensor(hot_lane[:, ch.s], bcast_mid(iota_b[:, :], TPC),
                                              bcast_last(lane[0][:, cols], P), ALU.is_equal).then_inc(hot_made, 1)
                            dve.tensor_tensor(hot_blk[:, ch.s], bcast_mid(iota_b[:, 0:BLOCKS], TPC),
                                              bcast_last(blk[0][:, cols], BLOCKS), ALU.is_equal).then_inc(hot_made, 1)
                            wait(dve, row_in[ch.s], ch.landed(1))
                            for t in range(TPC):
                                dve.scalar_tensor_tensor(junk[:, ch.s, t], row[:, ch.s, t * P:(t + 1) * P],
                                                         key[:, bass.ds(ch.n * TPC + t, 1)], before,
                                                         ALU.is_equal, ALU.mult,
                                                         accum_out=inside[:, ch.s, t:t + 1]).then_inc(eq_made, 1)

                        def follow(ch):
                            wait(dve, hist_made, ch.n + 1)
                            wait(dve, seen_made, ch.n)
                            wait(dve, got_made, ch.n + 2 - RING)
                            dve.tensor_tensor(seen[:, ch.s], hist[ch.p],
                                              bcast_mid(seen[:, ch.last, TPC - 1], TPC), ALU.add).then_inc(seen_made, 1)

                        def places(ch):
                            wait(dve, got_made, ch.n + 1)
                            wait(dve, hot_made, (ch.n + 1) * 2)
                            dve.tensor_tensor(picked[:, ch.s], got[ch.p], hot_blk[:, ch.s], ALU.mult).then_inc(pick_made, 1)
                            wait(dve, pick_made, ch.n + 1)
                            dve.tensor_reduce(place[:, ch.s], picked[:, ch.s], AX, ALU.add).then_inc(place_made, 1)
                            wait(dve, place_made, ch.n + 1)
                            wait(dve, eq_made, (ch.n + 1) * TPC)
                            wait(dve, sent[ch.s], ch.landed_before(TPC))
                            dve.tensor_tensor(place_i[:, ch.s], place[:, ch.s], inside[:, ch.s],
                                              ALU.add).then_inc(place_cast, 1)
                        pipeline(dve, [(hots, 0), (follow, 1), (places, 2)])

                    @block.tensor
                    def _(pe):
                        pe.wait_ge(seeded, 1)

                        def products(ch):
                            wait(pe, hot_made, (ch.n + 1) * 2)
                            wait(pe, flip_copied, ch.n - 1)
                            for t in range(TPC):
                                mm = pe.transpose(flip[ch.p][:, t * P:(t + 1) * P], hot_lane[:, ch.s, t], eye_b[:, :])
                            mm.then_inc(flipped, 1)
                            wait(pe, seen_made, ch.n - 1)
                            for t in range(TPC):
                                for j in range(t + 1):
                                    mm = pe.matmul(hist[ch.p][:, t, :], hot_lane[:, ch.s, j], hot_blk[:, ch.s, j],
                                                   start=(j == 0), stop=(j == t))
                            mm.then_inc(hist_made, 1)

                        def fetch(ch):
                            wait(pe, flip_copied, ch.n + 1)
                            wait(pe, seen_made, ch.n + 1)
                            wait(pe, pick_made, ch.n - 1)
                            for t in range(TPC):
                                now = seen[:, ch.s, t - 1] if t else seen[:, ch.last, TPC - 1]
                                mm = pe.matmul(got[ch.p][:, t, :], hot_t[:, ch.s, t * P:(t + 1) * P], now,
                                               start=True, stop=True)
                            mm.then_inc(got_made, 1)
                        pipeline(pe, [(products, 0), (fetch, 1)])

                    @block.scalar
                    def _(act):
                        def copy(ch):
                            wait(act, flipped, ch.n + 1)
                            wait(act, got_made, ch.n + 1 - RING)
                            act.copy(hot_t[:, ch.s], flip[ch.p]).then_inc(flip_copied, 1)
                            wait(act, sent[ch.s], ch.landed_before(TPC))
                            act.copy(rec[:, ch.s, :, RECF].bitcast(I32),
                                     keys_i[:, 1, bass.ds(ch.n * TPC, TPC)]).then_inc(id_made, 1)
                        pipeline(act, [(copy, 0)])

                    @block.gpsimd
                    def _(pool):
                        def send(ch):
                            wait(pool, place_cast, ch.n + 1)
                            wait(pool, rec_in[ch.s], ch.landed(1))
                            wait(pool, id_made, ch.n + 1)
                            hold(pool)
                            for t in range(TPC):
                                pool.indirect_dma_start(rec_s, bass.IndirectOffsetOnAxis(place_i[:, ch.s, t:t + 1], 0),
                                                        rec[:, ch.s, t, :], None).then_inc(sent[ch.s], 16)
                        pipeline(pool, [(send, 0)])
                        for s in range(RING):
                            pool.wait_ge(sent[s], uses_of(s, CHUNKS, RING) * 16 * TPC)

        def column(name, ap, ctx):
            t = sb(name, [ap.shape[0], 1], F32, ctx)
            return t, ap.rearrange("(p o) -> p o", o=1)

        def load(pairs, tag):
            done = sem(tag + "_loaded")
            with nc.Block() as block:
                @block.sync
                def _(sp):
                    for t, view in pairs:
                        sp.dma_start(t, view).then_inc(done, 16)
                    sp.wait_ge(done, 16 * len(pairs))

        def collect(tag, table, k, agg):
            landed, masked = sem(tag + "_landed"), sem(tag + "_masked")
            with nc.Block() as block:
                @block.gpsimd
                def _(pool):
                    for b in range(BLOCKS):
                        pool.indirect_dma_start(agg[:, b, :], None, table,
                                                bass.IndirectOffsetOnAxis(end_i[k][:, b:b + 1], 0)).then_inc(landed, 16)

                @block.vector
                def _(dve):
                    dve.wait_ge(landed, 16 * BLOCKS)
                    dve.tensor_tensor(agg[:, :, :], agg[:, :, :], bcast_last(has[k][:, :], agg.shape[2]),
                                      ALU.mult).then_inc(masked, 1)
                    dve.wait_ge(masked, 1)

        def mend(tag, table, k, steps):
            streams = spans[k].shape[1] + 1
            wide = table.shape[1]
            with ExitStack() as ctx:
                ends = sb(tag + "_ends", [P, streams - 1, wide], F32, ctx)
                load([(ends[:, j, :], table[(j + 1) * (EP // streams) - 1:(j + 1) * (EP // streams), :]
                       .rearrange("a f -> (a f)").partition_broadcast(P)) for j in range(streams - 1)], tag)
                small(tag + "s", [op for j in range(streams - 1) for op in steps(ctx, j, ends[:, j, :])])

        def norm(tag, src, dst, gain=None, shift=None):
            with ExitStack() as ctx:
                stat = sb(tag + "_stat", [P, 4, BLOCKS], F32, ctx)
                cent = sb(tag + "_cent", [P, BLOCKS, D], F32, ctx)
                sq = sb(tag + "_sq", [P, BLOCKS, D], F32, ctx)
                chain, var_made, rooted = sem(tag + "_chain"), sem(tag + "_var"), sem(tag + "_root")
                with nc.Block() as block:
                    @block.vector
                    def _(dve):
                        links = [0]

                        def link(ins):
                            links[0] += 1
                            ins.then_inc(chain, 1)
                            dve.wait_ge(chain, links[0])

                        link(dve.tensor_reduce(stat[:, 0, :], src[:, :, :], AX, ALU.add))
                        link(dve.tensor_scalar(stat[:, 1, :], stat[:, 0, :], 1.0 / D, None, ALU.mult))
                        link(dve.tensor_tensor(cent[:, :, :], src[:, :, :], bcast_last(stat[:, 1, :], D), ALU.subtract))
                        link(dve.tensor_tensor(sq[:, :, :], cent[:, :, :], cent[:, :, :], ALU.mult))
                        dve.tensor_reduce(stat[:, 2, :], sq[:, :, :], AX, ALU.add).then_inc(var_made, 1)
                        dve.wait_ge(rooted, 1)
                        link(dve.reciprocal(stat[:, 0, :], stat[:, 3, :]))
                        link(dve.tensor_tensor(dst[:, :, :], cent[:, :, :], bcast_last(stat[:, 0, :], D), ALU.mult))
                        if gain is not None:
                            link(dve.tensor_tensor(dst[:, :, :], dst[:, :, :], bcast_mid(gain, BLOCKS), ALU.mult))
                            link(dve.tensor_tensor(dst[:, :, :], dst[:, :, :], bcast_mid(shift, BLOCKS), ALU.add))

                    @block.scalar
                    def _(act):
                        act.wait_ge(var_made, 1)
                        act.activation(stat[:, 3, :], stat[:, 2, :], ACT.Sqrt, bias=eps_col[:, :],
                                       scale=1.0 / D).then_inc(rooted, 1)

        def node_product(tag, src, width, w2, cols, emit):
            with ExitStack() as ctx:
                part = sb(tag + "_part", [P, GB, width], F32, ctx)
                flat = sb(tag + "_flat", [width, GB * P], F32, ctx)
                flip = ctx.enter_context(nc.psum_tensor(tag + "_flip", [width, 2 * 512], F32))
                prod = ctx.enter_context(nc.psum_tensor(tag + "_prod", [P, GB, 512 if cols > 64 else 64], F32))
                taken, flipped, copied, made, used = (sem(f"{tag}_{n}") for n in ("taken", "flipped", "copied", "made", "used"))
                with nc.Block() as block:
                    @block.scalar
                    def _(act):
                        def step(g):
                            wait(act, flipped, g)
                            act.copy(part[:, :, :], src[:, bass.ds(g * GB, GB), 0:width]).then_inc(taken, 1)
                            wait(act, flipped, g + 1)
                            wait(act, made, g)
                            act.copy(flat[:, :], flip[:, 0:GB * P]).then_inc(copied, 1)
                        groups(act, step)

                    @block.tensor
                    def _(pe):
                        def step(g):
                            wait(pe, copied, g)
                            wait(pe, taken, g + 1)
                            hold(pe)
                            for b in range(GB):
                                mm = pe.transpose(flip[:, b * P:(b + 1) * P], part[:, b, :], eye)
                            mm.then_inc(flipped, 1)
                            wait(pe, used, g)
                            wait(pe, copied, g + 1)
                            hold(pe)
                            for b in range(GB):
                                mm = pe.matmul(prod[:, b, 0:cols], flat[:, b * P:(b + 1) * P], w2, start=True, stop=True)
                            mm.then_inc(made, 1)
                        groups(pe, step)

                    @block.vector
                    def _(dve):
                        def step(g):
                            wait(dve, made, g + 1)
                            emit(dve, g, prod[:, :, 0:cols]).then_inc(used, 1)
                        groups(dve, step)

        def node_mlp(tag, parts, w2, bias1, bias2, func, dst, add):
            halves = len(w2)
            hid_w = 128 if halves > 1 else w2[0].shape[0]
            with ExitStack() as ctx:
                part = [sb(f"{tag}_part{i}", [P, GB, w], F32, ctx) for i, (_, w, _) in enumerate(parts)]
                flat = [sb(f"{tag}_flat{i}", [w, GB * P], F32, ctx) for i, (_, w, _) in enumerate(parts)]
                flip = [ctx.enter_context(nc.psum_tensor(f"{tag}_flip{i}", [w, 2 * 512], F32))
                        for i, (_, w, _) in enumerate(parts[:1])]
                flip = flip * len(parts)
                if len(parts) > 1:
                    wide = max(w for _, w, _ in parts)
                    ctx_flip = ctx.enter_context(nc.psum_tensor(f"{tag}_flipw", [wide, 2 * 512], F32))
                    flip = [flip[0], ctx_flip]
                hid_ps = ctx.enter_context(nc.psum_tensor(f"{tag}_hid", [hid_w, 2 * 512], F32))
                prod = bank(f"{tag}_prod", ctx, P, GB, D)
                hid = sb(f"{tag}_hid_s", [hid_w, halves, GB * P], F32, ctx)
                tmp = sb(f"{tag}_tmp", [hid_w, 5, GB * P], F32, ctx) if func == "mish" else None
                names = ("taken", "flipped", "copied", "hidden", "acted", "made", "used", "capped", "exped", "lin", "chain",
                         "lifted", "summed", "inverted")
                (taken, flipped, copied, hidden, acted, made, used, capped, exped, lin, chain, lifted, lifted2,
                 inverted) = (
                    sem(f"{tag}_{n}") for n in names)
                N = len(parts)
                with nc.Block() as block:
                    @block.scalar
                    def _(act):
                        def step(g):
                            wait(act, flipped, g)
                            for i, (src, w, _) in enumerate(parts):
                                ins = act.copy(part[i][:, :, :], src[:, bass.ds(g * GB, GB), 0:w])
                                ins.then_inc(taken, 1)
                            wait(act, flipped, g + 1)
                            wait(act, hidden, g * halves)
                            for i, (_, w, _) in enumerate(parts):
                                act.copy(flat[i][:, :], flip[i][0:w, 0:GB * P]).then_inc(copied, 1)
                            for h in range(halves):
                                wait(act, hidden, g * halves + (h + 1))
                                wait(act, made, g)
                                if func == "mish":
                                    wait(act, acted, g * halves + h)
                                    act.activation(tmp[:, 0, :], hid_ps[:, 0:GB * P], ACT.Identity,
                                                   bias=bias1[h]).then_inc(lin, 1)
                                    wait(act, capped, g * halves + (h + 1))
                                    act.activation(tmp[:, 2, :], tmp[:, 1, :], ACT.Exp).then_inc(exped, 1)
                                else:
                                    act.activation(hid[:, h, :], hid_ps[:, 0:GB * P], func,
                                                   bias=bias1[h]).then_inc(acted, 1)
                        groups(act, step)

                    @block.tensor
                    def _(pe):
                        def step(g):
                            wait(pe, copied, g * N)
                            wait(pe, taken, g * N + N)
                            hold(pe)
                            for i, (_, w, _) in enumerate(parts):
                                for b in range(GB):
                                    mm = pe.transpose(flip[i][0:w, b * P:(b + 1) * P], part[i][:, b, :], eye)
                            mm.then_inc(flipped, 1)
                            wait(pe, copied, g * N + N)
                            for h in range(halves):
                                wait(pe, acted, g * halves + h)
                                hold(pe)
                                for lo, hi in ((0, 512), (512, GB * P)):
                                    for i, (_, w, w1) in enumerate(parts):
                                        mm = pe.matmul(hid_ps[:, lo:hi], w1[:, h * P:h * P + hid_w], flat[i][:, lo:hi],
                                                       start=(i == 0), stop=(i == N - 1))
                                mm.then_inc(hidden, 1)
                            wait(pe, used, g)
                            wait(pe, acted, g * halves + halves)
                            hold(pe)
                            for b in range(GB):
                                for h in range(halves):
                                    mm = pe.matmul(prod[:, b, :], hid[:, h, b * P:(b + 1) * P], w2[h],
                                                   start=(h == 0), stop=(h == halves - 1))
                            mm.then_inc(made, 1)
                        groups(pe, step)

                    @block.vector
                    def _(dve):
                        def step(g):
                            if func == "mish":
                                for h in range(halves):
                                    n = g * halves + h
                                    y, cap, u, q, r = (tmp[:, j, :] for j in range(5))
                                    wait(dve, lin, n + 1)
                                    dve.tensor_scalar(cap, y, CAP, None, ALU.min).then_inc(capped, 1)
                                    wait(dve, exped, n + 1)
                                    dve.scalar_tensor_tensor(q, u, 2.0, u, ALU.add, ALU.mult).then_inc(lifted, 1)
                                    wait(dve, lifted, n + 1)
                                    dve.tensor_scalar(cap, q, 2.0, None, ALU.add).then_inc(lifted2, 1)
                                    wait(dve, lifted2, n + 1)
                                    dve.reciprocal(r, cap).then_inc(inverted, 1)
                                    wait(dve, inverted, n + 1)
                                    dve.tensor_tensor(q, q, r, ALU.mult).then_inc(chain, 1)
                                    wait(dve, chain, n + 1)
                                    wait(dve, made, g)
                                    dve.tensor_tensor(hid[:, h, :], q, y, ALU.mult).then_inc(acted, 1)
                            wait(dve, made, g + 1)
                            dve.tensor_tensor(dst[:, bass.ds(g * GB, GB), :], prod[:, :, :],
                                              add[:, bass.ds(g * GB, GB), :], ALU.add).then_inc(used, 1)
                        groups(dve, step)
                        dve.wait_ge(used, GROUPS)
                        dve.tensor_tensor(dst[:, :, :], dst[:, :, :], bcast_mid(bias2, BLOCKS), ALU.add).then_inc(used, 1)
                        dve.wait_ge(used, GROUPS + 1)

        def edges01():
            with ExitStack() as ctx:
                we = sb("e0_we", [32, P], F32, ctx)
                be = sb("e0_be", [P, 1], F32, ctx)
                idx = sb("e0_idx", [P, RING, 2, TPC], I32, ctx)
                sent_x = sb("e0_x", [P, RING, TPC, 2, D], F32, ctx)
                attr = sb("e0_attr", [32, RING, CH], F32, ctx)
                keep0 = sb("e0_keep", [P, RING, CH], BF16, ctx)
                y = sb("e0_y", [P, RING, CH], F32, ctx)
                cap, u, w, den, r, t, m, scan = (sb("e0_" + n, [P, 2, CH], F32, ctx) for n in
                                                 ("cap", "u", "w", "den", "r", "t", "m", "scan"))
                rows0 = sb("e0_rows", [P, 2, 2, TPC, D], F32, ctx)
                z = [bank(f"e0_z{s}", ctx, P, CH) for s in range(2)]
                back0 = [bank(f"e0_back{s}", ctx, P, TPC, P) for s in range(2)]
                J, W = STREAMS_S, 2 * P
                rec = sb("e1_rec", [P, RING, J, 2, REC], F32, ctx)
                side = sb("e1_side", [P, 2, 2, J, DE], F32, ctx)
                keep1 = sb("e1_keep", [P, RING, W], BF16, ctx)
                fresh = sb("e1_fresh", [P, 2, W], F32, ctx)
                sums = sb("e1_sum", [P, 2, W], F32, ctx)
                tops = sb("e1_top", [P, 2, W], F32, ctx)
                rows1 = sb("e1_rows", [P, 2, J, 2, 2 * DE], F32, ctx)
                flat = [bank(f"e1_flat{s}", ctx, P, W) for s in range(2)]
                back1 = [bank(f"e1_back{s}", ctx, P, 4, P) for s in range(2)]

                zeroed = sem("e0_zeroed")
                with nc.Block() as block:
                    @block.vector
                    def _(dve):
                        dve.memset(we[:, :], 0.0).then_inc(zeroed, 1)
                        dve.wait_ge(zeroed, 1)
                load([(we[0:16, 0:D], a["L0_We_kernel"]), (we[16:32, D:P], a["L0_We_kernel"]),
                      (be[0:D, :], a["L0_We_bias"].rearrange("(p o) -> p o", o=1)),
                      (be[D:P, :], a["L0_We_bias"].rearrange("(p o) -> p o", o=1))], "e0w")
                (idx_made, z_made, y_made, cap_made, u_made, w_made, den_made, r_made, t_made, m_made, scanned, flipped0,
                 copied0) = (sem("e0_" + n) for n in ("si", "sz", "sy", "sc", "su", "sw", "sd", "sr", "st", "sm", "ss", "sf", "so"))
                flat_made, fresh_made, summed, topped, flipped1, copied1, ids_made, sided = (
                    sem("e1_" + n) for n in ("sf", "sr", "ss", "st", "sb", "sc", "si", "sd"))
                got, in0, in1, in_keep0 = ([sem(f"e01_{n}{s}") for s in range(RING)] for n in ("got", "in0", "in1", "ik"))
                out0, out1 = ([sem(f"e01_{n}{s}") for s in range(2)] for n in ("out0", "out1"))
                rec_streams = rec_s.rearrange("(j u) f -> j u f", j=J)
                run1_streams = run1.rearrange("(j u) f -> j u f", j=J)
                run0_streams = run0.rearrange("(h u) f -> h u f", h=2)
                attr_halves = a["attr16_t"].rearrange("f (h u) -> h f u", h=2)
                keep_d_halves = keep["d"].rearrange("(h u) -> h u", h=2)
                keep_s_streams = keep["s"].rearrange("(j u) -> j u", j=J)
                src_halves = src_i[:, :].rearrange("p (h t) -> p h t", h=2)
                ids_quarters = ids_s[:, :].rearrange("p (j t) -> p j t", j=J)
                weight_quarters = weight_s[:, :].rearrange("p (j t) -> p j t", j=J)
                with nc.Block() as block:
                    @block.gpsimd
                    def _(pool):
                        def gather(un):
                            wait(pool, got[un.s], un.landed_before(2 * TPC))
                            pool.tensor_copy(idx[:, un.s], src_halves[:, :, bass.ds(un.n * TPC, TPC)]).then_inc(idx_made, 1)
                            wait(pool, idx_made, un.n + 1)
                            wait(pool, z_made, un.n + 1 - RING)
                            hold(pool)
                            for q in range(TPC):
                                for h in range(2):
                                    pool.indirect_dma_start(sent_x[:, un.s, q, h, :], None, a["x"],
                                                            bass.IndirectOffsetOnAxis(idx[:, un.s, h, q:q + 1], 0)
                                                            ).then_inc(got[un.s], 16)
                        pipeline(pool, [(gather, 0)], UNITS, RING)

                    @block.sync
                    def _(sp):
                        def fetch(un):
                            wait(sp, z_made, un.n + 1 - RING)
                            hold(sp)
                            sp.dma_start(attr[:, un.s], attr_halves[:, :, bass.ds(un.n * CH, CH)]).then_inc(in0[un.s], 16)
                            wait(sp, sided, un.n + 1 - RING)
                            hold(sp)
                            wait(sp, ids_made, (un.n + 1 - RING) * 2)
                            hold(sp)
                            sp.dma_start(rec[:, un.s], rec_streams[:, bass.ds(un.n * W, W), :]
                                         .rearrange("j (p t) f -> p j (t f)", p=P)).then_inc(in1[un.s], 16)
                            wait(sp, summed, un.n + 1 - RING)
                            hold(sp)
                            wait(sp, fresh_made, un.n + 1 - RING)
                            hold(sp)
                            sp.dma_start(keep1[:, un.s], keep_s_streams[:, bass.ds(un.n * W, W)].unsqueeze(1)
                                         .to_broadcast([J, DE, W])).then_inc(in1[un.s], 16)

                        def fetch_keep0(un):
                            wait(sp, scanned, un.n + 1 - RING)
                            hold(sp)
                            sp.dma_start(keep0[:, un.s], keep_d_halves[:, bass.ds(un.n * CH, CH)].unsqueeze(1)
                                         .to_broadcast([2, D, CH])).then_inc(in_keep0[un.s], 16)
                        pipeline(sp, [(fetch, 0), (fetch_keep0, 2)], UNITS, RING)

                    @block.tensor
                    def _(pe):
                        def turn_in(un):
                            wait(pe, summed, un.n - 1)
                            wait(pe, topped, un.n - 1)
                            wait(pe, sided, un.n + 1)
                            hold(pe)
                            for q in range(2):
                                mm = pe.transpose(tile_cols(flat[un.p], q, 2),
                                                  side[:, un.p, q].rearrange("p j f -> p (j f)"), eye)
                            mm.then_inc(flat_made, 1)

                        def make_z(un):
                            wait(pe, in0[un.s], un.landed(1))
                            wait(pe, got[un.s], un.landed(2 * TPC))
                            wait(pe, y_made, un.n - 1)
                            hold(pe)
                            pe.matmul(z[un.p], we[:, :], attr[:, un.s], start=True, stop=False)
                            for q in range(TPC):
                                mm = pe.matmul(tile_cols(z[un.p], q, TPC),
                                               sent_x[:, un.s, q].rearrange("p h f -> p (h f)"), eye,
                                               start=False, stop=(q == TPC - 1))
                            mm.then_inc(z_made, 1)

                        def turn_out1(un):
                            wait(pe, summed, un.n + 1)
                            wait(pe, topped, un.n + 1)
                            wait(pe, copied1, (un.n - 1) * 2)
                            hold(pe)
                            for q in range(2):
                                pe.transpose(back1[un.p][:, q, :], tile_cols(sums[:, un.p], q, 2), eye)
                                mm = pe.transpose(back1[un.p][:, 2 + q, :], tile_cols(tops[:, un.p], q, 2), eye)
                            mm.then_inc(flipped1, 1)

                        def turn_out0(un):
                            wait(pe, scanned, un.n + 1)
                            wait(pe, copied0, un.n - 1)
                            hold(pe)
                            for q in range(TPC):
                                mm = pe.transpose(back0[un.p][:, q, :], tile_cols(scan[:, un.p], q, TPC), eye)
                            mm.then_inc(flipped0, 1)
                        pipeline(pe, [(turn_out0, 4), (turn_in, 0), (make_z, 0), (turn_out1, 2)], UNITS, RING)

                    @block.scalar
                    def _(act):
                        def store0(un):
                            wait(act, flipped0, un.n + 1)
                            wait(act, out0[un.p], un.uses2 * 16)
                            act.copy(rows0[:, un.p], back0[un.p].rearrange("p t (h f) -> p h t f", h=2)).then_inc(copied0, 1)
                            wait(act, copied0, un.n + 1)
                            act.dma_start(run0_streams[:, bass.ds(un.n * CH, CH), :].rearrange("h (p t) f -> p h (t f)", p=P),
                                          rows0[:, un.p]).then_inc(out0[un.p], 16)

                        def store1(un):
                            wait(act, flipped1, un.n + 1)
                            wait(act, out1[un.p], un.uses2 * 16)
                            for k in range(2):
                                act.copy(rows1[:, un.p, :, :, k * DE:(k + 1) * DE],
                                         back1[un.p][:, 2 * k:2 * k + 2, :].rearrange("p q (j f) -> p j q f", j=J)
                                         ).then_inc(copied1, 1)
                            wait(act, copied1, (un.n + 1) * 2)
                            act.dma_start(run1_streams[:, bass.ds(un.n * W, W), :].rearrange("j (p t) f -> p j (t f)", p=P),
                                          rows1[:, un.p]).then_inc(out1[un.p], 16)

                        def front1(un):
                            wait(act, in1[un.s], un.landed(2))
                            wait(act, flat_made, un.n - 1)
                            act.copy(side[:, un.p], rec[:, un.s, :, :, 0:DE].rearrange("p j q f -> p q j f")).then_inc(sided, 1)
                            wait(act, topped, un.n - 1)
                            act.activation(fresh[:, un.p], keep1[:, un.s], ACT.Copy, bias=-BIG, scale=BIG).then_inc(fresh_made, 1)

                        def bias(un):
                            wait(act, z_made, un.n + 1)
                            wait(act, cap_made, un.n + 1 - RING)
                            wait(act, m_made, un.n + 1 - RING)
                            act.activation(y[:, un.s], z[un.p], ACT.Identity, bias=be[:, :]).then_inc(y_made, 1)

                        def lift(un):
                            wait(act, w_made, un.n + 1)
                            wait(act, r_made, un.n - 1)
                            act.activation(den[:, un.p], w[:, un.p], ACT.Copy, bias=2.0).then_inc(den_made, 1)

                        def expo(un):
                            wait(act, cap_made, un.n + 1)
                            wait(act, w_made, un.n - 1)
                            act.activation(u[:, un.p], cap[:, un.p], ACT.Exp).then_inc(u_made, 1)
                        pipeline(act, [(store0, 4), (front1, 0), (bias, 1), (lift, 2), (expo, 1), (store1, 3)], UNITS, RING)
                        for s in range(2):
                            act.wait_ge(out0[s], uses_of(s, UNITS, 2) * 16)
                            act.wait_ge(out1[s], uses_of(s, UNITS, 2) * 16)

                    @block.vector
                    def _(dve):
                        def square(un):
                            wait(dve, u_made, un.n + 1)
                            wait(dve, den_made, un.n - 1)
                            wait(dve, t_made, un.n - 1)
                            dve.scalar_tensor_tensor(w[:, un.p], u[:, un.p], 2.0, u[:, un.p], ALU.add,
                                                     ALU.mult).then_inc(w_made, 1)

                        def bound(un):
                            wait(dve, y_made, un.n + 1)
                            wait(dve, u_made, un.n - 1)
                            dve.tensor_scalar(cap[:, un.p], y[:, un.s], CAP, None, ALU.min).then_inc(cap_made, 1)

                        def mish(un):
                            wait(dve, den_made, un.n + 1)
                            dve.reciprocal(r[:, un.p], den[:, un.p]).then_inc(r_made, 1)
                            wait(dve, r_made, un.n + 1)
                            wait(dve, w_made, un.n + 1)
                            dve.tensor_tensor(t[:, un.p], w[:, un.p], r[:, un.p], ALU.mult).then_inc(t_made, 1)
                            wait(dve, t_made, un.n + 1)
                            wait(dve, y_made, un.n + 1)
                            wait(dve, scanned, un.n - 1)
                            dve.tensor_tensor(m[:, un.p], t[:, un.p], y[:, un.s], ALU.mult).then_inc(m_made, 1)
                            wait(dve, m_made, un.n + 1)
                            wait(dve, in_keep0[un.s], un.landed(1))
                            wait(dve, scanned, un.n)
                            wait(dve, flipped0, un.n - 1)
                            dve.tensor_tensor_scan(scan[:, un.p], keep0[:, un.s], m[:, un.p],
                                                   0.0 if un.first else scan[:, 1 - un.p, CH - 1:CH],
                                                   ALU.mult, ALU.add).then_inc(scanned, 1)

                        def layer1(un):
                            wait(dve, in1[un.s], un.landed(2))
                            tiles = bass.ds(un.n * 2, 2)
                            dve.tensor_copy(ids_quarters[:, :, tiles], rec[:, un.s, :, :, RECF].bitcast(I32)).then_inc(ids_made, 1)
                            dve.tensor_copy(weight_quarters[:, :, tiles], rec[:, un.s, :, :, DE]).then_inc(ids_made, 1)
                            wait(dve, flat_made, un.n + 1)
                            wait(dve, flipped1, un.n - 1)
                            wait(dve, summed, un.n)
                            dve.tensor_tensor_scan(sums[:, un.p], keep1[:, un.s], flat[un.p],
                                                   0.0 if un.first else sums[:, 1 - un.p, W - 1:W],
                                                   ALU.mult, ALU.add).then_inc(summed, 1)
                            wait(dve, fresh_made, un.n + 1)
                            wait(dve, topped, un.n)
                            dve.tensor_tensor_scan(tops[:, un.p], fresh[:, un.p], flat[un.p],
                                                   -BIG if un.first else tops[:, 1 - un.p, W - 1:W],
                                                   ALU.add, ALU.max).then_inc(topped, 1)
                        pipeline(dve, [(square, 2), (bound, 1), (mish, 3), (layer1, 1)], UNITS, RING)
                        dve.wait_ge(ids_made, UNITS * 2)

        def edges2():
            with ExitStack() as ctx:
                we = sb("e2_we", [DE, P], F32, ctx)
                heads = sb("e2_heads", [P, P], F32, ctx)
                idx = sb("e2_idx", [P, RING, TPC], I32, ctx)
                q_g = sb("e2_qg", [P, RING, TPC, P], F32, ctx)
                kv_g = sb("e2_kv", [P, RING, TPC, 2 * P], F32, ctx)
                attr = sb("e2_attr", [DE, RING, CH], F32, ctx)
                keep2 = sb("e2_keep", [P, RING, CH], BF16, ctx)
                qf, qk, low, drop, num, den = (sb("e2_" + n, [P, 2, CH], F32, ctx) for n in
                                               ("qf", "qk", "low", "drop", "num", "den"))
                fresh, pr, fade = (sb("e2_" + n, [P, RING, CH], F32, ctx) for n in ("fresh", "pr", "fade"))
                pv = sb("e2_pv", [P, CH], F32, ctx)
                top_ = sb("e2_top", [P, 2, CH + 1], F32, ctx)
                rows = sb("e2_rows", [P, 2, TPC, 130], F32, ctx)
                q_p, k_p = [bank(f"e2_qp{s}", ctx, P, CH) for s in range(1)], [bank(f"e2_kp{s}", ctx, P, CH) for s in range(2)]
                v_p = [bank(f"e2_vp{s}", ctx, P, CH) for s in range(2)]
                al_p, num_p, den_p = bank("e2_alp", ctx, P, CH), bank("e2_nump", ctx, P, TPC, P), bank("e2_denp", ctx, P, TPC, 2)
                load([(we[:, :], a["L2_We"]), (heads[:, :], a["heads"])], "e2w")
                names = ("idx", "q", "k", "v", "qf", "qk", "al", "fresh", "edge", "top", "low", "rise", "drop", "pr", "fade",
                         "pv", "num", "den", "flip", "copy")
                (idx_made, q_made, k_made, v_made, filled, qk_made, al_made, fresh_made, edge_made, top_made, low_made,
                 rise_made, drop_made, pr_made, fade_made, pv_made, num_made, den_made, flipped, copied) = (
                     sem("e2_s" + n) for n in names)
                got, q_in, loaded, stored = ([sem(f"e2_{n}{s}") for s in range(RING)] for n in ("got", "qi", "ld", "st_"))
                with nc.Block() as block:
                    @block.gpsimd
                    def _(pool):
                        def gather(ch):
                            wait(pool, got[ch.s], ch.landed_before(TPC))
                            pool.tensor_copy(idx[:, ch.s], src_i[:, bass.ds(ch.n * TPC, TPC)]).then_inc(idx_made, 1)
                            wait(pool, idx_made, ch.n + 1)
                            wait(pool, v_made, ch.n + 1 - RING)
                            hold(pool)
                            for t in range(TPC):
                                pool.indirect_dma_start(kv_g[:, ch.s, t, :], None, kv_tab,
                                                        bass.IndirectOffsetOnAxis(idx[:, ch.s, t:t + 1], 0)
                                                        ).then_inc(got[ch.s], 16)
                        pipeline(pool, [(gather, 0)])

                    @block.sync
                    def _(sp):
                        def fetch(ch):
                            rows_ = bass.ds(ch.n * CH, CH)
                            wait(sp, q_made, ch.n + 1 - RING)
                            hold(sp)
                            sp.dma_start(q_g[:, ch.s], q_rows[rows_, :].rearrange("(p t) f -> p t f", p=P)
                                         ).then_inc(q_in[ch.s], 16)
                            wait(sp, v_made, ch.n + 1 - RING)
                            hold(sp)
                            wait(sp, filled, ch.n + 1 - RING)
                            hold(sp)
                            wait(sp, fresh_made, ch.n + 1 - RING)
                            hold(sp)
                            sp.dma_start(attr[:, ch.s], a["attr32_t"][:, rows_]).then_inc(loaded[ch.s], 16)
                            sp.dma_start(keep2[:, ch.s], keep["d"][rows_].partition_broadcast(P)).then_inc(loaded[ch.s], 16)
                        pipeline(sp, [(fetch, 0)])

                    @block.tensor
                    def _(pe):
                        def plus_edges(ch, dst, j):
                            pe.matmul(dst, we[:, :], attr[:, ch.s], start=True, stop=False)
                            for t in range(TPC):
                                mm = pe.matmul(tile_cols(dst, t, TPC), kv_g[:, ch.s, t, j * P:(j + 1) * P], eye,
                                               start=False, stop=(t == TPC - 1))
                            return mm

                        def make_qk(ch):
                            wait(pe, q_in[ch.s], ch.landed(1))
                            wait(pe, filled, ch.n)
                            hold(pe)
                            for t in range(TPC):
                                mm = pe.transpose(tile_cols(q_p[0], t, TPC), q_g[:, ch.s, t, :], eye)
                            mm.then_inc(q_made, 1)
                            wait(pe, got[ch.s], ch.landed(TPC))
                            wait(pe, loaded[ch.s], ch.landed(2))
                            wait(pe, qk_made, ch.n - 1)
                            hold(pe)
                            plus_edges(ch, k_p[ch.p], 0).then_inc(k_made, 1)

                        def make_al(ch):
                            wait(pe, qk_made, ch.n + 1)
                            wait(pe, low_made, ch.n)
                            hold(pe)
                            pe.matmul(al_p, heads[:, :], qk[:, ch.p], start=True, stop=True).then_inc(al_made, 1)

                        def make_v(ch):
                            wait(pe, pv_made, ch.n - 1)
                            hold(pe)
                            plus_edges(ch, v_p[ch.p], 1).then_inc(v_made, 1)

                        def turn(ch):
                            wait(pe, num_made, ch.n + 1)
                            wait(pe, den_made, ch.n + 1)
                            wait(pe, copied, ch.n * 2)
                            hold(pe)
                            for t in range(TPC):
                                pe.transpose(num_p[:, t, :], tile_cols(num[:, ch.p], t, TPC), eye)
                                mm = pe.matmul(den_p[:, t, :], tile_cols(den[:, ch.p], t, TPC), eye[:, 0:P:D],
                                               start=True, stop=True)
                            mm.then_inc(flipped, 1)
                        pipeline(pe, [(make_qk, 0), (make_al, 1), (make_v, 1), (turn, 3)])

                    @block.scalar
                    def _(act):
                        def front(ch):
                            wait(act, loaded[ch.s], ch.landed(2))
                            wait(act, drop_made, ch.n + 1 - RING)
                            act.activation(fresh[:, ch.s], keep2[:, ch.s], ACT.Copy, bias=-BIG, scale=BIG).then_inc(fresh_made, 1)

                        def weigh(ch):
                            wait(act, low_made, ch.n + 1)
                            wait(act, den_made, ch.n + 1 - RING)
                            act.activation(pr[:, ch.s], low[:, ch.p], ACT.Exp, scale=D ** -0.5).then_inc(pr_made, 1)
                            wait(act, drop_made, ch.n + 1)
                            act.activation(fade[:, ch.s], drop[:, ch.p], ACT.Exp, scale=D ** -0.5).then_inc(fade_made, 1)

                        def store(ch):
                            wait(act, flipped, ch.n + 1)
                            wait(act, stored[ch.p], (ch.uses2) * 16)
                            act.copy(rows[:, ch.p, :, 0:P], num_p).then_inc(copied, 1)
                            act.copy(rows[:, ch.p, :, P:130], den_p).then_inc(copied, 1)
                            wait(act, copied, ch.n * 2 + 2)
                            act.dma_start(run2[bass.ds(ch.n * CH, CH), :].rearrange("(p t) f -> p t f", p=P),
                                          rows[:, ch.p]).then_inc(stored[ch.p], 16)
                        pipeline(act, [(front, 0), (weigh, 1), (store, 3)])
                        for s in range(2):
                            act.wait_ge(stored[s], uses_of(s, CHUNKS, 2) * 16)

                    @block.vector
                    def _(dve):
                        dve.memset(top_[:, 1, CH:CH + 1], 0.0).then_inc(edge_made, 1)

                        def front(ch):
                            wait(dve, q_made, ch.n + 1)
                            wait(dve, loaded[ch.s], ch.landed(2))
                            wait(dve, qk_made, ch.n)
                            dve.tensor_tensor_scan(qf[:, ch.p], keep2[:, ch.s], q_p[0],
                                                   0.0 if ch.first else qf[:, 1 - ch.p, CH - 1:CH],
                                                   ALU.mult, ALU.add).then_inc(filled, 1)
                            wait(dve, filled, ch.n + 1)
                            wait(dve, k_made, ch.n + 1)
                            wait(dve, al_made, ch.n - 1)
                            dve.tensor_tensor(qk[:, ch.p], qf[:, ch.p], k_p[ch.p], ALU.mult).then_inc(qk_made, 1)

                        def maxima(ch):
                            wait(dve, drop_made, ch.n)
                            if ch.first:
                                dve.wait_ge(edge_made, 1)
                            dve.tensor_copy(top_[:, ch.p, 0:1], top_[:, 1 - ch.p, CH:CH + 1]).then_inc(edge_made, 1)
                            wait(dve, edge_made, ch.n + 2)
                            wait(dve, al_made, ch.n + 1)
                            wait(dve, fresh_made, ch.n + 1)
                            dve.tensor_tensor_scan(top_[:, ch.p, 1:CH + 1], fresh[:, ch.s], al_p,
                                                   top_[:, ch.p, 0:1], ALU.add, ALU.max).then_inc(top_made, 1)
                            wait(dve, top_made, ch.n + 1)
                            wait(dve, pr_made, ch.n - 1)
                            dve.tensor_tensor(low[:, ch.p], al_p, top_[:, ch.p, 1:CH + 1], ALU.subtract).then_inc(low_made, 1)
                            wait(dve, fade_made, ch.n - 1)
                            dve.tensor_tensor(drop[:, ch.p], top_[:, ch.p, 0:CH], top_[:, ch.p, 1:CH + 1],
                                              ALU.subtract).then_inc(rise_made, 1)
                            wait(dve, rise_made, ch.n + 1)
                            dve.tensor_tensor(drop[:, ch.p], drop[:, ch.p], fresh[:, ch.s], ALU.add).then_inc(drop_made, 1)

                        def sums(ch):
                            wait(dve, pr_made, ch.n + 1)
                            wait(dve, v_made, ch.n + 1)
                            wait(dve, num_made, ch.n)
                            dve.tensor_tensor(pv[:, :], pr[:, ch.s], v_p[ch.p], ALU.mult).then_inc(pv_made, 1)
                            wait(dve, fade_made, ch.n + 1)
                            wait(dve, den_made, ch.n)
                            wait(dve, flipped, ch.n - 1)
                            dve.tensor_tensor_scan(den[:, ch.p], fade[:, ch.s], pr[:, ch.s],
                                                   0.0 if ch.first else den[:, 1 - ch.p, CH - 1:CH],
                                                   ALU.mult, ALU.add).then_inc(den_made, 1)
                            wait(dve, pv_made, ch.n + 1)
                            dve.tensor_tensor_scan(num[:, ch.p], fade[:, ch.s], pv[:, :],
                                                   0.0 if ch.first else num[:, 1 - ch.p, CH - 1:CH],
                                                   ALU.mult, ALU.add).then_inc(num_made, 1)
                        pipeline(dve, [(front, 0), (maxima, 1), (sums, 2)])

        def edges3():
            with ExitStack() as ctx:
                w_d = sb("e3_wd", [P, P], F32, ctx)
                w2 = sb("e3_w2", [P, P], F32, ctx)
                b1, b1v = column("e3_b1", a["L3_eb1"], ctx)
                b2, b2v = column("e3_b2", a["L3_eb2"], ctx)
                idx = sb("e3_idx", [P, RING, TPC], I32, ctx)
                a_g = sb("e3_ag", [P, RING, TPC, P], F32, ctx)
                b_g = sb("e3_bg", [P, RING, TPC, P], F32, ctx)
                keep3 = sb("e3_keep", [P, RING, CH], BF16, ctx)
                af, zs, h1, h2, scan = (sb("e3_" + n, [P, 2, CH], F32, ctx) for n in ("af", "zs", "h1", "h2", "scan"))
                rows = sb("e3_rows", [P, 2, TPC, P], F32, ctx)
                ps = lambda n: [bank(f"{n}{s}", ctx, P, CH) for s in range(2)]
                a_p, z, z2, back = ps("e3_ap"), ps("e3_z"), ps("e3_z2"), ps("e3_back")
                load([(w_d[:, :], a["L3_eW1"][2 * D:2 * D + 1, :].rearrange("a b -> (a b)").partition_broadcast(P)),
                      (w2[:, :], a["L3_eW2"]), (b1[:, :], b1v), (b2[:, :], b2v)], "e3w")

                def cols(ap, t):
                    return tile_cols(ap[:, t // 2 * 2 * P:(t // 2 + 1) * 2 * P], t % 2, 2)
                names = ("idx", "fold", "a", "z", "af", "zs", "h1", "z2", "h2", "scan", "flip", "copy")
                (idx_made, folded, a_made, z_made, filled, zs_made, h1_made, z2_made, h2_made, scanned, flipped, copied) = (
                    sem("e3_s" + n) for n in names)
                got, a_in = ([sem(f"e3_{n}{s}") for s in range(RING)] for n in ("got", "ai"))
                kept, stored = [sem(f"e3_kp{s}") for s in range(RING)], [sem(f"e3_st{s}") for s in range(2)]
                with nc.Block() as block:
                    @block.gpsimd
                    def _(pool):
                        def gather(ch):
                            wait(pool, got[ch.s], ch.landed_before(TPC))
                            pool.tensor_copy(idx[:, ch.s], ids_s[:, bass.ds(ch.n * TPC, TPC)]).then_inc(idx_made, 1)
                            wait(pool, idx_made, ch.n + 1)
                            wait(pool, z_made, ch.n + 1 - RING)
                            hold(pool)
                            for t in range(TPC):
                                pool.indirect_dma_start(b_g[:, ch.s, t, :], None, b_tab,
                                                        bass.IndirectOffsetOnAxis(idx[:, ch.s, t:t + 1], 0)
                                                        ).then_inc(got[ch.s], 16)
                        pipeline(pool, [(gather, 0)])

                    @block.sync
                    def _(sp):
                        def fetch(ch):
                            rows_ = bass.ds(ch.n * CH, CH)
                            wait(sp, a_made, ch.n + 1 - RING)
                            hold(sp)
                            sp.dma_start(a_g[:, ch.s], a_rows[rows_, :].rearrange("(u p q) f -> p u (q f)", p=P, q=2)
                                         ).then_inc(a_in[ch.s], 16)
                            wait(sp, scanned, ch.n + 1 - RING)
                            hold(sp)
                            sp.dma_start(keep3[:, ch.s], keep["s"][rows_].partition_broadcast(P)).then_inc(kept[ch.s], 16)
                        pipeline(sp, [(fetch, 0)])

                    @block.tensor
                    def _(pe):
                        def turn_a(ch):
                            wait(pe, a_in[ch.s], ch.landed(1))
                            wait(pe, filled, ch.n - 1)
                            hold(pe)
                            for t in range(TPC):
                                mm = pe.transpose(cols(a_p[ch.p], t), a_g[:, ch.s, t, :], eye)
                            mm.then_inc(a_made, 1)

                        def turn_b(ch):
                            wait(pe, folded, (ch.n + 1) * TPC)
                            wait(pe, zs_made, ch.n - 1)
                            hold(pe)
                            for t in range(TPC):
                                mm = pe.transpose(cols(z[ch.p], t), b_g[:, ch.s, t, :], eye)
                            mm.then_inc(z_made, 1)

                        def second(ch):
                            wait(pe, h1_made, ch.n + 1)
                            wait(pe, h2_made, ch.n - 1)
                            hold(pe)
                            pe.matmul(z2[ch.p], w2[:, :], h1[:, ch.p], start=True, stop=True).then_inc(z2_made, 1)

                        def turn_out(ch):
                            wait(pe, scanned, ch.n + 1)
                            wait(pe, copied, ch.n - 1)
                            hold(pe)
                            for t in range(TPC):
                                mm = pe.transpose(back[ch.p][:, t * P:(t + 1) * P], cols(scan[:, ch.p], t), eye)
                            mm.then_inc(flipped, 1)
                        pipeline(pe, [(turn_a, 0), (turn_b, 0), (second, 1), (turn_out, 2)])

                    @block.scalar
                    def _(act):
                        def first(ch):
                            wait(act, zs_made, ch.n + 1)
                            wait(act, z2_made, ch.n - 1)
                            act.activation(h1[:, ch.p], zs[:, ch.p], ACT.Silu, bias=b1[:, :]).then_inc(h1_made, 1)

                        def second(ch):
                            wait(act, z2_made, ch.n + 1)
                            wait(act, scanned, ch.n - 1)
                            act.activation(h2[:, ch.p], z2[ch.p], ACT.Silu, bias=b2[:, :]).then_inc(h2_made, 1)

                        def store(ch):
                            wait(act, flipped, ch.n + 1)
                            wait(act, stored[ch.p], ch.uses2 * 16)
                            act.copy(rows[:, ch.p].rearrange("p t f -> p (t f)"), back[ch.p]).then_inc(copied, 1)
                            wait(act, copied, ch.n + 1)
                            act.dma_start(run3[bass.ds(ch.n * CH, CH), :].rearrange("(u p q) f -> p u (q f)", p=P, q=2),
                                          rows[:, ch.p]).then_inc(stored[ch.p], 16)
                        pipeline(act, [(first, 1), (second, 1), (store, 2)])
                        for s in range(2):
                            act.wait_ge(stored[s], uses_of(s, CHUNKS, 2) * 16)

                    @block.vector
                    def _(dve):
                        def fold(ch):
                            wait(dve, got[ch.s], ch.landed(TPC))
                            for t in range(TPC):
                                dve.scalar_tensor_tensor(b_g[:, ch.s, t, :], w_d[:, :], weight_s[:, bass.ds(ch.n * TPC + t, 1)],
                                                         b_g[:, ch.s, t, :], ALU.mult, ALU.add).then_inc(folded, 1)

                        def fill(ch):
                            wait(dve, a_made, ch.n + 1)
                            wait(dve, kept[ch.s], ch.landed(1))
                            wait(dve, filled, ch.n)
                            wait(dve, zs_made, ch.n - 1)
                            dve.tensor_tensor_scan(af[:, ch.p], keep3[:, ch.s], a_p[ch.p],
                                                   0.0 if ch.first else af[:, 1 - ch.p, CH - 1:CH],
                                                   ALU.mult, ALU.add).then_inc(filled, 1)

                        def add(ch):
                            wait(dve, z_made, ch.n + 1)
                            wait(dve, filled, ch.n + 1)
                            wait(dve, h1_made, ch.n - 1)
                            dve.tensor_tensor(zs[:, ch.p], af[:, ch.p], z[ch.p], ALU.add).then_inc(zs_made, 1)

                        def scan_(ch):
                            wait(dve, h2_made, ch.n + 1)
                            wait(dve, scanned, ch.n)
                            wait(dve, flipped, ch.n - 1)
                            dve.tensor_tensor_scan(scan[:, ch.p], keep3[:, ch.s], h2[:, ch.p],
                                                   0.0 if ch.first else scan[:, 1 - ch.p, CH - 1:CH],
                                                   ALU.mult, ALU.add).then_inc(scanned, 1)
                        pipeline(dve, [(fold, 0), (add, 1), (fill, 0), (scan_, 2)])

        def small(tag, build):
            chain = sem(tag + "_chain")
            with nc.Block() as block:
                @block.vector
                def _(dve):
                    n = 0
                    for make in build:
                        make(dve).then_inc(chain, 1)
                        n += 1
                        dve.wait_ge(chain, n)

        def bias_column(tag, w_rows, vec, base, dst, ctx):
            halves = len(dst)
            ps = ctx.enter_context(nc.psum_tensor(tag + "_ps", [P, halves], F32))
            made, added = sem(tag + "_made"), sem(tag + "_added")
            with nc.Block() as block:
                @block.tensor
                def _(pe):
                    for h in range(halves):
                        mm = pe.matmul(ps[:, h:h + 1], w_rows[:, h * P:(h + 1) * P], vec, start=True, stop=True)
                    mm.then_inc(made, 1)

                @block.vector
                def _(dve):
                    dve.wait_ge(made, 1)
                    for h in range(halves):
                        last = dve.tensor_tensor(dst[h], ps[:, h:h + 1], base[h], ALU.add)
                        last.then_inc(added, 1)
                    dve.wait_ge(added, halves)

        def nodes0():
            with ExitStack() as ctx:
                agg = sb("n0_agg", [P, BLOCKS, D], F32, ctx)
                w1a = sb("n0_w1a", [D, 2 * P], F32, ctx)
                w1g = sb("n0_w1g", [D, 2 * P], F32, ctx)
                w2 = [sb(f"n0_w2{h}", [P, D], F32, ctx) for h in range(2)]
                glob, gv = column("n0_glob", a["L0_globals_"].rearrange("a b -> (a b)"), ctx)
                b1 = sb("n0_b1", [P, 2], F32, ctx)
                b1g = [sb(f"n0_b1g{h}", [P, 1], F32, ctx) for h in range(2)]
                b2 = sb("n0_b2", [P, D], F32, ctx)
                eps = sb("n0_eps", [P, 1], F32, ctx)
                load([(w1a[:, :], a["L0_W1"][0:D, :]), (w1g[:, :], a["L0_W1"][D:2 * D, :]),
                      (w2[0][:, :], a["L0_W2"][0:P, :]), (w2[1][:, :], a["L0_W2"][P:2 * P, :]), (glob[:, :], gv),
                      (b1[:, 0:1], a["L0_b1"][0:P].rearrange("(p o) -> p o", o=1)),
                      (b1[:, 1:2], a["L0_b1"][P:2 * P].rearrange("(p o) -> p o", o=1)),
                      (b2[:, :], a["L0_b2"].partition_broadcast(P)),
                      (eps[:, :], a["L0_epsilon"].rearrange("a b -> (a b)").partition_broadcast(P))], "n0")
                collect("n0c", run0, 1, agg)
                piece = sb("n0_piece", [P, BLOCKS, D], F32, ctx)
                mend("n0e", run0, 1, lambda c, j, row: [
                    lambda dve: dve.tensor_tensor(piece[:, :, :], bcast_last(spans[1][:, j, :], D), bcast_mid(row, BLOCKS), ALU.mult),
                    lambda dve: dve.tensor_tensor(agg[:, :, :], agg[:, :, :], piece[:, :, :], ALU.add)])
                with ExitStack() as c2:
                    bias_column("n0b", w1g, glob[:, :], [b1[:, 0:1], b1[:, 1:2]], [t[:, :] for t in b1g], c2)
                small("n0s", [
                    lambda dve: dve.tensor_scalar(eps[:, :], eps[:, :], 1.0, None, ALU.add),
                    lambda dve: dve.scalar_tensor_tensor(agg[:, :, :], x[:, :, :], eps[:, :], agg[:, :, :],
                                                         ALU.mult, ALU.add)])
                node_mlp("n0m", [(agg, D, w1a)], [t[:, :] for t in w2], [t[:, :] for t in b1g], b2[:, :], "mish", x, x)
                norm("n0n", x, x)

        def nodes1():
            with ExitStack() as ctx:
                agg = sb("n1_agg", [P, BLOCKS, 2 * DE], F32, ctx)
                cat = sb("n1_cat", [P, BLOCKS, 3 * DE], F32, ctx)
                w1 = sb("n1_w1", [3 * DE, P], F32, ctx)
                w1u, w1uv = column("n1_w1u", a["L1_W1"][3 * DE:3 * DE + 1, :].rearrange("a b -> (a b)"), ctx)
                b1, b1v = column("n1_b1", a["L1_b1"], ctx)
                u0 = sb("n1_u0", [P, 1], F32, ctx)
                w2 = sb("n1_w2", [P, D], F32, ctx)
                b2 = sb("n1_b2", [P, D], F32, ctx)
                inv = sb("n1_inv", [P, 2, BLOCKS], F32, ctx)
                load([(w1[:, :], a["L1_W1"][0:3 * DE, :]), (w1u[:, :], w1uv), (b1[:, :], b1v),
                      (u0[:, :], a["L1_u"][0:1, :].rearrange("a b -> (a b)").partition_broadcast(P)),
                      (w2[:, :], a["L1_W2"]), (b2[:, :], a["L1_b2"].partition_broadcast(P))], "n1")
                collect("n1c", run1, 0, agg)
                piece = sb("n1_piece", [P, BLOCKS, DE], F32, ctx)
                absent = sb("n1_absent", [P, STREAMS_S - 1, BLOCKS], F32, ctx)
                small("n1a", [lambda dve: dve.tensor_scalar(absent[:, :, :], spans[0][:, :, :], BIG, -BIG, ALU.mult, ALU.add)])
                mend("n1e", run1, 0, lambda c, j, row: [
                    lambda dve: dve.tensor_tensor(piece[:, :, :], bcast_last(spans[0][:, j, :], DE),
                                                  bcast_mid(row[:, 0:DE], BLOCKS), ALU.mult),
                    lambda dve: dve.tensor_tensor(agg[:, :, 0:DE], agg[:, :, 0:DE], piece[:, :, :], ALU.add),
                    lambda dve: dve.tensor_tensor(piece[:, :, :], bcast_last(absent[:, j, :], DE),
                                                  bcast_mid(row[:, DE:2 * DE], BLOCKS), ALU.add),
                    lambda dve: dve.tensor_tensor(agg[:, :, DE:2 * DE], agg[:, :, DE:2 * DE], piece[:, :, :], ALU.max)])
                small("n1s", [
                    lambda dve: dve.scalar_tensor_tensor(b1[:, :], w1u[:, :], u0[:, :], b1[:, :], ALU.mult, ALU.add),
                    lambda dve: dve.tensor_scalar(inv[:, 0, :], count[0][:, :], 1.0, None, ALU.max),
                    lambda dve: dve.reciprocal(inv[:, 1, :], inv[:, 0, :]),
                    lambda dve: dve.tensor_copy(cat[:, :, 0:2 * DE], agg[:, :, :]),
                    lambda dve: dve.tensor_tensor(cat[:, :, 2 * DE:3 * DE], agg[:, :, 0:DE],
                                                  bcast_last(inv[:, 1, :], DE), ALU.mult)])
                node_mlp("n1m", [(cat, 3 * DE, w1)], [w2[:, :]], [b1[:, :]], b2[:, :], ACT.Relu, x, x)
                norm("n1n", x, x)

        def store_rows(tag, pairs):
            done = sem(tag + "_done")
            with nc.Block() as block:
                @block.sync
                def _(sp):
                    for t, view in pairs:
                        sp.dma_start(view.rearrange("(b p) f -> p b f", p=P), t).then_inc(done, 16)
                    sp.wait_ge(done, 16 * len(pairs))

        def scatter_rows(tag, rows, k, table):
            done = sem(tag + "_done")
            with nc.Block() as block:
                @block.gpsimd
                def _(pool):
                    for b in range(BLOCKS):
                        pool.indirect_dma_start(table, bass.IndirectOffsetOnAxis(mark_i[k][:, b:b + 1], 0),
                                                rows[:, b, 0:P], None).then_inc(done, 16)
                    pool.wait_ge(done, 16 * BLOCKS)

        def tables2():
            with ExitStack() as ctx:
                h = sb("t2_h", [P, BLOCKS, D], F32, ctx)
                g, b = sb("t2_g", [P, D], F32, ctx), sb("t2_b", [P, D], F32, ctx)
                w = sb("t2_w", [D, 3 * P], F32, ctx)
                bias = sb("t2_bias", [P, 3 * P], F32, ctx)
                qkv = sb("t2_qkv", [P, BLOCKS, 3 * P], F32, ctx)
                pairs = [(g[:, :], a["L2_ln1_g"].partition_broadcast(P)), (b[:, :], a["L2_ln1_b"].partition_broadcast(P))]
                for j, n in enumerate("qkv"):
                    pairs.append((w[:, j * P:(j + 1) * P], a["L2_W" + n]))
                    pairs.append((bias[:, j * P:(j + 1) * P], a["L2_b" + n].partition_broadcast(P)))
                load(pairs, "t2")
                norm("t2n", x, h, g[:, :], b[:, :])
                node_product("t2p", h, D, w[:, :], 3 * P, lambda dve, i, rows: dve.tensor_tensor(
                    qkv[:, bass.ds(i * GB, GB), :], rows, bcast_mid(bias[:, :], GB), ALU.add))
                scatter_rows("t2q", qkv, 1, q_rows)
                store_rows("t2s", [(qkv[:, :, P:3 * P], kv_tab)])

        def nodes2():
            with ExitStack() as ctx:
                agg = sb("n2_agg", [P, BLOCKS, 130], F32, ctx)
                res = sb("n2_res", [P, BLOCKS, D], F32, ctx)
                o = sb("n2_o", [P, BLOCKS, D], F32, ctx)
                wp = sb("n2_wp", [P, D], F32, ctx)
                w1, w2 = sb("n2_w1", [D, D], F32, ctx), sb("n2_w2", [D, D], F32, ctx)
                b1, b1v = column("n2_b1", a["L2_b1"], ctx)
                bp, g, b, b2 = (sb("n2_" + n, [P, D], F32, ctx) for n in ("bp", "g", "b", "b2"))
                inv = sb("n2_inv", [P, BLOCKS, 2], F32, ctx)
                load([(wp[:, :], a["L2_Wp"]), (w1[:, :], a["L2_W1"]), (w2[:, :], a["L2_W2"]), (b1[:, :], b1v),
                      (bp[:, :], a["L2_bp"].partition_broadcast(P)), (g[:, :], a["L2_ln2_g"].partition_broadcast(P)),
                      (b[:, :], a["L2_ln2_b"].partition_broadcast(P)), (b2[:, :], a["L2_b2"].partition_broadcast(P))], "n2")
                collect("n2c", run2, 1, agg)

                def scaled(h):
                    part = agg[:, :, h * D:(h + 1) * D]
                    return lambda dve: dve.tensor_tensor(part, part, bcast_last(inv[:, :, h], D), ALU.mult)
                small("n2s", [
                    lambda dve: dve.tensor_scalar(inv[:, :, :], agg[:, :, P:130], 1e-8, None, ALU.add),
                    lambda dve: dve.reciprocal(inv[:, :, :], inv[:, :, :]),
                    scaled(0), scaled(1)])
                node_product("n2p", agg, P, wp[:, :], D, lambda dve, i, rows: dve.tensor_tensor(
                    res[:, bass.ds(i * GB, GB), :], rows, bcast_mid(bp[:, :], GB), ALU.add))
                small("n2t", [lambda dve: dve.tensor_tensor(res[:, :, :], res[:, :, :], x[:, :, :], ALU.add)])
                norm("n2n", res, o, g[:, :], b[:, :])
                small("n2u", [lambda dve: dve.tensor_tensor(x[:, :, :], res[:, :, :], x[:, :, :], ALU.add)])
                node_mlp("n2m", [(o, D, w1)], [w2[:, :]], [b1[:, :]], b2[:, :], ACT.Gelu, x, x)
                norm("n2o", x, x)

        def tables3():
            with ExitStack() as ctx:
                w = sb("t3_w", [D, 2 * P], F32, ctx)
                ab = sb("t3_ab", [P, BLOCKS, 2 * P], F32, ctx)
                load([(w[:, 0:P], a["L3_eW1"][0:D, :]), (w[:, P:2 * P], a["L3_eW1"][D:2 * D, :])], "t3")
                node_product("t3p", x, D, w[:, :], 2 * P, lambda dve, i, rows: dve.tensor_copy(
                    ab[:, bass.ds(i * GB, GB), :], rows))
                scatter_rows("t3a", ab, 0, a_rows)
                store_rows("t3s", [(ab[:, :, P:2 * P], b_tab)])

        def nodes3():
            with ExitStack() as ctx:
                agg = sb("n3_agg", [P, BLOCKS, P], F32, ctx)
                w1x, w1a = sb("n3_w1x", [D, P], F32, ctx), sb("n3_w1a", [P, P], F32, ctx)
                w2 = sb("n3_w2", [P, D], F32, ctx)
                b1, b1v = column("n3_b1", a["L3_nb1"], ctx)
                b2 = sb("n3_b2", [P, D], F32, ctx)
                load([(w1x[:, :], a["L3_nW1"][0:D, :]), (w1a[:, :], a["L3_nW1"][D:D + P, :]), (w2[:, :], a["L3_nW2"]),
                      (b1[:, :], b1v), (b2[:, :], a["L3_nb2"].partition_broadcast(P))], "n3")
                collect("n3c", run3, 0, agg)
                node_mlp("n3m", [(x, D, w1x), (agg, P, w1a)], [w2[:, :]], [b1[:, :]], b2[:, :], ACT.Silu, x, x)
                norm("n3n", x, x)
                store_rows("n3s", [(x[:, :, :], out)])

        with sort:
            load_keys()
            histograms()
            sort_by_source()
            end_stage()
        edges01()
        end_stage()
        nodes0()
        end_stage()
        nodes1()
        end_stage()
        tables2()
        end_stage()
        edges2()
        end_stage()
        nodes2()
        end_stage()
        tables3()
        end_stage()
        edges3()
        end_stage()
        nodes3()


def kernel(**inputs):
    import numpy as np
    import concourse.bacc as bacc
    from concourse.bass_utils import run_bass_kernel_spmd as run

    v = {k: np.asarray(t) for k, t in inputs.items()}
    pad = EP - EDGES

    def pad_rows(t, rows, fill=0):
        return np.concatenate([t, np.full((rows - t.shape[0],) + t.shape[1:], fill, t.dtype)])

    src, dst = pad_rows(v["src"], EP, NODES), pad_rows(v["dst"], EP, NODES)
    ea16, ea32 = pad_rows(v["edge_attr_16"], EP), pad_rows(v["edge_attr_32"], EP)
    weight = pad_rows(v["edge_weight1"], EP)
    lanes = np.arange(P)
    consts = np.zeros((P, C_COLS), np.float32)
    consts[:, C_EYE:C_EYE + P] = np.eye(P)
    consts[:, C_BEFORE:C_BEFORE + P] = lanes[None, :] < lanes[:, None]
    consts[:, C_UPPER:C_UPPER + P] = lanes[:, None] < lanes[None, :]
    consts[:, C_IOTA:C_IOTA + P] = lanes[None, :]
    consts[:, C_ONES:C_ONES + P] = 1.0
    consts[:, C_SPARE:] = EP + np.arange(BLOCKS)[None, :] * P + lanes[:, None]
    heads = (lanes[:, None] // D == lanes[None, :] // D).astype(np.float32)
    arrays = {
        "consts": consts, "heads": heads,
        "x": pad_rows(v["x"], NP_),
        "src_flat": src, "src_cols": np.ascontiguousarray(src.reshape(TILES, P).T),
        "src_rows": np.ascontiguousarray(src.reshape(CHUNKS, P, TPC).transpose(1, 0, 2).reshape(P, TILES)),
        "dst_cols": np.ascontiguousarray(dst.reshape(TILES, P).T),
        "rec_f": np.concatenate([ea32, weight], axis=1),
        "attr16_t": np.ascontiguousarray(ea16.T), "attr32_t": np.ascontiguousarray(ea32.T),
    }
    for k, t in v.items():
        if "_gnn_" in k:
            arrays[k.replace("_gnn", "")] = t
    arrays = {k: np.ascontiguousarray(t) for k, t in arrays.items()}
    nc = bacc.Bacc("TRN2", target_bir_lowering=False, num_devices=1)
    a = {k: nc.dram_tensor("in_" + k, t.shape, mybir.dt.from_np(t.dtype), kind="ExternalInput").ap()
         for k, t in arrays.items()}
    out = nc.dram_tensor("out", (NP_, D), F32, kind="ExternalOutput").ap()
    program(nc, a, out)
    r = run(nc, [{"in_" + k: t for k, t in arrays.items()}], core_ids=[0])
    return r.results[0]["out"][:NODES]
```

```python
from contextlib import ExitStack

import concourse.bass as bass
from concourse import mybir

P = 128
D = 64
NODES = 3125
BLOCKS = -(-NODES // P)
NP_ = BLOCKS * P
EDGES = 103125
TPC = 4
CH = TPC * P
TILES = 808
EP = TILES * P
CHUNKS = TILES // TPC
DE = 32
RECF = DE + 1
REC = RECF + 1
GB = 5
GROUPS = BLOCKS // GB
BIG = 1.0e38
STREAMS_D, STREAMS_S = 2, 4
UNITS = CHUNKS // 2
RING = 4
LN_EPS = 1e-5
CAP = 20.0

ALU = mybir.AluOpType
ACT = mybir.ActivationFunctionType
F32 = mybir.dt.float32
BF16 = mybir.dt.bfloat16
I32 = mybir.dt.int32
AX = mybir.AxisListType.X

C_EYE, C_BEFORE, C_UPPER, C_IOTA, C_ONES, C_SPARE = 0, P, 2 * P, 3 * P, 4 * P, 5 * P
C_COLS = 5 * P + BLOCKS


class Step:

    def __init__(self, i, k, ring):
        self.n = i * ring + k if not isinstance(i, int) else k
        self.s = k % ring
        self.p = k % 2
        self.first = isinstance(i, int) and k == 0
        self.last = (k - 1) % ring
        self.uses = i + k // ring
        self.uses2 = i * (ring // 2) + k // 2

    def landed(self, per_step):
        return (self.uses + 1) * (16 * per_step)

    def landed_before(self, per_step):
        return self.uses * (16 * per_step)


def wait(eng, sem, value):
    if isinstance(value, int) and value <= 0:
        return
    eng.wait_ge(sem, value)


def pipeline(eng, parts, steps=CHUNKS, ring=RING):
    lag = max(d for _, d in parts)
    head = min(ring + lag + (steps - ring - lag) % ring, steps)

    def turn(i, k):
        for part, d in parts:
            if isinstance(i, int) and not 0 <= k - d < steps:
                continue
            part(Step(i, k - d, ring))
    for k in range(head):
        turn(0, k)
    if head < steps:
        with eng.Fori(0, (steps - head) // ring, 1) as i:
            for k in range(head, head + ring):
                turn(i, k)
    for k in range(steps, steps + lag):
        turn(0, k)


def uses_of(slot, steps, ring):
    return (steps - slot - 1) // ring + 1


def program(nc, a, out):
    top = ExitStack()

    def dram(name, shape, dt=F32):
        return nc.dram_tensor(name, shape, dt).ap()

    rec_s = dram("rec_s", (EP, REC))
    keep_f = dram("keep_f", (EP + NP_, 1))
    keep = {k: dram("keep_" + k, (EP,), BF16) for k in "sd"}
    run0 = dram("run0", (EP, D))
    run1 = dram("run1", (EP, 2 * DE))
    run2 = dram("run2", (EP, 130))
    run3 = dram("run3", (EP, P))
    q_rows = dram("q_rows", (EP + NP_, P))
    a_rows = dram("a_rows", (EP + NP_, P))
    kv_tab = dram("kv_tab", (NP_, 2 * P))
    b_tab = dram("b_tab", (NP_, P))

    with top:
        def sb(name, shape, dt=F32, ctx=top):
            return ctx.enter_context(nc.sbuf_tensor(name, shape, dt))

        taken_sems = []

        def sem(name):
            taken_sems.append(nc.alloc_semaphore(name=name))
            return taken_sems[-1]

        gate = top.enter_context(nc.semaphore("gate"))

        def hold(eng):
            eng.sem_inc(gate, 1)

        def end_stage():
            nc.all_engine_barrier()
            nc.clear_and_free_semaphores(taken_sems)
            taken_sems.clear()
            nc.all_engine_barrier()

        consts = sb("consts", [P, C_COLS])
        eye = consts[:, C_EYE:C_EYE + P]
        before = consts[:, C_BEFORE:C_BEFORE + P]
        upper = consts[:, C_UPPER:C_UPPER + P]
        iota = consts[:, C_IOTA:C_IOTA + P]
        ones = consts[:, C_ONES:C_ONES + P]
        spare = consts[:, C_SPARE:C_SPARE + BLOCKS]
        eye_b = sb("eye_b", [P, P], BF16)
        src_i = sb("src_i", [P, TILES], I32)
        ids_s = sb("ids_s", [P, TILES], I32)
        weight_s = sb("weight_s", [P, TILES])
        x = sb("x", [P, BLOCKS, D])
        end_i = [sb(f"end_i{k}", [P, BLOCKS], I32) for k in "sd"]
        has = [sb(f"has{k}", [P, BLOCKS]) for k in "sd"]
        count = [sb(f"count{k}", [P, BLOCKS]) for k in "sd"]
        start = [sb(f"start{k}", [P, BLOCKS]) for k in "sd"]
        mark_i = [sb(f"mark_i{k}", [P, BLOCKS], I32) for k in "sd"]
        spans = [sb("span_s", [P, STREAMS_S - 1, BLOCKS]), sb("span_d", [P, STREAMS_D - 1, BLOCKS])]
        eps_col = sb("eps_col", [P, 1])

        def bank(name, ctx, parts, *shape, dt=F32):
            t = ctx.enter_context(nc.psum_tensor(name, [P, 512 * 4 // (2 if dt == BF16 else 4)], dt))
            n = 1
            for d in shape:
                n *= d
            v = t[0:parts, 0:n]
            return v.rearrange("p (a b) -> p a b", a=shape[0]) if len(shape) == 2 else v

        def tile_cols(ap, t, per):
            return ap.rearrange("f (p t) -> f t p", t=per)[:, t, :]

        def bcast_mid(ap, n):
            return ap.unsqueeze(1).to_broadcast([ap.shape[0], n, ap.shape[-1]])

        def bcast_last(ap, n):
            return ap.unsqueeze(2).to_broadcast([ap.shape[0], ap.shape[1], n])

        early_ctx = ExitStack()
        early_x = sb("early_x", [P, UNITS, D], F32, early_ctx)
        sort = ExitStack()
        keys_i = sb("keys_i", [P, 2, TILES], I32, sort)
        half_i = sb("half_i", [P, 2, 2, TILES], I32, sort)
        key = sb("key", [P, TILES], F32, sort)
        lane = [sb(f"lane{k}", [P, TILES], BF16, sort) for k in "sd"]
        blk = [sb(f"blk{k}", [P, TILES], BF16, sort) for k in "sd"]
        iota_b = sb("iota_b", [P, P], BF16, sort)
        minus_lane = sb("minus_lane", [P, TILES], F32, sort)
        zero_b = sb("zero_b", [P, P], BF16, sort)
        near = sb("near", [P, 2, TILES], I32, sort)
        keep_d = sb("keep_d_sb", [P, TILES], BF16, sort)
        bits = sb("bits", [P, TILES], F32, sort)
        bits_b = sb("bits_b", [P, TILES], BF16, sort)
        keep1_f = sb("keep1_f", [P, TILES + BLOCKS], F32, sort)
        zero_f = sb("zero_f", [P, 1], F32, sort)
        dst_sums = sort.enter_context(nc.psum_tensor("dst_sums", [P, 512], F32))[:, 0:BLOCKS]

        def load_keys():
            loaded, split, made = sem("k_loaded"), sem("k_split"), sem("k_made")
            with nc.Block() as block:
                @block.sync
                def _(sp):
                    sp.dma_start(consts[:, :], a["consts"]).then_inc(loaded, 16)
                    sp.dma_start(keys_i[:, 0, :], a["src_cols"]).then_inc(loaded, 16)
                    sp.dma_start(keys_i[:, 1, :], a["dst_cols"]).then_inc(loaded, 16)
                    sp.dma_start(src_i[:, :], a["src_rows"]).then_inc(loaded, 16)
                    for k in range(2):
                        sp.dma_start(near[:, k, :], a["dst_after"][1 - k:EP + 1 - k].rearrange("(p f) -> p f", p=P)).then_inc(loaded, 16)
                    sp.dma_start(x[:, :, :], a["x"].rearrange("(b p) f -> p b f", p=P)).then_inc(loaded, 16)

                @block.vector
                def _(dve):
                    dve.memset(eps_col[:, :], LN_EPS)
                    dve.wait_ge(loaded, 112)
                    for k in range(2):
                        dve.tensor_scalar(half_i[:, k, 0, :], keys_i[:, k, :], P - 1, None,
                                          ALU.bitwise_and).then_inc(split, 1)
                        dve.tensor_scalar(half_i[:, k, 1, :], keys_i[:, k, :], 7, None,
                                          ALU.logical_shift_right).then_inc(split, 1)
                    dve.tensor_copy(eye_b[:, :], eye)
                    dve.tensor_copy(iota_b[:, :], iota)
                    dve.tensor_copy(key[:, :], keys_i[:, 0, :])
                    dve.wait_ge(split, 4)
                    for k in range(2):
                        dve.tensor_copy(lane[k][:, :], half_i[:, k, 0, :])
                        last = dve.tensor_copy(blk[k][:, :], half_i[:, k, 1, :])
                    dve.tensor_scalar(minus_lane[:, :], half_i[:, 0, 0, :], -1.0, None, ALU.mult)
                    last = dve.tensor_tensor(keep_d[:, :], near[:, 0, :], near[:, 1, :], ALU.is_equal)
                    last.then_inc(made, 1)
                    dve.wait_ge(made, 1)

        def source_histogram(sums):
            with ExitStack() as ctx:
                deep = 2 * RING
                idx = sb("h_idx", [P, RING, 1], I32, ctx)
                early = sb("h_early", [P, RING, D], F32, ctx)
                far = sb("h_far", [P, deep, P], BF16, ctx)
                idx_made, moved, fars, lasts = sem("h_idxs"), sem("h_moved"), sem("h_fars"), sem("h_lasts")
                got = [sem(f"h_got{s}") for s in range(RING)]
                hot_lane = sb("h_lane", [P, deep, TPC, P], BF16, ctx)
                hot_blk = sb("h_blk", [P, deep, TPC, BLOCKS], BF16, ctx)
                zeroed, lanes, blks, added, final = (sem("h_" + n) for n in ("zeroed", "lanes", "blks", "added", "final"))
                with nc.Block() as block:
                    @block.vector
                    def _(dve):
                        dve.memset(zero_b[:, :], 0.0).then_inc(zeroed, 1)

                        def index(un):
                            wait(dve, got[un.s], un.landed_before(1))
                            dve.tensor_copy(idx[:, un.s], src_i[:, bass.ds(un.n * TPC, 1)]).then_inc(idx_made, 1)

                        def hots(un):
                            wait(dve, added, un.n * 2 + (2 - deep))
                            for j in range(2):
                                at = (un.n * 2 + j) * TPC
                                dve.tensor_tensor(hot_lane[:, un.s * 2 + j, 0:TPC - 1], bcast_mid(iota_b[:, :], TPC - 1),
                                                  bcast_last(lane[0][:, bass.ds(at, TPC - 1)], P),
                                                  ALU.is_equal).then_inc(lanes, 1)
                                dve.tensor_tensor(hot_blk[:, un.s * 2 + j], bcast_mid(iota_b[:, 0:BLOCKS], TPC),
                                                  bcast_last(blk[0][:, bass.ds(at, TPC)], BLOCKS),
                                                  ALU.is_equal).then_inc(blks, 1)
                        pipeline(dve, [(index, 0), (hots, 1)], UNITS, RING)

                    @block.gpsimd
                    def _(pool):
                        def gather(un):
                            wait(pool, idx_made, un.n + 1)
                            wait(pool, moved, un.n + 1 - RING)
                            hold(pool)
                            pool.indirect_dma_start(early[:, un.s, :], None, a["x"],
                                                    bass.IndirectOffsetOnAxis(idx[:, un.s, 0:1], 0)).then_inc(got[un.s], 16)
                        pipeline(pool, [(gather, 0)], UNITS, RING)

                    @block.scalar
                    def _(act):
                        def distances(un):
                            wait(act, lasts, (un.n + 1 - RING) * 2)
                            for j in range(2):
                                act.activation(far[:, un.s * 2 + j, :], iota_b[:, :], ACT.Abs,
                                               bias=minus_lane[:, bass.ds((un.n * 2 + j) * TPC + (TPC - 1), 1)]).then_inc(fars, 1)

                        def last_hots(un):
                            wait(act, fars, un.n * 2 + 2)
                            wait(act, added, un.n * 2 + (2 - deep))
                            for j in range(2):
                                act.activation(hot_lane[:, un.s * 2 + j, TPC - 1], far[:, un.s * 2 + j, :], ACT.Relu,
                                               bias=ones[:, 0:1], scale=-1.0).then_inc(lasts, 1)

                        def move(un):
                            wait(act, got[un.s], un.landed(1))
                            act.copy(early_x[:, bass.ds(un.n, 1), :], early[:, un.s:un.s + 1, :]).then_inc(moved, 1)
                        pipeline(act, [(distances, 0), (last_hots, 1), (move, 2)], UNITS, RING)
                        act.wait_ge(moved, UNITS)

                    @block.tensor
                    def _(pe):
                        pe.wait_ge(zeroed, 1)
                        pe.matmul(sums, zero_b[:, :], zero_b[:, 0:BLOCKS], start=True, stop=False)

                        def add(ch):
                            wait(pe, lanes, ch.n + 1)
                            wait(pe, blks, ch.n + 1)
                            wait(pe, lasts, ch.n + 1)
                            for t in range(TPC):
                                mm = pe.matmul(sums, hot_lane[:, ch.s, t], hot_blk[:, ch.s, t], start=False, stop=False)
                            mm.then_inc(added, 1)
                        pipeline(pe, [(add, 0)], ring=deep)
                        pe.matmul(sums, zero_b[:, :], zero_b[:, 0:BLOCKS], start=False, stop=True).then_inc(final, 1)
                        pe.wait_ge(final, 1)

        def starts(k, sums):
            tag = "p" + "sd"[k]
            with ExitStack() as ctx:
                tot = ctx.enter_context(nc.psum_tensor(tag + "_tot", [P, 2, 64], F32))
                w = sb(tag + "_w", [P, 5, BLOCKS], F32, ctx)
                copied, prefixed, chain = sem(tag + "_copied"), sem(tag + "_prefixed"), sem(tag + "_chain")
                with nc.Block() as block:
                    @block.vector
                    def _(dve):
                        links = [0]

                        def link(ins):
                            links[0] += 1
                            ins.then_inc(chain, 1)
                            dve.wait_ge(chain, links[0])

                        dve.tensor_copy(count[k][:, :], sums).then_inc(copied, 1)
                        dve.wait_ge(copied, 1)
                        dve.wait_ge(prefixed, 1)
                        below, total = tot[:, 0, 0:BLOCKS], tot[:, 1, 0:BLOCKS]
                        incl, excl, t0, t1, t2 = (w[:, j, :] for j in range(5))
                        link(dve.tensor_copy(t0, total))
                        link(dve.tensor_tensor_scan(incl, t0, ones[:, 0:BLOCKS], 0.0, ALU.add, ALU.mult))
                        link(dve.tensor_tensor(excl, incl, t0, ALU.subtract))
                        link(dve.tensor_tensor(start[k][:, :], excl, below, ALU.add))
                        link(dve.tensor_scalar(has[k][:, :], count[k][:, :], 0.0, None, ALU.is_gt))
                        link(dve.scalar_tensor_tensor(t1, start[k][:, :], -1.0, count[k][:, :], ALU.add, ALU.add))
                        link(dve.tensor_tensor(end_i[k][:, :], t1, has[k][:, :], ALU.mult))
                        link(dve.tensor_tensor(t1, start[k][:, :], spare, ALU.subtract))
                        link(dve.tensor_tensor(t2, t1, has[k][:, :], ALU.mult))
                        link(dve.tensor_tensor(mark_i[k][:, :], t2, spare, ALU.add))
                        link(dve.tensor_tensor(t1, start[k][:, :], count[k][:, :], ALU.add))
                        streams = spans[k].shape[1] + 1
                        for j in range(1, streams):
                            border = float(j * EP // streams)
                            link(dve.tensor_scalar(t0, t1, border, None, ALU.is_gt))
                            link(dve.scalar_tensor_tensor(spans[k][:, j - 1, :], start[k][:, :], border, t0,
                                                          ALU.is_lt, ALU.mult))

                    @block.tensor
                    def _(pe):
                        pe.wait_ge(copied, 1)
                        pe.matmul(tot[:, 0, 0:BLOCKS], upper, count[k][:, :], start=True, stop=True)
                        pe.matmul(tot[:, 1, 0:BLOCKS], ones, count[k][:, :], start=True, stop=True).then_inc(prefixed, 1)

        def sort_by_source():
            with ExitStack() as ctx:
                hot_lane = sb("r_lane", [P, RING, TPC, P], BF16, ctx)
                hot_blk = sb("r_blk", [P, RING, TPC, BLOCKS], BF16, ctx)
                hot_t = sb("r_hot_t", [P, RING, TPC * P], F32, ctx)
                dlane = sb("r_dlane", [P, RING, TPC, P], BF16, ctx)
                dblk = sb("r_dblk", [P, RING, TPC, BLOCKS], BF16, ctx)
                row = sb("r_row", [P, RING, CH], I32, ctx)
                junk = sb("r_junk", [P, RING, TPC, P], BF16, ctx)
                seen = sb("r_seen", [P, RING, TPC, BLOCKS], F32, ctx)
                picked = sb("r_picked", [P, RING, TPC, BLOCKS], F32, ctx)
                place = sb("r_place", [P, RING, TPC], F32, ctx)
                inside = sb("r_inside", [P, RING, TPC], F32, ctx)
                place_i = sb("r_place_i", [P, RING, TPC], I32, ctx)
                rec = sb("r_rec", [P, RING, TPC, REC], F32, ctx)
                flip = [bank(f"r_flip{s}", ctx, P, TPC * P, dt=BF16) for s in range(2)]
                hist = [bank(f"r_hist{s}", ctx, P, TPC, BLOCKS) for s in range(2)]
                got = [bank(f"r_got{s}", ctx, P, TPC, BLOCKS) for s in range(2)]
                hot_made, eq_made, flipped, flip_copied = sem("r_hot"), sem("r_eq"), sem("r_flip"), sem("r_flipc")
                hist_made, seen_made, got_made, pick_made = sem("r_hist"), sem("r_seen"), sem("r_got"), sem("r_pick")
                place_made, place_cast, seeded = sem("r_place"), sem("r_cast"), sem("r_seeded")
                keep1_made, id_made = sem("r_keep1"), sem("r_id")
                dhot_made, dadded, final = sem("r_dhot"), sem("r_dadded"), sem("r_final")
                inited, marked, read, narrowed, written = (sem("r_" + n) for n in ("inited", "marked", "read", "narrow", "written"))
                row_in = [sem(f"r_row{s}") for s in range(RING)]
                rec_in = [sem(f"r_rec{s}") for s in range(RING)]
                sent = [sem(f"r_sent{s}") for s in range(RING)]
                with nc.Block() as block:
                    @block.sync
                    def _(sp):
                        sp.wait_ge(keep1_made, 1)
                        sp.dma_start(keep_f.rearrange("(p f) o -> p (f o)", p=P), keep1_f[:, :]).then_inc(inited, 16)
                        sp.dma_start(keep["d"].rearrange("(p f) -> p f", p=P), keep_d[:, :]).then_inc(written, 16)

                        def fetch(ch):
                            rows = bass.ds(ch.n * CH, CH)
                            wait(sp, eq_made, (ch.n + 1 - RING) * TPC)
                            hold(sp)
                            sp.dma_start(row[:, ch.s], a["src_flat"][rows].partition_broadcast(P)
                                         ).then_inc(row_in[ch.s], 16)
                            wait(sp, sent[ch.s], ch.landed_before(TPC))
                            hold(sp)
                            sp.dma_start(rec[:, ch.s, :, 0:RECF],
                                         a["rec_f"][rows, :].rearrange("(t p) f -> p t f", p=P)).then_inc(rec_in[ch.s], 16)
                        pipeline(sp, [(fetch, 0)])
                        sp.wait_ge(marked, 16 * BLOCKS)
                        sp.dma_start(bits[:, :], keep_f[0:EP, :].rearrange("(p f) o -> p (f o)", p=P)).then_inc(read, 16)
                        sp.wait_ge(narrowed, 1)
                        sp.dma_start(keep["s"].rearrange("(p f) -> p f", p=P), bits_b[:, :]).then_inc(written, 16)
                        sp.wait_ge(written, 32)

                    @block.vector
                    def _(dve):
                        dve.memset(zero_f[:, :], 0.0)
                        dve.memset(keep1_f[:, :], 1.0).then_inc(keep1_made, 1)
                        dve.tensor_copy(seen[:, RING - 1, TPC - 1], start[0][:, :]).then_inc(seeded, 1)
                        dve.wait_ge(seeded, 1)

                        def hots(ch):
                            cols = bass.ds(ch.n * TPC, TPC)
                            wait(dve, hist_made, ch.n + 1 - RING)
                            wait(dve, place_cast, ch.n + 1 - RING)
                            dve.tensor_tensor(hot_lane[:, ch.s], bcast_mid(iota_b[:, :], TPC),
                                              bcast_last(lane[0][:, cols], P), ALU.is_equal).then_inc(hot_made, 1)
                            dve.tensor_tensor(hot_blk[:, ch.s], bcast_mid(iota_b[:, 0:BLOCKS], TPC),
                                              bcast_last(blk[0][:, cols], BLOCKS), ALU.is_equal).then_inc(hot_made, 1)
                            wait(dve, row_in[ch.s], ch.landed(1))
                            for t in range(TPC):
                                dve.scalar_tensor_tensor(junk[:, ch.s, t], row[:, ch.s, t * P:(t + 1) * P],
                                                         key[:, bass.ds(ch.n * TPC + t, 1)], before,
                                                         ALU.is_equal, ALU.mult,
                                                         accum_out=inside[:, ch.s, t:t + 1]).then_inc(eq_made, 1)

                        def dst_hots(ch):
                            cols = bass.ds(ch.n * TPC, TPC)
                            wait(dve, dadded, ch.n + 1 - RING)
                            dve.tensor_tensor(dlane[:, ch.s], bcast_mid(iota_b[:, :], TPC),
                                              bcast_last(lane[1][:, cols], P), ALU.is_equal).then_inc(dhot_made, 1)
                            dve.tensor_tensor(dblk[:, ch.s], bcast_mid(iota_b[:, 0:BLOCKS], TPC),
                                              bcast_last(blk[1][:, cols], BLOCKS), ALU.is_equal).then_inc(dhot_made, 1)

                        def follow(ch):
                            wait(dve, hist_made, ch.n + 1)
                            wait(dve, seen_made, ch.n)
                            wait(dve, got_made, ch.n + 2 - RING)
                            dve.tensor_tensor(seen[:, ch.s], hist[ch.p],
                                              bcast_mid(seen[:, ch.last, TPC - 1], TPC), ALU.add).then_inc(seen_made, 1)

                        def places(ch):
                            wait(dve, got_made, ch.n + 1)
                            wait(dve, hot_made, (ch.n + 1) * 2)
                            dve.tensor_tensor(picked[:, ch.s], got[ch.p], hot_blk[:, ch.s], ALU.mult).then_inc(pick_made, 1)
                            wait(dve, pick_made, ch.n + 1)
                            dve.tensor_reduce(place[:, ch.s], picked[:, ch.s], AX, ALU.add).then_inc(place_made, 1)
                            wait(dve, place_made, ch.n + 1)
                            wait(dve, eq_made, (ch.n + 1) * TPC)
                            wait(dve, sent[ch.s], ch.landed_before(TPC))
                            dve.tensor_tensor(place_i[:, ch.s], place[:, ch.s], inside[:, ch.s],
                                              ALU.add).then_inc(place_cast, 1)
                        pipeline(dve, [(hots, 0), (follow, 1), (places, 2), (dst_hots, 1)])
                        dve.wait_ge(read, 16)
                        dve.tensor_copy(bits_b[:, :], bits[:, :]).then_inc(narrowed, 1)

                    @block.tensor
                    def _(pe):
                        pe.wait_ge(seeded, 1)

                        def products(ch):
                            wait(pe, hot_made, (ch.n + 1) * 2)
                            wait(pe, flip_copied, ch.n - 1)
                            for t in range(TPC):
                                mm = pe.transpose(flip[ch.p][:, t * P:(t + 1) * P], hot_lane[:, ch.s, t], eye_b[:, :])
                            mm.then_inc(flipped, 1)
                            wait(pe, seen_made, ch.n - 1)
                            for t in range(TPC):
                                for j in range(t + 1):
                                    mm = pe.matmul(hist[ch.p][:, t, :], hot_lane[:, ch.s, j], hot_blk[:, ch.s, j],
                                                   start=(j == 0), stop=(j == t))
                            mm.then_inc(hist_made, 1)

                        def fetch(ch):
                            wait(pe, flip_copied, ch.n + 1)
                            wait(pe, seen_made, ch.n + 1)
                            wait(pe, pick_made, ch.n - 1)
                            for t in range(TPC):
                                now = seen[:, ch.s, t - 1] if t else seen[:, ch.last, TPC - 1]
                                mm = pe.matmul(got[ch.p][:, t, :], hot_t[:, ch.s, t * P:(t + 1) * P], now,
                                               start=True, stop=True)
                            mm.then_inc(got_made, 1)

                        def count_dst(ch):
                            wait(pe, dhot_made, (ch.n + 1) * 2)
                            for t in range(TPC):
                                mm = pe.matmul(dst_sums, dlane[:, ch.s, t], dblk[:, ch.s, t], start=False, stop=False)
                            mm.then_inc(dadded, 1)
                        pe.matmul(dst_sums, zero_b[:, :], zero_b[:, 0:BLOCKS], start=True, stop=False)
                        pipeline(pe, [(products, 0), (fetch, 1), (count_dst, 2)])
                        pe.matmul(dst_sums, zero_b[:, :], zero_b[:, 0:BLOCKS], start=False, stop=True).then_inc(final, 1)
                        pe.wait_ge(final, 1)

                    @block.scalar
                    def _(act):
                        def copy(ch):
                            wait(act, flipped, ch.n + 1)
                            wait(act, got_made, ch.n + 1 - RING)
                            act.copy(hot_t[:, ch.s], flip[ch.p]).then_inc(flip_copied, 1)
                            wait(act, sent[ch.s], ch.landed_before(TPC))
                            act.copy(rec[:, ch.s, :, RECF].bitcast(I32),
                                     keys_i[:, 1, bass.ds(ch.n * TPC, TPC)]).then_inc(id_made, 1)
                        pipeline(act, [(copy, 0)])

                    @block.gpsimd
                    def _(pool):
                        pool.wait_ge(inited, 16)
                        for b in range(BLOCKS):
                            pool.indirect_dma_start(keep_f, bass.IndirectOffsetOnAxis(mark_i[0][:, b:b + 1], 0),
                                                    zero_f[:, :], None).then_inc(marked, 16)

                        def send(ch):
                            wait(pool, place_cast, ch.n + 1)
                            wait(pool, rec_in[ch.s], ch.landed(1))
                            wait(pool, id_made, ch.n + 1)
                            hold(pool)
                            for t in range(TPC):
                                pool.indirect_dma_start(rec_s, bass.IndirectOffsetOnAxis(place_i[:, ch.s, t:t + 1], 0),
                                                        rec[:, ch.s, t, :], None).then_inc(sent[ch.s], 16)
                        pipeline(pool, [(send, 0)])
                        for s in range(RING):
                            pool.wait_ge(sent[s], uses_of(s, CHUNKS, RING) * 16 * TPC)

        def column(name, ap, ctx):
            t = sb(name, [ap.shape[0], 1], F32, ctx)
            return t, ap.rearrange("(p o) -> p o", o=1)

        def load(pairs, tag):
            done = sem(tag + "_loaded")
            with nc.Block() as block:
                @block.sync
                def _(sp):
                    for t, view in pairs[0::2]:
                        sp.dma_start(t, view).then_inc(done, 16)
                    sp.wait_ge(done, 16 * len(pairs))

                @block.scalar
                def _(act):
                    for t, view in pairs[1::2]:
                        act.dma_start(t, view).then_inc(done, 16)

        def take_ends(pool, table, k, agg, landed):
            for b in range(BLOCKS):
                pool.indirect_dma_start(agg[:, b, :], None, table,
                                        bass.IndirectOffsetOnAxis(end_i[k][:, b:b + 1], 0)).then_inc(landed[b // GB], 16)
            for s in landed:
                pool.wait_ge(s, 16 * GB)

        def no_edges(agg, k, rows=slice(0, BLOCKS)):
            return lambda dve: dve.tensor_tensor(agg[:, rows, :], agg[:, rows, :],
                                                 bcast_last(has[k][:, rows], agg.shape[2]), ALU.mult)

        class Arrival:

            def __init__(self, tag, table, k, agg, steps):
                self.table, self.k, self.agg, self.steps = table, k, agg, steps
                self.landed = [sem(f"{tag}_landed{g}") for g in range(GROUPS)]
                self.chain, self.ready = sem(tag + "_chain"), sem(tag + "_ready")

            def bring(self, pool):
                take_ends(pool, self.table, self.k, self.agg, self.landed)

            def prepare(self, dve):
                n = 0
                for g in range(GROUPS):
                    dve.wait_ge(self.landed[g], 16 * GB)
                    rows = slice(g * GB, (g + 1) * GB)
                    for make in [no_edges(self.agg, self.k, rows)] + self.steps(rows):
                        make(dve).then_inc(self.chain, 1)
                        n += 1
                        dve.wait_ge(self.chain, n)
                    dve.sem_inc(self.ready, 1)

        def stream_ends(name, table, k, ctx):
            streams = spans[k].shape[1] + 1
            ends = sb(name, [P, streams - 1, table.shape[1]], F32, ctx)
            return ends, [(ends[:, j, :], table[(j + 1) * (EP // streams) - 1:(j + 1) * (EP // streams), :]
                           .rearrange("a f -> (a f)").partition_broadcast(P)) for j in range(streams - 1)]

        def norm(tag, src, dst, gain=None, shift=None):
            with ExitStack() as ctx:
                stat = sb(tag + "_stat", [P, 4, BLOCKS], F32, ctx)
                cent = sb(tag + "_cent", [P, BLOCKS, D], F32, ctx)
                sq = sb(tag + "_sq", [P, BLOCKS, D], F32, ctx)
                chain, var_made, rooted = sem(tag + "_chain"), sem(tag + "_var"), sem(tag + "_root")
                with nc.Block() as block:
                    @block.vector
                    def _(dve):
                        links = [0]

                        def link(ins):
                            links[0] += 1
                            ins.then_inc(chain, 1)
                            dve.wait_ge(chain, links[0])

                        link(dve.tensor_reduce(stat[:, 0, :], src[:, :, :], AX, ALU.add))
                        link(dve.tensor_scalar(stat[:, 1, :], stat[:, 0, :], 1.0 / D, None, ALU.mult))
                        link(dve.tensor_tensor(cent[:, :, :], src[:, :, :], bcast_last(stat[:, 1, :], D), ALU.subtract))
                        link(dve.tensor_tensor(sq[:, :, :], cent[:, :, :], cent[:, :, :], ALU.mult))
                        dve.tensor_reduce(stat[:, 2, :], sq[:, :, :], AX, ALU.add).then_inc(var_made, 1)
                        dve.wait_ge(rooted, 1)
                        link(dve.reciprocal(stat[:, 0, :], stat[:, 3, :]))
                        link(dve.tensor_tensor(dst[:, :, :], cent[:, :, :], bcast_last(stat[:, 0, :], D), ALU.mult))
                        if gain is not None:
                            link(dve.tensor_tensor(dst[:, :, :], dst[:, :, :], bcast_mid(gain, BLOCKS), ALU.mult))
                            link(dve.tensor_tensor(dst[:, :, :], dst[:, :, :], bcast_mid(shift, BLOCKS), ALU.add))

                    @block.scalar
                    def _(act):
                        act.wait_ge(var_made, 1)
                        act.activation(stat[:, 3, :], stat[:, 2, :], ACT.Sqrt, bias=eps_col[:, :],
                                       scale=1.0 / D).then_inc(rooted, 1)

        def node_product(tag, src, width, w2, cols, emit, arrival=None,
                         rows=None, k=None, sparse=None, dense=None):
            with ExitStack() as ctx:
                part = sb(tag + "_part", [P, 2, GB, width], F32, ctx)
                flat = sb(tag + "_flat", [width, 2, GB * P], F32, ctx)
                flip = ctx.enter_context(nc.psum_tensor(tag + "_flip", [width, 2 * 512], F32))
                prod = ctx.enter_context(nc.psum_tensor(tag + "_prod", [P, GB, 512 if cols > 64 else 64], F32))
                taken, flipped, copied, made, used = (sem(f"{tag}_{n}") for n in ("taken", "flipped", "copied", "made", "used"))
                with nc.Block() as block:
                    @block.scalar
                    def _(act):
                        def take(gr):
                            if arrival is not None:
                                wait(act, arrival.ready, gr.n + 1)
                            wait(act, flipped, gr.n - 1)
                            act.copy(part[:, gr.s], src[:, bass.ds(gr.n * GB, GB), 0:width]).then_inc(taken, 1)

                        def flatten(gr):
                            wait(act, flipped, gr.n + 1)
                            wait(act, made, gr.n - 1)
                            act.copy(flat[:, gr.s], flip[:, 0:GB * P]).then_inc(copied, 1)
                        pipeline(act, [(take, 0), (flatten, 0)], GROUPS, 2)

                    @block.tensor
                    def _(pe):
                        def turn(gr):
                            wait(pe, copied, gr.n)
                            wait(pe, taken, gr.n + 1)
                            hold(pe)
                            for b in range(GB):
                                mm = pe.transpose(flip[:, b * P:(b + 1) * P], part[:, gr.s, b, :], eye)
                            mm.then_inc(flipped, 1)

                        def multiply(gr):
                            wait(pe, used, gr.n)
                            wait(pe, copied, gr.n + 1)
                            hold(pe)
                            for b in range(GB):
                                mm = pe.matmul(prod[:, b, 0:cols], flat[:, gr.s, b * P:(b + 1) * P], w2, start=True, stop=True)
                            mm.then_inc(made, 1)
                        pipeline(pe, [(turn, 0), (multiply, 1)], GROUPS, 2)

                    @block.vector
                    def _(dve):
                        if arrival is not None:
                            arrival.prepare(dve)

                        def take_out(gr):
                            wait(dve, made, gr.n + 1)
                            emit(dve, gr.n, prod[:, :, 0:cols]).then_inc(used, 1)
                        pipeline(dve, [(take_out, 0)], GROUPS, 2)
                        dve.wait_ge(used, GROUPS)

                    if arrival is not None:
                        @block.gpsimd
                        def _(pool):
                            arrival.bring(pool)

                    if rows is not None:
                        scattered, stored = sem(tag + "_scattered"), sem(tag + "_stored")

                        @block.gpsimd
                        def _(pool):
                            for b in range(BLOCKS):
                                if b % GB == 0:
                                    pool.wait_ge(used, b // GB + 1)
                                pool.indirect_dma_start(sparse, bass.IndirectOffsetOnAxis(mark_i[k][:, b:b + 1], 0),
                                                        rows[:, b, 0:P], None).then_inc(scattered, 16)
                            pool.wait_ge(scattered, 16 * BLOCKS)

                        @block.sync
                        def _(sp):
                            blocks = dense.rearrange("(b p) f -> p b f", p=P)
                            for g in range(GROUPS):
                                sp.wait_ge(used, g + 1)
                                sp.dma_start(blocks[:, g * GB:(g + 1) * GB, :], rows[:, g * GB:(g + 1) * GB, P:]).then_inc(stored, 16)
                            sp.wait_ge(stored, 16 * GROUPS)

        def node_mlp(tag, parts, w2, bias1, bias2, func, dst, add, arrival=None, beside=None):
            halves = len(w2)
            hid_w = w2[0].shape[0]
            N = len(parts)
            with ExitStack() as ctx:
                part = [sb(f"{tag}_part{i}", [P, 2, GB, w], F32, ctx) for i, (_, w, _) in enumerate(parts)]
                flat = [sb(f"{tag}_flat{i}", [w, 2, GB * P], F32, ctx) for i, (_, w, _) in enumerate(parts)]
                flip = [ctx.enter_context(nc.psum_tensor(f"{tag}_flip{i}", [w, 2 * 512], F32)) for i, (_, w, _) in enumerate(parts)]
                hid_ps = [ctx.enter_context(nc.psum_tensor(f"{tag}_hid{h}", [hid_w, 2 * 512], F32)) for h in range(halves)]
                prod = bank(f"{tag}_prod", ctx, P, GB, D)
                hid = sb(f"{tag}_hid_s", [hid_w, 2, halves, GB * P], F32, ctx)
                if func == "mish":
                    y, u, q, r = (sb(f"{tag}_{n}", [hid_w, 2, halves, GB * P], F32, ctx) for n in "yuqr")
                names = ("taken", "flipped", "copied", "hidden", "read", "acted", "made", "used", "capped", "exped",
                         "squared", "lifted", "inverted", "scaled")
                (taken, flipped, copied, hidden, read, acted, made, used, capped, exped,
                 squared, lifted, inverted, scaled) = (sem(f"{tag}_{n}") for n in names)
                with nc.Block() as block:
                    @block.gpsimd
                    def _(pool):
                        if arrival is not None:
                            arrival.bring(pool)
                        if beside is not None:
                            beside(pool)

                    @block.scalar
                    def _(act):
                        def take(gr):
                            if arrival is not None:
                                wait(act, arrival.ready, gr.n + 1)
                            wait(act, flipped, gr.n - 1)
                            for i, (src, w, _) in enumerate(parts):
                                act.copy(part[i][:, gr.s], src[:, bass.ds(gr.n * GB, GB), 0:w]).then_inc(taken, 1)

                        def flatten(gr):
                            wait(act, flipped, gr.n + 1)
                            wait(act, hidden, (gr.n - 1) * halves)
                            for i, (_, w, _) in enumerate(parts):
                                act.copy(flat[i][:, gr.s], flip[i][0:w, 0:GB * P]).then_inc(copied, 1)

                        def activate(gr):
                            wait(act, made, gr.n - 1)
                            for h in range(halves):
                                wait(act, hidden, gr.n * halves + (h + 1))
                                if func == "mish":
                                    wait(act, acted, (gr.n - 1) * halves)
                                    act.activation(y[:, gr.s, h], hid_ps[h][:, 0:GB * P], ACT.Identity,
                                                   bias=bias1[h]).then_inc(read, 1)
                                else:
                                    act.activation(hid[:, gr.s, h], hid_ps[h][:, 0:GB * P], func, bias=bias1[h]).then_inc(read, 1)
                            if func == "mish":
                                for h in range(halves):
                                    wait(act, capped, gr.n * halves + (h + 1))
                                    act.activation(u[:, gr.s, h], u[:, gr.s, h], ACT.Exp).then_inc(exped, 1)
                        pipeline(act, [(take, 0), (flatten, 0), (activate, 1)], GROUPS, 2)

                    @block.tensor
                    def _(pe):
                        def turn(gr):
                            wait(pe, copied, gr.n * N)
                            wait(pe, taken, (gr.n + 1) * N)
                            hold(pe)
                            for i, (_, w, _) in enumerate(parts):
                                for b in range(GB):
                                    mm = pe.transpose(flip[i][0:w, b * P:(b + 1) * P], part[i][:, gr.s, b, :], eye)
                            mm.then_inc(flipped, 1)

                        def hide(gr):
                            wait(pe, copied, (gr.n + 1) * N)
                            for h in range(halves):
                                wait(pe, read, (gr.n - 1) * halves + (h + 1))
                                hold(pe)
                                for lo, hi in ((0, 512), (512, GB * P)):
                                    for i, (_, w, w1) in enumerate(parts):
                                        mm = pe.matmul(hid_ps[h][:, lo:hi], w1[:, h * P:h * P + hid_w], flat[i][:, gr.s, lo:hi],
                                                       start=(i == 0), stop=(i == N - 1))
                                mm.then_inc(hidden, 1)

                        def multiply(gr):
                            wait(pe, used, gr.n)
                            wait(pe, acted if func == "mish" else read, (gr.n + 1) * halves)
                            hold(pe)
                            for b in range(GB):
                                for h in range(halves):
                                    mm = pe.matmul(prod[:, b, :], hid[:, gr.s, h, b * P:(b + 1) * P], w2[h],
                                                   start=(h == 0), stop=(h == halves - 1))
                            mm.then_inc(made, 1)
                        pipeline(pe, [(turn, 0), (hide, 0), (multiply, 2)], GROUPS, 2)

                    @block.vector
                    def _(dve):
                        if arrival is not None:
                            arrival.prepare(dve)

                        def mish(gr):
                            for h in range(halves):
                                n = gr.n * halves + h
                                wait(dve, read, n + 1)
                                wait(dve, squared, n - 1 - (halves - 1))
                                dve.tensor_scalar(u[:, gr.s, h], y[:, gr.s, h], CAP, None, ALU.min).then_inc(capped, 1)
                            for h in range(halves):
                                n = gr.n * halves + h
                                y_, u_, q_, r_ = (t[:, gr.s, h] for t in (y, u, q, r))
                                wait(dve, exped, n + 1)
                                dve.scalar_tensor_tensor(q_, u_, 2.0, u_, ALU.add, ALU.mult).then_inc(squared, 1)
                                wait(dve, squared, n + 1)
                                dve.tensor_scalar(r_, q_, 2.0, None, ALU.add).then_inc(lifted, 1)
                                wait(dve, lifted, n + 1)
                                dve.reciprocal(r_, r_).then_inc(inverted, 1)
                                wait(dve, inverted, n + 1)
                                dve.tensor_tensor(q_, q_, r_, ALU.mult).then_inc(scaled, 1)
                                wait(dve, scaled, n + 1)
                                wait(dve, made, gr.n - 1)
                                dve.tensor_tensor(hid[:, gr.s, h], q_, y_, ALU.mult).then_inc(acted, 1)

                        def take_out(gr):
                            wait(dve, made, gr.n + 1)
                            rows = bass.ds(gr.n * GB, GB)
                            dve.tensor_tensor(dst[:, rows, :], prod[:, :, :], add[:, rows, :], ALU.add).then_inc(used, 1)
                        pipeline(dve, ([(mish, 1)] if func == "mish" else []) + [(take_out, 2)], GROUPS, 2)
                        dve.wait_ge(used, GROUPS)
                        dve.tensor_tensor(dst[:, :, :], dst[:, :, :], bcast_mid(bias2, BLOCKS), ALU.add).then_inc(used, 1)
                        dve.wait_ge(used, GROUPS + 1)

        def edges01():
            with ExitStack() as ctx:
                we = sb("e0_we", [32, P], F32, ctx)
                be = sb("e0_be", [P, 1], F32, ctx)
                idx = sb("e0_idx", [P, RING, 2, TPC], I32, ctx)
                sent_x = sb("e0_x", [P, RING, TPC, 2, D], F32, ctx)
                attr = sb("e0_attr", [32, RING, CH], F32, ctx)
                keep0 = sb("e0_keep", [P, RING, CH], BF16, ctx)
                y = sb("e0_y", [P, RING, CH], F32, ctx)
                cap, u, w, den, r, t, m, scan = (sb("e0_" + n, [P, 2, CH], F32, ctx) for n in
                                                 ("cap", "u", "w", "den", "r", "t", "m", "scan"))
                rows0 = sb("e0_rows", [P, 2, 2, TPC, D], F32, ctx)
                z = [bank(f"e0_z{s}", ctx, P, CH) for s in range(2)]
                back0 = [bank(f"e0_back{s}", ctx, P, TPC, P) for s in range(2)]
                J, W = STREAMS_S, 2 * P
                rec = sb("e1_rec", [P, RING, J, 2, REC], F32, ctx)
                side = sb("e1_side", [P, 2, 2, J, DE], F32, ctx)
                keep1 = sb("e1_keep", [P, RING, W], BF16, ctx)
                fresh = sb("e1_fresh", [P, 2, W], F32, ctx)
                sums = sb("e1_sum", [P, 2, W], F32, ctx)
                tops = sb("e1_top", [P, 2, W], F32, ctx)
                rows1 = sb("e1_rows", [P, 2, J, 2, 2 * DE], F32, ctx)
                flat = [bank(f"e1_flat{s}", ctx, P, W) for s in range(2)]
                back1 = [bank(f"e1_back{s}", ctx, P, 4, P) for s in range(2)]

                zero = sb("e0_zero", [P, EP // UNITS], F32, ctx)
                zeroed, cleared, early_moved = sem("e0_zeroed"), sem("e0_cleared"), sem("e0_early")
                with nc.Block() as block:
                    @block.vector
                    def _(dve):
                        dve.memset(zero[:, :], 0.0).then_inc(zeroed, 1)
                        dve.memset(we[:, :], 0.0).then_inc(zeroed, 1)
                        dve.wait_ge(zeroed, 2)
                load([(we[0:16, 0:D], a["L0_We_kernel"]), (we[16:32, D:P], a["L0_We_kernel"]),
                      (be[0:D, :], a["L0_We_bias"].rearrange("(p o) -> p o", o=1)),
                      (be[D:P, :], a["L0_We_bias"].rearrange("(p o) -> p o", o=1))], "e0w")
                (idx_made, z_made, y_made, cap_made, u_made, w_made, den_made, r_made, t_made, m_made, scanned, flipped0,
                 copied0) = (sem("e0_" + n) for n in ("si", "sz", "sy", "sc", "su", "sw", "sd", "sr", "st", "sm", "ss", "sf", "so"))
                flat_made, fresh_made, summed, topped, flipped1, copied1, ids_made, sided = (
                    sem("e1_" + n) for n in ("sf", "sr", "ss", "st", "sb", "sc", "si", "sd"))
                got, in0, in1, in_keep0 = ([sem(f"e01_{n}{s}") for s in range(RING)] for n in ("got", "in0", "in1", "ik"))
                out0, out1 = ([sem(f"e01_{n}{s}") for s in range(2)] for n in ("out0", "out1"))
                rec_streams = rec_s.rearrange("(j u) f -> j u f", j=J)
                run1_streams = run1.rearrange("(j u) f -> j u f", j=J)
                run0_streams = run0.rearrange("(h u) f -> h u f", h=2)
                attr_halves = a["attr16_t"].rearrange("f (h u) -> h f u", h=2)
                keep_d_halves = keep["d"].rearrange("(h u) -> h u", h=2)
                keep_s_streams = keep["s"].rearrange("(j u) -> j u", j=J)
                src_halves = src_i[:, :].rearrange("p (h t) -> p h t", h=2)
                ids_quarters = ids_s[:, :].rearrange("p (j t) -> p j t", j=J)
                weight_quarters = weight_s[:, :].rearrange("p (j t) -> p j t", j=J)
                with nc.Block() as block:
                    @block.gpsimd
                    def _(pool):
                        def gather(un):
                            wait(pool, idx_made, un.n + 1)
                            wait(pool, z_made, un.n + 1 - RING)
                            hold(pool)
                            for q in range(TPC):
                                for h in range(2):
                                    if (q, h) == (0, 0):
                                        continue
                                    pool.indirect_dma_start(sent_x[:, un.s, q, h, :], None, a["x"],
                                                            bass.IndirectOffsetOnAxis(idx[:, un.s, h, q:q + 1], 0)
                                                            ).then_inc(got[un.s], 16)
                        pipeline(pool, [(gather, 0)], UNITS, RING)

                    @block.sync
                    def _(sp):
                        def fetch(un):
                            wait(sp, z_made, un.n + 1 - RING)
                            hold(sp)
                            sp.dma_start(attr[:, un.s], attr_halves[:, :, bass.ds(un.n * CH, CH)]).then_inc(in0[un.s], 16)
                            wait(sp, sided, un.n + 1 - RING)
                            hold(sp)
                            wait(sp, ids_made, (un.n + 1 - RING) * 2)
                            hold(sp)
                            sp.dma_start(rec[:, un.s], rec_streams[:, bass.ds(un.n * W, W), :]
                                         .rearrange("j (p t) f -> p j (t f)", p=P)).then_inc(in1[un.s], 16)
                            wait(sp, summed, un.n + 1 - RING)
                            hold(sp)
                            wait(sp, fresh_made, un.n + 1 - RING)
                            hold(sp)
                            sp.dma_start(keep1[:, un.s], keep_s_streams[:, bass.ds(un.n * W, W)].unsqueeze(1)
                                         .to_broadcast([J, DE, W])).then_inc(in1[un.s], 16)

                        def fetch_keep0(un):
                            wait(sp, scanned, un.n + 1 - RING)
                            hold(sp)
                            sp.dma_start(keep0[:, un.s], keep_d_halves[:, bass.ds(un.n * CH, CH)].unsqueeze(1)
                                         .to_broadcast([2, D, CH])).then_inc(in_keep0[un.s], 16)

                        def clear(un):
                            for table in (q_rows, a_rows):
                                sp.dma_start(table[bass.ds(un.n * (EP // UNITS), EP // UNITS), :].rearrange("(p t) f -> p (t f)", p=P),
                                             zero[:, :]).then_inc(cleared, 16)
                        pipeline(sp, [(fetch, 0), (fetch_keep0, 2), (clear, 2)], UNITS, RING)
                        sp.wait_ge(cleared, 2 * UNITS * 16)

                    @block.tensor
                    def _(pe):
                        def turn_in(un):
                            wait(pe, summed, un.n - 1)
                            wait(pe, topped, un.n - 1)
                            wait(pe, sided, un.n + 1)
                            hold(pe)
                            for q in range(2):
                                mm = pe.transpose(tile_cols(flat[un.p], q, 2),
                                                  side[:, un.p, q].rearrange("p j f -> p (j f)"), eye)
                            mm.then_inc(flat_made, 1)

                        def make_z(un):
                            wait(pe, in0[un.s], un.landed(1))
                            wait(pe, got[un.s], un.landed(2 * TPC - 1))
                            wait(pe, early_moved, un.n + 1)
                            wait(pe, y_made, un.n - 1)
                            hold(pe)
                            pe.matmul(z[un.p], we[:, :], attr[:, un.s], start=True, stop=False)
                            for q in range(TPC):
                                mm = pe.matmul(tile_cols(z[un.p], q, TPC),
                                               sent_x[:, un.s, q].rearrange("p h f -> p (h f)"), eye,
                                               is_transpose=True, start=False, stop=(q == TPC - 1))
                            mm.then_inc(z_made, 1)

                        def turn_out1(un):
                            wait(pe, summed, un.n + 1)
                            wait(pe, topped, un.n + 1)
                            wait(pe, copied1, (un.n - 1) * 2)
                            hold(pe)
                            for q in range(2):
                                pe.transpose(back1[un.p][:, q, :], tile_cols(sums[:, un.p], q, 2), eye)
                                mm = pe.transpose(back1[un.p][:, 2 + q, :], tile_cols(tops[:, un.p], q, 2), eye)
                            mm.then_inc(flipped1, 1)

                        def turn_out0(un):
                            wait(pe, scanned, un.n + 1)
                            wait(pe, copied0, un.n - 1)
                            hold(pe)
                            for q in range(TPC):
                                mm = pe.transpose(back0[un.p][:, q, :], tile_cols(scan[:, un.p], q, TPC), eye)
                            mm.then_inc(flipped0, 1)
                        pipeline(pe, [(turn_in, 0), (make_z, 0), (turn_out1, 2), (turn_out0, 4)], UNITS, RING)

                    @block.scalar
                    def _(act):
                        def store0(un):
                            wait(act, flipped0, un.n + 1)
                            wait(act, out0[un.p], un.uses2 * 16)
                            act.copy(rows0[:, un.p], back0[un.p].rearrange("p t (h f) -> p h t f", h=2)).then_inc(copied0, 1)
                            wait(act, copied0, un.n + 1)
                            act.dma_start(run0_streams[:, bass.ds(un.n * CH, CH), :].rearrange("h (p t) f -> p h (t f)", p=P),
                                          rows0[:, un.p]).then_inc(out0[un.p], 16)

                        def store1(un):
                            wait(act, flipped1, un.n + 1)
                            wait(act, out1[un.p], un.uses2 * 16)
                            for k in range(2):
                                act.copy(rows1[:, un.p, :, :, k * DE:(k + 1) * DE],
                                         back1[un.p][:, 2 * k:2 * k + 2, :].rearrange("p q (j f) -> p j q f", j=J)
                                         ).then_inc(copied1, 1)
                            wait(act, copied1, (un.n + 1) * 2)
                            act.dma_start(run1_streams[:, bass.ds(un.n * W, W), :].rearrange("j (p t) f -> p j (t f)", p=P),
                                          rows1[:, un.p]).then_inc(out1[un.p], 16)

                        def index(un):
                            wait(act, got[un.s], un.landed_before(2 * TPC - 1))
                            act.copy(idx[:, un.s], src_halves[:, :, bass.ds(un.n * TPC, TPC)]).then_inc(idx_made, 1)

                        def move_early(un):
                            wait(act, z_made, un.n + 1 - RING)
                            act.copy(sent_x[:, un.s, 0, 0:1, :], early_x[:, bass.ds(un.n, 1), :]).then_inc(early_moved, 1)

                        def front1(un):
                            wait(act, in1[un.s], un.landed(2))
                            wait(act, flat_made, un.n - 1)
                            act.copy(side[:, un.p], rec[:, un.s, :, :, 0:DE].rearrange("p j q f -> p q j f")).then_inc(sided, 1)
                            wait(act, topped, un.n - 1)
                            act.activation(fresh[:, un.p], keep1[:, un.s], ACT.Copy, bias=-BIG, scale=BIG).then_inc(fresh_made, 1)

                        def bias(un):
                            wait(act, z_made, un.n + 1)
                            wait(act, cap_made, un.n + 1 - RING)
                            wait(act, m_made, un.n + 1 - RING)
                            act.activation(y[:, un.s], z[un.p], ACT.Identity, bias=be[:, :]).then_inc(y_made, 1)

                        def lift(un):
                            wait(act, w_made, un.n + 1)
                            wait(act, r_made, un.n - 1)
                            act.activation(den[:, un.p], w[:, un.p], ACT.Copy, bias=2.0).then_inc(den_made, 1)

                        def expo(un):
                            wait(act, cap_made, un.n + 1)
                            wait(act, w_made, un.n - 1)
                            act.activation(u[:, un.p], cap[:, un.p], ACT.Exp).then_inc(u_made, 1)
                        pipeline(act, [(index, 0), (move_early, 3), (bias, 4), (lift, 5), (expo, 4), (front1, 3), (store1, 6), (store0, 8)], UNITS, RING)
                        for s in range(2):
                            act.wait_ge(out0[s], uses_of(s, UNITS, 2) * 16)
                            act.wait_ge(out1[s], uses_of(s, UNITS, 2) * 16)

                    @block.vector
                    def _(dve):
                        def square(un):
                            wait(dve, u_made, un.n + 1)
                            wait(dve, den_made, un.n - 1)
                            wait(dve, t_made, un.n - 1)
                            dve.scalar_tensor_tensor(w[:, un.p], u[:, un.p], 2.0, u[:, un.p], ALU.add,
                                                     ALU.mult).then_inc(w_made, 1)

                        def bound(un):
                            wait(dve, y_made, un.n + 1)
                            wait(dve, u_made, un.n - 1)
                            dve.tensor_scalar(cap[:, un.p], y[:, un.s], CAP, None, ALU.min).then_inc(cap_made, 1)

                        def mish(un):
                            wait(dve, den_made, un.n + 1)
                            dve.reciprocal(r[:, un.p], den[:, un.p]).then_inc(r_made, 1)
                            wait(dve, r_made, un.n + 1)
                            wait(dve, w_made, un.n + 1)
                            dve.tensor_tensor(t[:, un.p], w[:, un.p], r[:, un.p], ALU.mult).then_inc(t_made, 1)
                            wait(dve, t_made, un.n + 1)
                            wait(dve, y_made, un.n + 1)
                            wait(dve, scanned, un.n - 1)
                            dve.tensor_tensor(m[:, un.p], t[:, un.p], y[:, un.s], ALU.mult).then_inc(m_made, 1)
                            wait(dve, m_made, un.n + 1)
                            wait(dve, in_keep0[un.s], un.landed(1))
                            wait(dve, scanned, un.n)
                            wait(dve, flipped0, un.n - 1)
                            dve.tensor_tensor_scan(scan[:, un.p], keep0[:, un.s], m[:, un.p],
                                                   0.0 if un.first else scan[:, 1 - un.p, CH - 1:CH],
                                                   ALU.mult, ALU.add).then_inc(scanned, 1)

                        def layer1(un):
                            wait(dve, in1[un.s], un.landed(2))
                            tiles = bass.ds(un.n * 2, 2)
                            dve.tensor_copy(ids_quarters[:, :, tiles], rec[:, un.s, :, :, RECF].bitcast(I32)).then_inc(ids_made, 1)
                            dve.tensor_copy(weight_quarters[:, :, tiles], rec[:, un.s, :, :, DE]).then_inc(ids_made, 1)
                            wait(dve, flat_made, un.n + 1)
                            wait(dve, flipped1, un.n - 1)
                            wait(dve, summed, un.n)
                            dve.tensor_tensor_scan(sums[:, un.p], keep1[:, un.s], flat[un.p],
                                                   0.0 if un.first else sums[:, 1 - un.p, W - 1:W],
                                                   ALU.mult, ALU.add).then_inc(summed, 1)
                            wait(dve, fresh_made, un.n + 1)
                            wait(dve, topped, un.n)
                            dve.tensor_tensor_scan(tops[:, un.p], fresh[:, un.p], flat[un.p],
                                                   -BIG if un.first else tops[:, 1 - un.p, W - 1:W],
                                                   ALU.add, ALU.max).then_inc(topped, 1)
                        pipeline(dve, [(square, 2), (bound, 1), (mish, 3), (layer1, 1)], UNITS, RING)
                        dve.wait_ge(ids_made, UNITS * 2)

        def edges2():
            with ExitStack() as ctx:
                we = sb("e2_we", [DE, P], F32, ctx)
                heads = sb("e2_heads", [P, P], F32, ctx)
                idx = sb("e2_idx", [P, RING, TPC], I32, ctx)
                q_g = sb("e2_qg", [P, RING, TPC, P], F32, ctx)
                kv_g = sb("e2_kv", [P, RING, TPC, 2 * P], F32, ctx)
                attr = sb("e2_attr", [DE, RING, CH], F32, ctx)
                keep2 = sb("e2_keep", [P, RING, CH], BF16, ctx)
                qf, qk, low, drop, num, den = (sb("e2_" + n, [P, 2, CH], F32, ctx) for n in
                                               ("qf", "qk", "low", "drop", "num", "den"))
                fresh, pr, fade = (sb("e2_" + n, [P, RING, CH], F32, ctx) for n in ("fresh", "pr", "fade"))
                pv = sb("e2_pv", [P, CH], F32, ctx)
                top_ = sb("e2_top", [P, 2, CH], F32, ctx)
                top_end = sb("e2_top_end", [P, 2], F32, ctx)
                rel = sb("e2_rel", [P, 2, CH], F32, ctx)
                rows = sb("e2_rows", [P, 2, TPC, 130], F32, ctx)
                q_p, k_p = [bank(f"e2_qp{s}", ctx, P, CH) for s in range(1)], [bank(f"e2_kp{s}", ctx, P, CH) for s in range(2)]
                v_p = [bank(f"e2_vp{s}", ctx, P, CH) for s in range(2)]
                al_p, num_p, den_p = bank("e2_alp", ctx, P, CH), bank("e2_nump", ctx, P, TPC, P), bank("e2_denp", ctx, P, TPC, D + 1)
                load([(we[:, :], a["L2_We"]), (heads[:, :], a["heads"])], "e2w")
                names = ("idx", "q", "k", "v", "qf", "qk", "al", "fresh", "edge", "top", "last", "rel", "low", "drop", "pr", "fade",
                         "pv", "num", "den", "flip", "copy")
                (idx_made, q_made, k_made, v_made, filled, qk_made, al_made, fresh_made, edge_made, top_made, last_made,
                 rel_made, low_made, drop_made, pr_made, fade_made, pv_made, num_made, den_made, flipped, copied) = (
                     sem("e2_s" + n) for n in names)
                got, q_in, loaded, stored = ([sem(f"e2_{n}{s}") for s in range(RING)] for n in ("got", "qi", "ld", "st_"))
                with nc.Block() as block:
                    @block.gpsimd
                    def _(pool):
                        def gather(ch):
                            wait(pool, got[ch.s], ch.landed_before(TPC))
                            pool.tensor_copy(idx[:, ch.s], src_i[:, bass.ds(ch.n * TPC, TPC)]).then_inc(idx_made, 1)
                            wait(pool, idx_made, ch.n + 1)
                            wait(pool, v_made, ch.n + 1 - RING)
                            hold(pool)
                            for t in range(TPC):
                                pool.indirect_dma_start(kv_g[:, ch.s, t, :], None, kv_tab,
                                                        bass.IndirectOffsetOnAxis(idx[:, ch.s, t:t + 1], 0)
                                                        ).then_inc(got[ch.s], 16)
                        pipeline(pool, [(gather, 0)])

                    @block.sync
                    def _(sp):
                        def fetch(ch):
                            rows_ = bass.ds(ch.n * CH, CH)
                            wait(sp, q_made, ch.n + 1 - RING)
                            hold(sp)
                            sp.dma_start(q_g[:, ch.s], q_rows[rows_, :].rearrange("(p t) f -> p t f", p=P)
                                         ).then_inc(q_in[ch.s], 16)
                            wait(sp, v_made, ch.n + 1 - RING)
                            hold(sp)
                            wait(sp, filled, ch.n + 1 - RING)
                            hold(sp)
                            wait(sp, fresh_made, ch.n + 1 - RING)
                            hold(sp)
                            sp.dma_start(attr[:, ch.s], a["attr32_t"][:, rows_]).then_inc(loaded[ch.s], 16)
                            sp.dma_start(keep2[:, ch.s], keep["d"][rows_].partition_broadcast(P)).then_inc(loaded[ch.s], 16)
                        pipeline(sp, [(fetch, 0)])

                    @block.tensor
                    def _(pe):
                        def plus_edges(ch, dst, j):
                            pe.matmul(dst, we[:, :], attr[:, ch.s], start=True, stop=False)
                            for t in range(TPC):
                                mm = pe.matmul(tile_cols(dst, t, TPC), kv_g[:, ch.s, t, j * P:(j + 1) * P], eye,
                                               is_transpose=True, start=False, stop=(t == TPC - 1))
                            return mm

                        def make_qk(ch):
                            wait(pe, q_in[ch.s], ch.landed(1))
                            wait(pe, filled, ch.n)
                            hold(pe)
                            for t in range(TPC):
                                mm = pe.transpose(tile_cols(q_p[0], t, TPC), q_g[:, ch.s, t, :], eye)
                            mm.then_inc(q_made, 1)
                            wait(pe, got[ch.s], ch.landed(TPC))
                            wait(pe, loaded[ch.s], ch.landed(2))
                            wait(pe, qk_made, ch.n - 1)
                            hold(pe)
                            plus_edges(ch, k_p[ch.p], 0).then_inc(k_made, 1)

                        def make_al(ch):
                            wait(pe, qk_made, ch.n + 1)
                            wait(pe, rel_made, ch.n)
                            hold(pe)
                            pe.matmul(al_p, heads[:, :], qk[:, ch.p], start=True, stop=True).then_inc(al_made, 1)

                        def make_v(ch):
                            wait(pe, pv_made, ch.n - 1)
                            hold(pe)
                            plus_edges(ch, v_p[ch.p], 1).then_inc(v_made, 1)

                        def turn(ch):
                            wait(pe, num_made, ch.n + 1)
                            wait(pe, den_made, ch.n + 1)
                            wait(pe, copied, ch.n * 2)
                            hold(pe)
                            for t in range(TPC):
                                pe.transpose(num_p[:, t, :], tile_cols(num[:, ch.p], t, TPC), eye)
                                mm = pe.transpose(den_p[:, t, :], tile_cols(den[0:D + 1, ch.p], t, TPC), eye[0:D + 1, 0:D + 1])
                            mm.then_inc(flipped, 1)
                        pipeline(pe, [(make_al, 1), (make_qk, 0), (make_v, 1), (turn, 3)])

                    @block.scalar
                    def _(act):
                        def front(ch):
                            wait(act, loaded[ch.s], ch.landed(2))
                            wait(act, top_made, ch.n + 1 - RING)
                            act.activation(fresh[:, ch.s], keep2[:, ch.s], ACT.Copy, bias=-BIG, scale=BIG).then_inc(fresh_made, 1)

                        def weigh(ch):
                            wait(act, rel_made, ch.n + 1)
                            wait(act, pr_made, ch.n - 1)
                            act.activation(low[:, ch.p], rel[:, ch.p], ACT.Relu).then_inc(low_made, 1)
                            wait(act, fade_made, ch.n - 1)
                            act.activation(drop[:, ch.p], rel[:, ch.p], ACT.Relu, scale=-1.0).then_inc(drop_made, 1)
                            wait(act, low_made, ch.n + 1)
                            wait(act, den_made, ch.n + 1 - RING)
                            act.activation(pr[:, ch.s], low[:, ch.p], ACT.Exp, scale=-D ** -0.5).then_inc(pr_made, 1)
                            wait(act, drop_made, ch.n + 1)
                            wait(act, num_made, ch.n + 1 - RING)
                            act.activation(fade[:, ch.s], drop[:, ch.p], ACT.Exp, scale=-D ** -0.5).then_inc(fade_made, 1)

                        def store(ch):
                            wait(act, flipped, ch.n + 1)
                            wait(act, stored[ch.p], (ch.uses2) * 16)
                            act.copy(rows[:, ch.p, :, 0:P], num_p).then_inc(copied, 1)
                            act.copy(rows[:, ch.p, :, P:130], den_p[:, :, 0:D + 1:D]).then_inc(copied, 1)
                            wait(act, copied, ch.n * 2 + 2)
                            act.dma_start(run2[bass.ds(ch.n * CH, CH), :].rearrange("(p t) f -> p t f", p=P),
                                          rows[:, ch.p]).then_inc(stored[ch.p], 16)
                        pipeline(act, [(front, 0), (weigh, 1), (store, 3)])
                        for s in range(2):
                            act.wait_ge(stored[s], uses_of(s, CHUNKS, 2) * 16)

                    @block.vector
                    def _(dve):
                        dve.memset(top_end[:, 1:2], 0.0).then_inc(last_made, 1)

                        def fill(ch):
                            wait(dve, q_made, ch.n + 1)
                            wait(dve, loaded[ch.s], ch.landed(2))
                            wait(dve, qk_made, ch.n)
                            dve.tensor_tensor_scan(qf[:, ch.p], keep2[:, ch.s], q_p[0],
                                                   0.0 if ch.first else qf[:, 1 - ch.p, CH - 1:CH],
                                                   ALU.mult, ALU.add).then_inc(filled, 1)

                        def multiply(ch):
                            wait(dve, filled, ch.n + 1)
                            wait(dve, k_made, ch.n + 1)
                            wait(dve, al_made, ch.n - 1)
                            dve.tensor_tensor(qk[:, ch.p], qf[:, ch.p], k_p[ch.p], ALU.mult).then_inc(qk_made, 1)

                        def first_max(ch):
                            wait(dve, last_made, ch.n + 1)
                            wait(dve, fresh_made, ch.n + 1)
                            wait(dve, rel_made, ch.n - 1)
                            dve.tensor_tensor(top_[:, ch.p, 0:1], top_end[:, 1 - ch.p:2 - ch.p], fresh[:, ch.s, 0:1],
                                              ALU.add).then_inc(edge_made, 1)

                        def maxima(ch):
                            wait(dve, edge_made, ch.n + 1)
                            wait(dve, al_made, ch.n + 1)
                            dve.tensor_tensor_scan(top_[:, ch.p, 1:CH], al_p[:, 0:CH - 1], fresh[:, ch.s, 1:CH],
                                                   top_[:, ch.p, 0:1], ALU.max, ALU.add).then_inc(top_made, 1)

                        def relate(ch):
                            wait(dve, top_made, ch.n + 1)
                            dve.tensor_tensor(top_end[:, ch.p:ch.p + 1], top_[:, ch.p, CH - 1:CH], al_p[:, CH - 1:CH],
                                              ALU.max).then_inc(last_made, 1)
                            wait(dve, low_made, ch.n - 1)
                            wait(dve, drop_made, ch.n - 1)
                            dve.tensor_tensor(rel[:, ch.p], top_[:, ch.p], al_p, ALU.subtract).then_inc(rel_made, 1)

                        def sums(ch):
                            wait(dve, pr_made, ch.n + 1)
                            wait(dve, v_made, ch.n + 1)
                            wait(dve, num_made, ch.n)
                            dve.tensor_tensor(pv[:, :], pr[:, ch.s], v_p[ch.p], ALU.mult).then_inc(pv_made, 1)
                            wait(dve, fade_made, ch.n + 1)
                            wait(dve, den_made, ch.n)
                            wait(dve, flipped, ch.n - 1)
                            dve.tensor_tensor_scan(den[:, ch.p], fade[:, ch.s], pr[:, ch.s],
                                                   0.0 if ch.first else den[:, 1 - ch.p, CH - 1:CH],
                                                   ALU.mult, ALU.add).then_inc(den_made, 1)
                            wait(dve, pv_made, ch.n + 1)
                            dve.tensor_tensor_scan(num[:, ch.p], fade[:, ch.s], pv[:, :],
                                                   0.0 if ch.first else num[:, 1 - ch.p, CH - 1:CH],
                                                   ALU.mult, ALU.add).then_inc(num_made, 1)
                        pipeline(dve, [(first_max, 1), (fill, 0), (maxima, 1), (multiply, 0), (relate, 1), (sums, 2)])

        def edges3():
            with ExitStack() as ctx:
                w_d = sb("e3_wd", [P, P], F32, ctx)
                w2 = sb("e3_w2", [P, P], F32, ctx)
                b1, b1v = column("e3_b1", a["L3_eb1"], ctx)
                b2, b2v = column("e3_b2", a["L3_eb2"], ctx)
                idx = sb("e3_idx", [P, RING, TPC], I32, ctx)
                a_g = sb("e3_ag", [P, RING, TPC, P], F32, ctx)
                b_g = sb("e3_bg", [P, RING, TPC, P], F32, ctx)
                keep3 = sb("e3_keep", [P, RING, CH], BF16, ctx)
                af, zs, h1, h2, scan = (sb("e3_" + n, [P, 2, CH], F32, ctx) for n in ("af", "zs", "h1", "h2", "scan"))
                rows = sb("e3_rows", [P, 2, TPC, P], F32, ctx)
                ps = lambda n: [bank(f"{n}{s}", ctx, P, CH) for s in range(2)]
                a_p, z, z2, back = ps("e3_ap"), ps("e3_z"), ps("e3_z2"), ps("e3_back")
                load([(w_d[:, :], a["L3_eW1"][2 * D:2 * D + 1, :].rearrange("a b -> (a b)").partition_broadcast(P)),
                      (w2[:, :], a["L3_eW2"]), (b1[:, :], b1v), (b2[:, :], b2v)], "e3w")

                def cols(ap, t):
                    return tile_cols(ap[:, t // 2 * 2 * P:(t // 2 + 1) * 2 * P], t % 2, 2)
                names = ("idx", "fold", "a", "z", "af", "zs", "h1", "z2", "h2", "scan", "flip", "copy")
                (idx_made, folded, a_made, z_made, filled, zs_made, h1_made, z2_made, h2_made, scanned, flipped, copied) = (
                    sem("e3_s" + n) for n in names)
                got, a_in = ([sem(f"e3_{n}{s}") for s in range(RING)] for n in ("got", "ai"))
                kept, stored = [sem(f"e3_kp{s}") for s in range(RING)], [sem(f"e3_st{s}") for s in range(2)]
                with nc.Block() as block:
                    @block.gpsimd
                    def _(pool):
                        def gather(ch):
                            wait(pool, idx_made, ch.n + 1)
                            wait(pool, z_made, ch.n + 1 - RING)
                            hold(pool)
                            for t in range(TPC):
                                pool.indirect_dma_start(b_g[:, ch.s, t, :], None, b_tab,
                                                        bass.IndirectOffsetOnAxis(idx[:, ch.s, t:t + 1], 0)
                                                        ).then_inc(got[ch.s], 16)
                        pipeline(pool, [(gather, 0)])

                    @block.sync
                    def _(sp):
                        def fetch(ch):
                            rows_ = bass.ds(ch.n * CH, CH)
                            wait(sp, a_made, ch.n + 1 - RING)
                            hold(sp)
                            sp.dma_start(a_g[:, ch.s], a_rows[rows_, :].rearrange("(u p q) f -> p u (q f)", p=P, q=2)
                                         ).then_inc(a_in[ch.s], 16)
                            wait(sp, scanned, ch.n + 1 - RING)
                            hold(sp)
                            sp.dma_start(keep3[:, ch.s], keep["s"][rows_].partition_broadcast(P)).then_inc(kept[ch.s], 16)
                        pipeline(sp, [(fetch, 0)])

                    @block.tensor
                    def _(pe):
                        def turn_a(ch):
                            wait(pe, a_in[ch.s], ch.landed(1))
                            wait(pe, filled, ch.n - 1)
                            hold(pe)
                            for t in range(TPC):
                                mm = pe.transpose(cols(a_p[ch.p], t), a_g[:, ch.s, t, :], eye)
                            mm.then_inc(a_made, 1)

                        def turn_b(ch):
                            wait(pe, folded, (ch.n + 1) * TPC)
                            wait(pe, zs_made, ch.n - 1)
                            hold(pe)
                            for t in range(TPC):
                                mm = pe.transpose(cols(z[ch.p], t), b_g[:, ch.s, t, :], eye)
                            mm.then_inc(z_made, 1)

                        def second(ch):
                            wait(pe, h1_made, ch.n + 1)
                            wait(pe, h2_made, ch.n - 1)
                            hold(pe)
                            pe.matmul(z2[ch.p], w2[:, :], h1[:, ch.p], start=True, stop=True).then_inc(z2_made, 1)

                        def turn_out(ch):
                            wait(pe, scanned, ch.n + 1)
                            wait(pe, copied, ch.n - 1)
                            hold(pe)
                            for t in range(TPC):
                                mm = pe.transpose(back[ch.p][:, t * P:(t + 1) * P], cols(scan[:, ch.p], t), eye)
                            mm.then_inc(flipped, 1)
                        pipeline(pe, [(turn_a, 0), (turn_b, 0), (second, 1), (turn_out, 2)])

                    @block.scalar
                    def _(act):
                        def index(ch):
                            wait(act, got[ch.s], ch.landed_before(TPC))
                            act.copy(idx[:, ch.s], ids_s[:, bass.ds(ch.n * TPC, TPC)]).then_inc(idx_made, 1)

                        def first(ch):
                            wait(act, zs_made, ch.n + 1)
                            wait(act, z2_made, ch.n - 1)
                            act.activation(h1[:, ch.p], zs[:, ch.p], ACT.Silu, bias=b1[:, :]).then_inc(h1_made, 1)

                        def second(ch):
                            wait(act, z2_made, ch.n + 1)
                            wait(act, scanned, ch.n - 1)
                            act.activation(h2[:, ch.p], z2[ch.p], ACT.Silu, bias=b2[:, :]).then_inc(h2_made, 1)

                        def store(ch):
                            wait(act, flipped, ch.n + 1)
                            wait(act, stored[ch.p], ch.uses2 * 16)
                            act.copy(rows[:, ch.p].rearrange("p t f -> p (t f)"), back[ch.p]).then_inc(copied, 1)
                            wait(act, copied, ch.n + 1)
                            act.dma_start(run3[bass.ds(ch.n * CH, CH), :].rearrange("(u p q) f -> p u (q f)", p=P, q=2),
                                          rows[:, ch.p]).then_inc(stored[ch.p], 16)
                        pipeline(act, [(index, 0), (first, 4), (second, 4), (store, 5)])
                        for s in range(2):
                            act.wait_ge(stored[s], uses_of(s, CHUNKS, 2) * 16)

                    @block.vector
                    def _(dve):
                        def fold(ch):
                            wait(dve, got[ch.s], ch.landed(TPC))
                            for t in range(TPC):
                                dve.scalar_tensor_tensor(b_g[:, ch.s, t, :], w_d[:, :], weight_s[:, bass.ds(ch.n * TPC + t, 1)],
                                                         b_g[:, ch.s, t, :], ALU.mult, ALU.add).then_inc(folded, 1)

                        def fill(ch):
                            wait(dve, a_made, ch.n + 1)
                            wait(dve, kept[ch.s], ch.landed(1))
                            wait(dve, filled, ch.n)
                            wait(dve, zs_made, ch.n - 1)
                            dve.tensor_tensor_scan(af[:, ch.p], keep3[:, ch.s], a_p[ch.p],
                                                   0.0 if ch.first else af[:, 1 - ch.p, CH - 1:CH],
                                                   ALU.mult, ALU.add).then_inc(filled, 1)

                        def add(ch):
                            wait(dve, z_made, ch.n + 1)
                            wait(dve, filled, ch.n + 1)
                            wait(dve, h1_made, ch.n - 1)
                            dve.tensor_tensor(zs[:, ch.p], af[:, ch.p], z[ch.p], ALU.add).then_inc(zs_made, 1)

                        def scan_(ch):
                            wait(dve, h2_made, ch.n + 1)
                            wait(dve, scanned, ch.n)
                            wait(dve, flipped, ch.n - 1)
                            dve.tensor_tensor_scan(scan[:, ch.p], keep3[:, ch.s], h2[:, ch.p],
                                                   0.0 if ch.first else scan[:, 1 - ch.p, CH - 1:CH],
                                                   ALU.mult, ALU.add).then_inc(scanned, 1)
                        pipeline(dve, [(fold, 0), (add, 1), (fill, 0), (scan_, 2)])

        def small(tag, build):
            chain = sem(tag + "_chain")
            with nc.Block() as block:
                @block.vector
                def _(dve):
                    n = 0
                    for make in build:
                        make(dve).then_inc(chain, 1)
                        n += 1
                        dve.wait_ge(chain, n)

        def bias_column(tag, w_rows, vec, base, dst, ctx):
            halves = len(dst)
            ps = ctx.enter_context(nc.psum_tensor(tag + "_ps", [P, halves], F32))
            made, added = sem(tag + "_made"), sem(tag + "_added")
            with nc.Block() as block:
                @block.tensor
                def _(pe):
                    for h in range(halves):
                        mm = pe.matmul(ps[:, h:h + 1], w_rows[:, h * P:(h + 1) * P], vec, start=True, stop=True)
                    mm.then_inc(made, 1)

                @block.vector
                def _(dve):
                    dve.wait_ge(made, 1)
                    for h in range(halves):
                        last = dve.tensor_tensor(dst[h], ps[:, h:h + 1], base[h], ALU.add)
                        last.then_inc(added, 1)
                    dve.wait_ge(added, halves)

        def nodes01():
            with ExitStack() as ctx:
                agg = sb("n0_agg", [P, BLOCKS, D], F32, ctx)
                w1a = sb("n0_w1a", [D, 2 * P], F32, ctx)
                w1g = sb("n0_w1g", [D, 2 * P], F32, ctx)
                w2 = [sb(f"n0_w2{h}", [P, D], F32, ctx) for h in range(2)]
                glob, gv = column("n0_glob", a["L0_globals_"].rearrange("a b -> (a b)"), ctx)
                b1 = sb("n0_b1", [P, 2], F32, ctx)
                b1g = [sb(f"n0_b1g{h}", [P, 1], F32, ctx) for h in range(2)]
                b2 = sb("n0_b2", [P, D], F32, ctx)
                eps = sb("n0_eps", [P, 1], F32, ctx)
                piece = sb("n0_piece", [P, BLOCKS, D], F32, ctx)
                ends, ends_loads = stream_ends("n0_ends", run0, 1, ctx)
                agg1 = sb("n1_agg", [P, BLOCKS, 2 * DE], F32, ctx)
                cat = sb("n1_cat", [P, BLOCKS, 3 * DE], F32, ctx)
                w11 = sb("n1_w1", [3 * DE, P], F32, ctx)
                w1u, w1uv = column("n1_w1u", a["L1_W1"][3 * DE:3 * DE + 1, :].rearrange("a b -> (a b)"), ctx)
                b11, b11v = column("n1_b1", a["L1_b1"], ctx)
                u0 = sb("n1_u0", [P, 1], F32, ctx)
                w21 = sb("n1_w2", [P, D], F32, ctx)
                b21 = sb("n1_b2", [P, D], F32, ctx)
                inv = sb("n1_inv", [P, 2, BLOCKS], F32, ctx)
                piece1 = sb("n1_piece", [P, BLOCKS, DE], F32, ctx)
                absent = sb("n1_absent", [P, STREAMS_S - 1, BLOCKS], F32, ctx)
                ends1, ends1_loads = stream_ends("n1_ends", run1, 0, ctx)
                load([
                    (w1a[:, :], a["L0_W1"][0:D, :]), (w1g[:, :], a["L0_W1"][D:2 * D, :]),
                    (w2[0][:, :], a["L0_W2"][0:P, :]), (w2[1][:, :], a["L0_W2"][P:2 * P, :]), (glob[:, :], gv),
                    (b1[:, 0:1], a["L0_b1"][0:P].rearrange("(p o) -> p o", o=1)),
                    (b1[:, 1:2], a["L0_b1"][P:2 * P].rearrange("(p o) -> p o", o=1)),
                    (b2[:, :], a["L0_b2"].partition_broadcast(P)),
                    (eps[:, :], a["L0_epsilon"].rearrange("a b -> (a b)").partition_broadcast(P)),
                    (w11[:, :], a["L1_W1"][0:3 * DE, :]), (w1u[:, :], w1uv), (b11[:, :], b11v),
                    (u0[:, :], a["L1_u"][0:1, :].rearrange("a b -> (a b)").partition_broadcast(P)),
                    (w21[:, :], a["L1_W2"]), (b21[:, :], a["L1_b2"].partition_broadcast(P))] + ends_loads + ends1_loads, "n0")
                with ExitStack() as c2:
                    bias_column("n0b", w1g, glob[:, :], [b1[:, 0:1], b1[:, 1:2]], [t[:, :] for t in b1g], c2)
                small("n0s", [lambda dve: dve.tensor_scalar(eps[:, :], eps[:, :], 1.0, None, ALU.add)])

                def finish0(rows):
                    joins = [op for j in range(STREAMS_D - 1) for op in (
                        lambda dve, j=j: dve.tensor_tensor(piece[:, rows, :], bcast_last(spans[1][:, j, rows], D),
                                                           bcast_mid(ends[:, j, :], GB), ALU.mult),
                        lambda dve: dve.tensor_tensor(agg[:, rows, :], agg[:, rows, :], piece[:, rows, :], ALU.add))]
                    return joins + [lambda dve: dve.scalar_tensor_tensor(agg[:, rows, :], x[:, rows, :], eps[:, :],
                                                                         agg[:, rows, :], ALU.mult, ALU.add)]
                arrival = Arrival("n0a", run0, 1, agg, finish0)
                landed1 = [sem(f"n1_landed{g}") for g in range(GROUPS)]
                node_mlp("n0m", [(agg, D, w1a)], [t[:, :] for t in w2], [t[:, :] for t in b1g], b2[:, :], "mish", x, x,
                         arrival, lambda pool: take_ends(pool, run1, 0, agg1, landed1))
                norm("n0n", x, x)

                joins1 = [op for j in range(STREAMS_S - 1) for op in (
                    lambda dve, j=j: dve.tensor_tensor(piece1[:, :, :], bcast_last(spans[0][:, j, :], DE),
                                                       bcast_mid(ends1[:, j, 0:DE], BLOCKS), ALU.mult),
                    lambda dve: dve.tensor_tensor(agg1[:, :, 0:DE], agg1[:, :, 0:DE], piece1[:, :, :], ALU.add),
                    lambda dve, j=j: dve.tensor_tensor(piece1[:, :, :], bcast_last(absent[:, j, :], DE),
                                                       bcast_mid(ends1[:, j, DE:2 * DE], BLOCKS), ALU.add),
                    lambda dve: dve.tensor_tensor(agg1[:, :, DE:2 * DE], agg1[:, :, DE:2 * DE], piece1[:, :, :], ALU.max))]
                small("n1s", [
                    lambda dve: dve.tensor_scalar(absent[:, :, :], spans[0][:, :, :], BIG, -BIG, ALU.mult, ALU.add),
                    no_edges(agg1, 0)] + joins1 + [
                    lambda dve: dve.scalar_tensor_tensor(b11[:, :], w1u[:, :], u0[:, :], b11[:, :], ALU.mult, ALU.add),
                    lambda dve: dve.tensor_scalar(inv[:, 0, :], count[0][:, :], 1.0, None, ALU.max),
                    lambda dve: dve.reciprocal(inv[:, 1, :], inv[:, 0, :]),
                    lambda dve: dve.tensor_copy(cat[:, :, 0:2 * DE], agg1[:, :, :]),
                    lambda dve: dve.tensor_tensor(cat[:, :, 2 * DE:3 * DE], agg1[:, :, 0:DE],
                                                  bcast_last(inv[:, 1, :], DE), ALU.mult)])
                node_mlp("n1m", [(cat, 3 * DE, w11)], [w21[:, :]], [b11[:, :]], b21[:, :], ACT.Relu, x, x)
                norm("n1n", x, x)

        def store_rows(tag, pairs):
            done = sem(tag + "_done")
            with nc.Block() as block:
                @block.sync
                def _(sp):
                    for t, view in pairs:
                        sp.dma_start(view.rearrange("(b p) f -> p b f", p=P), t).then_inc(done, 16)
                    sp.wait_ge(done, 16 * len(pairs))

        def tables2():
            with ExitStack() as ctx:
                h = sb("t2_h", [P, BLOCKS, D], F32, ctx)
                g, b = sb("t2_g", [P, D], F32, ctx), sb("t2_b", [P, D], F32, ctx)
                w = sb("t2_w", [D, 3 * P], F32, ctx)
                bias = sb("t2_bias", [P, 3 * P], F32, ctx)
                qkv = sb("t2_qkv", [P, BLOCKS, 3 * P], F32, ctx)
                pairs = [(g[:, :], a["L2_ln1_g"].partition_broadcast(P)), (b[:, :], a["L2_ln1_b"].partition_broadcast(P))]
                for j, n in enumerate("qkv"):
                    pairs.append((w[:, j * P:(j + 1) * P], a["L2_W" + n]))
                    pairs.append((bias[:, j * P:(j + 1) * P], a["L2_b" + n].partition_broadcast(P)))
                load(pairs, "t2")
                norm("t2n", x, h, g[:, :], b[:, :])
                node_product("t2p", h, D, w[:, :], 3 * P, lambda dve, i, rows: dve.tensor_tensor(
                    qkv[:, bass.ds(i * GB, GB), :], rows, bcast_mid(bias[:, :], GB), ALU.add),
                             None, qkv, 1, q_rows, kv_tab)

        def nodes2():
            with ExitStack() as ctx:
                agg = sb("n2_agg", [P, BLOCKS, 130], F32, ctx)
                res = sb("n2_res", [P, BLOCKS, D], F32, ctx)
                o = sb("n2_o", [P, BLOCKS, D], F32, ctx)
                wp = sb("n2_wp", [P, D], F32, ctx)
                w1, w2 = sb("n2_w1", [D, D], F32, ctx), sb("n2_w2", [D, D], F32, ctx)
                b1, b1v = column("n2_b1", a["L2_b1"], ctx)
                bp, g, b, b2 = (sb("n2_" + n, [P, D], F32, ctx) for n in ("bp", "g", "b", "b2"))
                inv = sb("n2_inv", [P, BLOCKS, 2], F32, ctx)
                load([(wp[:, :], a["L2_Wp"]), (w1[:, :], a["L2_W1"]), (w2[:, :], a["L2_W2"]), (b1[:, :], b1v),
                      (bp[:, :], a["L2_bp"].partition_broadcast(P)), (g[:, :], a["L2_ln2_g"].partition_broadcast(P)),
                      (b[:, :], a["L2_ln2_b"].partition_broadcast(P)), (b2[:, :], a["L2_b2"].partition_broadcast(P))], "n2")

                def finish2(rows):
                    def scaled(h):
                        part = agg[:, rows, h * D:(h + 1) * D]
                        return lambda dve: dve.tensor_tensor(part, part, bcast_last(inv[:, rows, h], D), ALU.mult)
                    return [lambda dve: dve.tensor_scalar(inv[:, rows, :], agg[:, rows, P:130], 1e-8, None, ALU.add),
                            lambda dve: dve.reciprocal(inv[:, rows, :], inv[:, rows, :]), scaled(0), scaled(1)]
                node_product("n2p", agg, P, wp[:, :], D, lambda dve, i, rows: dve.tensor_tensor(
                    res[:, bass.ds(i * GB, GB), :], rows, bcast_mid(bp[:, :], GB), ALU.add),
                             Arrival("n2a", run2, 1, agg, finish2))
                small("n2t", [lambda dve: dve.tensor_tensor(res[:, :, :], res[:, :, :], x[:, :, :], ALU.add)])
                norm("n2n", res, o, g[:, :], b[:, :])
                small("n2u", [lambda dve: dve.tensor_tensor(x[:, :, :], res[:, :, :], x[:, :, :], ALU.add)])
                node_mlp("n2m", [(o, D, w1)], [w2[:, :]], [b1[:, :]], b2[:, :], ACT.Gelu, x, x)
                norm("n2o", x, x)

        def tables3():
            with ExitStack() as ctx:
                w = sb("t3_w", [D, 2 * P], F32, ctx)
                ab = sb("t3_ab", [P, BLOCKS, 2 * P], F32, ctx)
                load([(w[:, 0:P], a["L3_eW1"][0:D, :]), (w[:, P:2 * P], a["L3_eW1"][D:2 * D, :])], "t3")
                node_product("t3p", x, D, w[:, :], 2 * P, lambda dve, i, rows: dve.tensor_copy(
                    ab[:, bass.ds(i * GB, GB), :], rows), None, ab, 0, a_rows, b_tab)

        def nodes3():
            with ExitStack() as ctx:
                agg = sb("n3_agg", [P, BLOCKS, P], F32, ctx)
                w1x, w1a = sb("n3_w1x", [D, P], F32, ctx), sb("n3_w1a", [P, P], F32, ctx)
                w2 = sb("n3_w2", [P, D], F32, ctx)
                b1, b1v = column("n3_b1", a["L3_nb1"], ctx)
                b2 = sb("n3_b2", [P, D], F32, ctx)
                load([(w1x[:, :], a["L3_nW1"][0:D, :]), (w1a[:, :], a["L3_nW1"][D:D + P, :]), (w2[:, :], a["L3_nW2"]),
                      (b1[:, :], b1v), (b2[:, :], a["L3_nb2"].partition_broadcast(P))], "n3")
                node_mlp("n3m", [(x, D, w1x), (agg, P, w1a)], [w2[:, :]], [b1[:, :]], b2[:, :], ACT.Silu, x, x,
                         Arrival("n3a", run3, 0, agg, lambda rows: []))
                norm("n3n", x, x)
                store_rows("n3o", [(x[:, :, :], out)])

        with sort:
            load_keys()
            with nc.psum_tensor("src_sums", [P, 512], F32) as src_sums:
                source_histogram(src_sums[:, 0:BLOCKS])
                starts(0, src_sums[:, 0:BLOCKS])
            sort_by_source()
            starts(1, dst_sums)
            end_stage()
        edges01()
        end_stage()
        early_ctx.close()
        nodes01()
        end_stage()
        tables2()
        end_stage()
        edges2()
        end_stage()
        nodes2()
        end_stage()
        tables3()
        end_stage()
        edges3()
        end_stage()
        nodes3()


def kernel(**inputs):
    import numpy as np
    import concourse.bacc as bacc
    from concourse.bass_utils import run_bass_kernel_spmd as run

    v = {k: np.asarray(t) for k, t in inputs.items()}
    pad = EP - EDGES

    def pad_rows(t, rows, fill=0):
        return np.concatenate([t, np.full((rows - t.shape[0],) + t.shape[1:], fill, t.dtype)])

    src, dst = pad_rows(v["src"], EP, NODES), pad_rows(v["dst"], EP, NODES)
    ea16, ea32 = pad_rows(v["edge_attr_16"], EP), pad_rows(v["edge_attr_32"], EP)
    weight = pad_rows(v["edge_weight1"], EP)
    lanes = np.arange(P)
    consts = np.zeros((P, C_COLS), np.float32)
    consts[:, C_EYE:C_EYE + P] = np.eye(P)
    consts[:, C_BEFORE:C_BEFORE + P] = lanes[None, :] < lanes[:, None]
    consts[:, C_UPPER:C_UPPER + P] = lanes[:, None] < lanes[None, :]
    consts[:, C_IOTA:C_IOTA + P] = lanes[None, :]
    consts[:, C_ONES:C_ONES + P] = 1.0
    consts[:, C_SPARE:] = EP + np.arange(BLOCKS)[None, :] * P + lanes[:, None]
    heads = (lanes[:, None] // D == lanes[None, :] // D).astype(np.float32)
    arrays = {
        "consts": consts, "heads": heads,
        "x": pad_rows(v["x"], NP_),
        "src_flat": src, "dst_after": np.concatenate([np.full(1, -1, dst.dtype), dst]), "src_cols": np.ascontiguousarray(src.reshape(TILES, P).T),
        "src_rows": np.ascontiguousarray(src.reshape(CHUNKS, P, TPC).transpose(1, 0, 2).reshape(P, TILES)),
        "dst_cols": np.ascontiguousarray(dst.reshape(TILES, P).T),
        "rec_f": np.concatenate([ea32, weight], axis=1),
        "attr16_t": np.ascontiguousarray(ea16.T), "attr32_t": np.ascontiguousarray(ea32.T),
    }
    for k, t in v.items():
        if "_gnn_" in k:
            arrays[k.replace("_gnn", "")] = t
    arrays = {k: np.ascontiguousarray(t) for k, t in arrays.items()}
    nc = bacc.Bacc("TRN2", target_bir_lowering=False, num_devices=1)
    a = {k: nc.dram_tensor("in_" + k, t.shape, mybir.dt.from_np(t.dtype), kind="ExternalInput").ap()
         for k, t in arrays.items()}
    out = nc.dram_tensor("out", (NP_, D), F32, kind="ExternalOutput").ap()
    program(nc, a, out)
    r = run(nc, [{"in_" + k: t for k, t in arrays.items()}], core_ids=[0])
    return r.results[0]["out"][:NODES]
```
